# Optimizing a Trainium2 kernel written in Bass

```python
import numpy as np
import jax
import jax.numpy as jnp

def _softmax(x, axis=-1):
    return jax.nn.softmax(x, axis=axis)

def _gelu(x):
    return jax.nn.gelu(x, approximate=True)

def _silu(x):
    return jax.nn.silu(x)

def _sigmoid(x):
    return jax.nn.sigmoid(x)

def _layernorm(x, axis=-1, eps=1e-05):
    m = jnp.mean(x, axis=axis, keepdims=True)
    v = jnp.var(x, axis=axis, keepdims=True)
    return (x - m) / jnp.sqrt(v + eps)

def _scatter_add(tgt, idx, src, axis=0):
    return tgt.at[idx].add(src)

def _segment_sum(src, seg, n):
    return jax.ops.segment_sum(src, seg, n)
kernel_name = 'mk_gps_d1_gnn_r8_86017e'

def setup_inputs(seed: int=0):
    np.random.seed(seed)
    _w = jnp.asarray

    def _rec_inputs():
        import jax
        import jax.numpy as jnp
        _gk = jax.random.key(seed)
        x = -0.0002117 + 1 * jax.random.normal(jax.random.fold_in(_gk, 1), (6250, 256), jnp.float32)
        src = jax.random.randint(jax.random.fold_in(_gk, 2), (200000,), 0, 6250, jnp.int32)
        dst = jax.random.randint(jax.random.fold_in(_gk, 3), (200000,), 0, 6250, jnp.int32)
        _o = jnp.argsort(dst, stable=True)
        src = src[_o]
        dst = dst[_o]
        edge_weight = jax.random.uniform(jax.random.fold_in(_gk, 12), (200000,), jnp.float32, 0.0, 0.999999)
        return (x, src, dst, edge_weight)
    x, src, dst, edge_weight = _rec_inputs()

    def _L0_gnn_setup():
        import jax, jax.numpy as jnp
        import numpy as np
        N_NODES = 12500
        N_EDGES = 200000
        D = 256
        key = jax.random.key(seed)
        ks = jax.random.split(key, 8)
        h6_all = jax.random.normal(ks[0], (N_NODES, D), dtype=jnp.float32)
        edge_index = jax.random.randint(ks[1], (2, N_EDGES), 0, N_NODES, dtype=jnp.int64)
        edge_weight = jax.random.uniform(ks[2], (N_EDGES,), dtype=jnp.float32)
        s = 1.0 / np.sqrt(D)
        W = jax.random.normal(ks[3], (D, D), dtype=jnp.float32) * s
        b = jnp.zeros((D,), dtype=jnp.float32)
        W1 = jax.random.normal(ks[4], (D, D), dtype=jnp.float32) * s
        b1 = jnp.zeros((D,), dtype=jnp.float32)
        W2 = jax.random.normal(ks[5], (D, D), dtype=jnp.float32) * s
        b2 = jnp.zeros((D,), dtype=jnp.float32)
        return {'h6_all': h6_all, 'edge_index': edge_index, 'edge_weight': edge_weight, 'W': W, 'b': b, 'W1': W1, 'b1': b1, 'W2': W2, 'b2': b2}
    _L0_gnn_all = _L0_gnn_setup()
    _L0_gnn_in = {k: v for k, v in _L0_gnn_all.items() if k in ('W', 'b', 'W1', 'b1', 'W2', 'b2')}
    del _L0_gnn_all

    def _L0_mix_setup():
        import jax, jax.numpy as jnp
        import numpy as np
        HEADS, DIM_HEAD = (8, 64)
        EPS = 1e-05

        def instance_norm(t):
            mu = jnp.mean(t, axis=-1, keepdims=True)
            var = jnp.mean((t - mu) ** 2, axis=-1, keepdims=True)
            return (t - mu) * jax.lax.rsqrt(var + EPS)
        key = jax.random.key(seed)
        k1, k2, k3, k4 = jax.random.split(key, 4)
        B, N, D = (8, 1024, 256)
        inner = HEADS * DIM_HEAD
        x = jax.random.normal(k1, (B, N, D), jnp.float32)
        w_qkv = jax.random.normal(k2, (3 * inner, D), jnp.float32) / np.sqrt(D).astype(np.float32)
        w_out = jax.random.normal(k3, (D, inner), jnp.float32) / np.sqrt(inner).astype(np.float32)
        b_out = 0.01 * jax.random.normal(k4, (D,), jnp.float32)
        return {'x': x, 'w_qkv': w_qkv, 'w_out': w_out, 'b_out': b_out}
    _L0_mix_all = _L0_mix_setup()
    _L0_mix_in = {k: v for k, v in _L0_mix_all.items() if k in ('w_qkv', 'w_out', 'b_out')}
    del _L0_mix_all

    def _L0_ffn_setup():
        import jax, jax.numpy as jnp
        import numpy as np
        B, S, D = (8, 512, 256)
        H = 4 * D
        CAPACITY = 0.5
        key = jax.random.key(seed)
        ks = jax.random.split(key, 6)
        x = jax.random.normal(ks[0], (B, S, D), dtype=jnp.float32)
        attention_mask = jnp.zeros((B, 1, 1, S), dtype=jnp.float32)
        wr = jax.random.normal(ks[1], (D, 1), dtype=jnp.float32) * 0.02
        br = jnp.zeros((1,), dtype=jnp.float32)
        w1 = jax.random.normal(ks[2], (D, H), dtype=jnp.float32) * 0.02
        b1 = jnp.zeros((H,), dtype=jnp.float32)
        w2 = jax.random.normal(ks[3], (H, D), dtype=jnp.float32) * 0.02
        b2 = jnp.zeros((D,), dtype=jnp.float32)
        return {'x': x, 'attention_mask': attention_mask, 'wr': wr, 'br': br, 'w1': w1, 'b1': b1, 'w2': w2, 'b2': b2}
    _L0_ffn_all = _L0_ffn_setup()
    _L0_ffn_in = {k: v for k, v in _L0_ffn_all.items() if k in ('attention_mask', 'wr', 'br', 'w1', 'b1', 'w2', 'b2')}
    del _L0_ffn_all
    return {'x': x, 'src': src, 'dst': dst, 'edge_weight': edge_weight, 'L0_gnn_W': _L0_gnn_in['W'], 'L0_gnn_b': _L0_gnn_in['b'], 'L0_gnn_W1': _L0_gnn_in['W1'], 'L0_gnn_b1': _L0_gnn_in['b1'], 'L0_gnn_W2': _L0_gnn_in['W2'], 'L0_gnn_b2': _L0_gnn_in['b2'], 'L0_mix_w_qkv': _L0_mix_in['w_qkv'], 'L0_mix_w_out': _L0_mix_in['w_out'], 'L0_mix_b_out': _L0_mix_in['b_out'], 'L0_ffn_attention_mask': _L0_ffn_in['attention_mask'], 'L0_ffn_wr': _L0_ffn_in['wr'], 'L0_ffn_br': _L0_ffn_in['br'], 'L0_ffn_w1': _L0_ffn_in['w1'], 'L0_ffn_b1': _L0_ffn_in['b1'], 'L0_ffn_w2': _L0_ffn_in['w2'], 'L0_ffn_b2': _L0_ffn_in['b2']}

def reference(x, src, dst, edge_weight, L0_gnn_W, L0_gnn_b, L0_gnn_W1, L0_gnn_b1, L0_gnn_W2, L0_gnn_b2, L0_mix_w_qkv, L0_mix_w_out, L0_mix_b_out, L0_ffn_attention_mask, L0_ffn_wr, L0_ffn_br, L0_ffn_w1, L0_ffn_b1, L0_ffn_w2, L0_ffn_b2):
    import jax
    import jax.numpy as jnp

    def _L0_gnn_ref(h6_all, edge_index, edge_weight, W, b, W1, b1, W2, b2):
        import jax, jax.numpy as jnp
        import numpy as np
        N_NODES = 12500
        N_EDGES = 200000
        D = 256
        'GCNConv(256->256, weighted, self-loops, symmetric norm) + 2-layer MLP head.'
        N = h6_all.shape[0]
        row, col = (edge_index[0], edge_index[1])
        sl = jnp.arange(N, dtype=edge_index.dtype)
        row_sl = jnp.concatenate([row, sl])
        col_sl = jnp.concatenate([col, sl])
        ew_sl = jnp.concatenate([edge_weight, jnp.ones((N,), dtype=edge_weight.dtype)])
        deg = jax.ops.segment_sum(ew_sl, row_sl, num_segments=N)
        dinv = jnp.where(deg > 0, jax.lax.rsqrt(deg), 0.0)
        norm = dinv[row_sl] * ew_sl * dinv[col_sl]
        xw = h6_all @ W
        msgs = xw[col_sl] * norm[:, None]
        h7 = jax.ops.segment_sum(msgs, row_sl, num_segments=N) + b
        h = jax.nn.relu(h7 @ W1 + b1)
        out = h @ W2 + b2
        return out

    def _L0_mix_ref(x, w_qkv, w_out, b_out):
        import jax, jax.numpy as jnp
        import numpy as np
        HEADS, DIM_HEAD = (8, 64)
        EPS = 1e-05

        def instance_norm(t):
            mu = jnp.mean(t, axis=-1, keepdims=True)
            var = jnp.mean((t - mu) ** 2, axis=-1, keepdims=True)
            return (t - mu) * jax.lax.rsqrt(var + EPS)
        B, N, _ = x.shape
        H, Dh = (HEADS, DIM_HEAD)
        qkv = jnp.einsum('bnd,ed->bne', x, w_qkv)
        q, k, v = jnp.split(qkv, 3, axis=-1)

        def to_heads(t):
            return t.reshape(B, N, H, Dh).transpose(0, 2, 1, 3)
        q, k, v = (to_heads(q), to_heads(k), to_heads(v))
        k = instance_norm(k)
        v = instance_norm(v)
        dots = jnp.einsum('bhnd,bhne->bhde', k, v)
        out = jnp.einsum('bhnd,bhde->bhne', q, dots) / N
        out = out.transpose(0, 2, 1, 3).reshape(B, N, H * Dh)
        return jnp.einsum('bne,de->bnd', out, w_out) + b_out

    def _L0_ffn_ref(x, attention_mask, wr, br, w1, b1, w2, b2):
        import jax, jax.numpy as jnp
        import numpy as np
        B, S, D = (8, 512, 256)
        H = 4 * D
        CAPACITY = 0.5
        b, s, d = x.shape
        weights = (jnp.einsum('bsd,do->bso', x, wr) + br)[..., 0]
        k = max(1, int(CAPACITY * s))
        kk = k - 1 if k > 1 else 1
        _, idx = jax.lax.top_k(weights, k)
        sel_idx = idx[:, :kk]
        sel = jnp.take_along_axis(x, sel_idx[:, :, None], axis=1)
        h = jax.nn.gelu(jnp.einsum('bkd,dh->bkh', sel, w1) + b1)
        y = jnp.einsum('bkh,hd->bkd', h, w2) + b2
        w_sel = jnp.take_along_axis(weights, sel_idx, axis=1)
        y = y * w_sel[..., None]
        batch_idx = jnp.arange(b)[:, None]
        processed = jnp.zeros_like(x).at[batch_idx, sel_idx].set(y)
        return processed + x
    edge_index = jnp.stack([src, dst])
    xn = _layernorm(x, axis=-1)
    x = x + _L0_gnn_ref(xn, edge_index, edge_weight, L0_gnn_W, L0_gnn_b, L0_gnn_W1, L0_gnn_b1, L0_gnn_W2, L0_gnn_b2) + _L0_mix_ref(xn[None], L0_mix_w_qkv, L0_mix_w_out, L0_mix_b_out)[0]
    x = x + _L0_ffn_ref(_layernorm(x, axis=-1)[None], L0_ffn_attention_mask, L0_ffn_wr, L0_ffn_br, L0_ffn_w1, L0_ffn_b1, L0_ffn_w2, L0_ffn_b2)[0]
    return x

_drawn_inputs = setup_inputs


def setup_inputs(seed=0):
    import zlib

    import numpy as np

    out = dict(_drawn_inputs(seed))
    spreads = {'L0_gnn_b': (0.0, 0.1),
     'L0_gnn_b1': (0.0, 0.1),
     'L0_gnn_b2': (0.0, 0.1),
     'L0_ffn_b1': (0.0, 0.8),
     'L0_ffn_b2': (0.0, 0.8)}
    factors = {'L0_mix_b_out': 7.091, 'L0_ffn_wr': 3.679, 'L0_ffn_w1': 5.487, 'L0_ffn_w2': 5.17}
    for name, (base, spread) in spreads.items():
        noise = np.random.default_rng([zlib.crc32(name.encode()), seed]).standard_normal(out[name].shape)
        drawn = base * np.exp(spread * noise) if base else spread * noise
        out[name] = jnp.asarray(drawn.astype(out[name].dtype))
    for name, factor in factors.items():
        out[name] = (out[name] * factor).astype(out[name].dtype)
    return out
```

```python
from contextlib import ExitStack

import concourse.bass as bass
from concourse import mybir

ALU = mybir.AluOpType
ACT = mybir.ActivationFunctionType
AX = mybir.AxisListType
F32 = mybir.dt.float32
BF16 = mybir.dt.bfloat16
I32 = mybir.dt.int32
ds = bass.ds

P = 128
EPS = 1e-5


def ceil_div(a, b):
    return -(-a // b)


def spread(v, axis, n):
    shape = list(v.shape)
    shape[axis] = n
    return v.broadcast_to(shape)


class Chain:

    def __init__(self, eng, sem):
        self.eng, self.sem, self.base, self.k, self.i, self.per = eng, sem, 0, 0, None, 0

    def mark(self, ins):
        self.k += 1
        ins.then_inc(self.sem, 1)

    def wait(self):
        at = self.base + self.k
        self.eng.wait_ge(self.sem, at if self.i is None else self.i * self.per + at)

    def link(self, ins):
        self.mark(ins)
        self.wait()

    def enter(self, i, per):
        self.base, self.k, self.i, self.per = self.base + self.k, 0, i, per

    def leave(self, n):
        assert self.k == self.per, (self.k, self.per)
        self.base, self.k, self.i = self.base + n * self.per, 0, None


def gps_layer(nc, A, out):
    x_d, src_d, dst_d, ew_d = A["x"], A["src"], A["dst"], A["edge_weight"]
    N, D = x_d.shape
    E = src_d.shape[0]
    NB = ceil_div(N, P)
    NT = NB + NB % 2
    LAST = N - (NB - 1) * P
    DK = D // P
    EP = 125
    EC = E // EP
    SJ = 40
    NS = EC // SJ
    HJ = SJ // 2
    B = 16
    RW = 2
    HI = ceil_div(ceil_div(EP * SJ + NB * (B - 1), B), P)
    SUB = HI * B
    CH = 4
    BPG = CH * P // B
    SLOTS = 5
    UG = 2 * SLOTS
    runs_max = (E + NS * NB * (B - 1)) // B
    groups_max = (runs_max + NB * (BPG - 1)) // BPG
    NG = ceil_div(groups_max, UG) * UG
    NIT = NG // UG
    RUNS = ceil_div(NG * BPG + HI * P, P) * P
    SPARE = RUNS - HI * P
    assert E == EP * EC and EC == SJ * NS and NIT >= NB and NB < P and NT == NB + 1 and NB % 7 == 0 and SPARE >= NG * BPG
    GD = A["woT"].shape[0]
    KV = 2 * GD
    HW = 64
    HEADS = GD // HW
    PAIRS = GD // P
    F = A["L0_ffn_w1"].shape[1]
    FB = F // P
    TOP = max(1, N // 2) - 1

    y_d = nc.dram_tensor("y_table", [NT * P, D], F32, kind="Internal").ap()
    rec_d = nc.dram_tensor("records", [RUNS, B * RW], F32, kind="Internal").ap()
    hmap_d = nc.dram_tensor("block_of_group", [4 * P], I32, kind="Internal").ap()

    with ExitStack() as ctx:
        def sb(name, shape, dt=F32):
            return ctx.enter_context(nc.sbuf_tensor(name, shape, dt))

        def sem(name):
            return ctx.enter_context(nc.semaphore(name))

        bank = [ctx.enter_context(nc.psum_tensor(f"bank{i}", [P, 512], F32)) for i in range(8)]

        X = sb("X", [P, NT, D])
        ACC = sb("ACC", [P, NT, D])
        AR = sb("AR", [P, 18304])
        accf = ACC[:, :, :].rearrange("p t d -> p (t d)")

        def cut(base, start, shape, rows=P):
            n = 1
            for s in shape:
                n *= s
            v = base[0:rows, start:start + n]
            if len(shape) == 2:
                v = v.rearrange("p (a b) -> p a b", a=shape[0])
            if len(shape) == 3:
                v = v.rearrange("p (a b c) -> p a b c", a=shape[0], b=shape[1])
            return v, start + n

        o = 0
        keyf, o = cut(AR, o, [EC], EP)
        hf, o = cut(AR, o, [EC], EP)
        ew, o = cut(AR, o, [EC], EP)
        rlof, o = cut(AR, o, [EC], EP)
        o_edges = o
        mv = []
        for _ in range(2):
            v, o = cut(AR, o, [HJ, SUB, RW], EP)
            mv.append(v)
        sub1h = []
        for _ in range(2):
            v, o = cut(AR, o, [HJ, SUB], EP)
            sub1h.append(v)
        zero, o_cnt = cut(AR, o, [RUNS // P * B * RW])
        cnt, _ = cut(AR, o_cnt, [NS, NB])
        lbx, _ = cut(AR, o, [NS, NB + 1])
        dlt, _ = cut(AR, o_edges, [NS, NB + 1])
        srcI = AR[0:EP, o_edges:o_edges + EC].bitcast(I32)
        dstI = AR[0:EP, o_edges + EC:o_edges + 2 * EC].bitcast(I32)
        tmpI = AR[0:EP, o_edges + 2 * EC:o_edges + 3 * EC].bitcast(I32)
        o = 0
        oh1 = []
        for _ in range(2):
            oh1.append(accf[0:EP, o:o + SJ * NB // 2].bitcast(BF16).rearrange("p (j h) -> p j h", j=SJ))
            o += SJ * NB // 2
        ohw = []
        for _ in range(2):
            v, o = cut(accf, o, [SJ, NB], EP)
            ohw.append(v)
        rl1h = []
        for _ in range(2):
            v, o = cut(accf, o, [HJ, P], EP)
            rl1h.append(v)
        o = 0
        pcf, o = cut(accf, o, [NS * NB])
        pcT, o = cut(accf, o, [NB, NS])
        inc, o = cut(accf, o, [NS * NB])
        keep, o = cut(accf, o, [NS * NB])
        big, o = cut(accf, o, [NS, NB + 1])
        assert o <= 12800
        o = 0
        O2, o = cut(accf, o, [NB, SJ], EP)
        Fx = accf[0:EP, o:o + 1 + NB * SJ]
        o += 1 + NB * SJ
        V2, o = cut(accf, o, [NB, SJ], EP)
        lo1h = []
        for _ in range(2):
            v, o = cut(accf, o, [HJ, P], EP)
            lo1h.append(v)
        assert o <= 12800
        o = 0
        rec, o = cut(AR, o, [NG + SLOTS - 1, CH * RW])
        cidx, o = cut(AR, o, [NG + SLOTS - 1, CH])
        rlo, o = cut(AR, o, [NG + SLOTS - 1, CH])
        rlo_i = rlo.bitcast(I32)
        recw = rec.rearrange("p g (c w) -> p g c w", w=RW)[:, :, :, 1]
        G, o = cut(AR, o, [SLOTS, CH, D])
        OH, o = cut(AR, o, [SLOTS, CH, P])
        kvsq, o = cut(AR, o, [KV])
        kn, o = cut(AR, o, [GD])
        vs, o = cut(AR, o, [GD])
        xs, o = cut(AR, o, [D])
        xT, o = cut(AR, o, [D])
        assert o <= 18304, o
        cidxI = AR[:, (NG + SLOTS - 1) * CH * RW:(NG + SLOTS - 1) * CH * (RW + 1)].bitcast(I32).rearrange("p (g c) -> p g c", c=CH)
        o = 0
        w1s, o = cut(AR, o, [DK, F])
        w2s, o = cut(AR, o, [FB, D])
        wq, o = cut(AR, o, [PAIRS, D])
        wo, o = cut(AR, o, [PAIRS, D])
        ot, o = cut(AR, o, [7, D])
        yt, o = cut(AR, o, [2, D])
        H1a, o = cut(AR, o, [FB, 4 * P])
        H1b, o2 = cut(AR, o, [FB, 3 * P])
        assert o2 <= 18304, o2
        ag, o = cut(AR, o, [2, D])
        agT, o = cut(AR, o, [2, D])
        hT, o = cut(AR, o, [2, D])
        xTs, o = cut(AR, o, [2, D])
        xin, o = cut(AR, o, [2, D])
        xn2, o = cut(AR, o, [2, D])
        assert o <= o2

        wkv = sb("wkv", [P, DK, KV])
        WT = sb("WT", [P, DK, D])
        W1 = sb("W1", [P, DK, D])
        W2 = sb("W2", [P, DK, D])
        WW = sb("WW", [P, DK, D])
        kvf = wkv[:, :, :].rearrange("p k n -> p (k n)")
        dots, o = cut(kvf, 0, [PAIRS, P])
        Vh, o = cut(kvf, o, [PAIRS, D])
        Mx, o = cut(kvf, o, [DK, D])
        assert o <= DK * KV
        bc = sb("bc", [P, DK])
        b1c = sb("b1c", [P, DK])
        fb1 = sb("fb1", [P, FB])
        b2o = sb("b2o", [P, D])
        brow = sb("brow", [P, D])
        fb2 = sb("fb2", [P, D])
        wr = sb("wr", [P, D])
        brc = sb("brc", [P, 1])
        iotaI = sb("iotaI", [P, P], I32)
        iota = sb("iota", [P, P])
        pidI = sb("pidI", [P, HI], I32)
        pid = sb("pid", [P, HI])
        ident = sb("ident", [P, P])
        strict = sb("strict", [P, P])
        ones = sb("ones", [P, P])
        onesb = sb("onesb", [P, P], BF16)
        zcol = sb("zcol", [P, P])
        st = sb("st", [P, NB, 6])
        mvar = sb("mvar", [P, NT, 2])
        rstd = sb("rstd", [P, NT])
        t49 = sb("t49", [P, NB])
        v49 = sb("v49", [P, NB])
        u49 = sb("u49", [P, NB])
        dinv = sb("dinv", [P, NT])
        wcol = sb("wcol", [P, 1])
        wmean = sb("wmean", [P, DK * 2 * HEADS])
        ginc = sb("ginc", [P, NB])
        tpf = sb("tpf", [P, NB])
        ridx = sb("ridx", [P, NS, HI], I32)
        ridxf = sb("ridxf", [P, NS])
        hm = sb("hm", [P, 4])
        hmI = sb("hmI", [P, 4], I32)
        hm49 = sb("hm49", [P, 4, NB])
        hrow = sb("hrow", [1, 4 * P], I32)
        cn = sb("cn", [EP, NB])
        A2 = sb("A2", [EP, NB])
        posf = sb("posf", [EP, SJ])
        posI = sb("posI", [EP, SJ], I32)
        poaI = sb("poaI", [EP, SJ], I32)
        pobI = sb("pobI", [EP, SJ], I32)
        lof = sb("lof", [EP, SJ])
        subf = sb("subf", [EP, SJ])
        sidx = sb("sidx", [P, HI], I32)
        sbuf = sb("sbuf", [P, SUB * RW])
        gidx = sb("gidx", [P, SLOTS, CH], I32)
        ss = sb("ss", [P, 2 * HEADS])
        pr = sb("pr", [P, HEADS])
        rr = sb("rr", [P, HEADS])
        r2 = sb("r2", [P, HEADS])
        wt = sb("wt", [P, NT])
        keyI = sb("keyI", [P, NB], I32)
        kbI = sb("kbI", [P, NB], I32)
        khi = sb("khi", [P, NB])
        klo = sb("klo", [P, NB])
        comb = sb("comb", [P, NB])
        gtm = sb("gtm", [P, NB])
        eqm = sb("eqm", [P, NB])
        tk = [sb(f"tk{i}", [P, 1]) for i in range(6)]
        wsel = sb("wsel", [P, NB])
        sel = sb("sel", [P, NB])


        s_x, s_xpad, s_edges, s_w, s_wf = sem("x_loaded"), sem("x_padded"), sem("edges_loaded"), sem("weights_loaded"), sem("tail_weights_loaded")
        s_iota, s_zero, s_const = sem("iota_done"), sem("zeros_ready"), sem("constants_ready")
        s_dve = sem("dve_chain")
        s_var, s_sqrt = sem("variances_ready"), sem("roots_taken")
        s_e = sem("edge_fields_ready")
        s_o1, s_ow, s_rl = sem("block_onehots"), sem("weighted_onehots"), sem("row_onehots")
        s_cntp, s_cntc, s_h1 = sem("cells_counted"), sem("cell_counts_copied"), sem("row_onehots_used")
        s_deg = sem("degrees_summed")
        s_ridx, s_hm, s_hmd, s_hrow = sem("run_places_ready"), sem("group_blocks_ready"), sem("group_blocks_stored"), sem("group_blocks_loaded")
        s_cn, s_cross = sem("partition_counts"), sem("partition_prefixes")
        s_sub, s_key, s_wm, s_lo = sem("run_onehots"), sem("keys_placed"), sem("edge_weights_placed"), sem("lane_onehots")
        s_half, s_runs, s_runc = sem("halves_multiplied"), sem("runs_summed"), sem("runs_copied")
        s_sidx, s_scat, s_scd = sem("run_indices"), sem("records_written"), sem("scatters_over")
        s_acc, s_y, s_rec = sem("acc_started"), sem("table_stored"), sem("records_loaded")
        s_prep, s_grp, s_added = sem("groups_prepared"), sem("groups_multiplied"), sem("all_groups_added")
        s_g = [sem(f"rows_gathered_{i}") for i in range(SLOTS)]
        s_seen = {e: sem(f"waits_passed_{e}") for e in ("pool", "pe", "act", "dve", "sp")}
        s_xs, s_xTp, s_xT, s_kvp, s_vc = sem("xn_staged"), sem("xn_transposed"), sem("xnT_copied"), sem("kv_multiplied"), sem("v_copied")
        s_sq, s_pr, s_sr, s_kn, s_dot = sem("kv_squared"), sem("norm_products"), sem("norm_roots"), sem("k_scaled"), sem("dots_summed")
        s_wc, s_dd, s_m1, s_vh, s_m2, s_mx = (sem(n) for n in ("kv_weights_centred", "dots_copied", "mixer_half", "mixer_half_copied", "mixer_whole", "mixer_copied"))
        s_b1 = sem("hidden_bias_ready")
        a_ag, a_tp, a_T, a_hp, a_h, a_o, a_x1 = (sem("a_" + n) for n in ("scaled", "transposed", "copied", "hidden", "relu", "summed", "x1"))
        a_xin = [sem("a_x_loaded_0"), sem("a_x_loaded_1")]
        b_var, b_root, b_xn, b_tp, b_tc = (sem("b_" + n) for n in ("variances", "roots", "normalised", "transposed", "copied"))
        k_cnt, k_sum = sem("k_counted"), sem("k_summed")
        c_h, c_g, c_y, c_free, c_ot = (sem("c_" + n) for n in ("hidden", "gelu", "out", "bank_read", "tile_ready"))
        c_st = [sem(f"c_stored_{i}") for i in range(7)]

        def passed(eng, name):
            eng.sem_inc(s_seen[name], 1)

        def row(v):
            return v.rearrange("p o d -> p (o d)")

        block = ctx.enter_context(nc.Block())
        xpart = NB - 1

        @block.sync
        def _(sp):
            sp.dma_start(srcI, src_d.rearrange("(p j) -> p j", p=EP)).then_inc(s_edges, 16)
            sp.dma_start(dstI, dst_d.rearrange("(p j) -> p j", p=EP)).then_inc(s_edges, 16)
            sp.dma_start(ew, ew_d.rearrange("(p j) -> p j", p=EP)).then_inc(s_edges, 16)
            sp.dma_start(X[:, 0:xpart, :], x_d[0:xpart * P, :].rearrange("(t p) d -> p t d", p=P)).then_inc(s_x, 16)
            sp.wait_ge(s_xpad, 1)
            sp.dma_start(X[0:LAST, xpart, :], x_d[xpart * P:N, :]).then_inc(s_x, 16)
            for t, a in ((wkv, "kvT"), (WT, "WT"), (W1, "L0_gnn_W1"), (W2, "L0_gnn_W2")):
                sp.dma_start(t[:, :, :], A[a].rearrange("(k p) n -> p k n", p=P)).then_inc(s_w, 16)
            with nc.allow_non_contiguous_dma(reason="a few hundred words of biases"):
                sp.dma_start(bc[:, :], A["L0_gnn_b"].rearrange("(k p) -> p k", p=P)).then_inc(s_w, 16)
                sp.dma_start(b1c[:, :], A["L0_gnn_b1"].rearrange("(k p) -> p k", p=P)).then_inc(s_w, 16)
                sp.dma_start(fb1[:, :], A["L0_ffn_b1"].rearrange("(k p) -> p k", p=P)).then_inc(s_w, 16)
            for t, a in ((b2o, A["L0_gnn_b2"]), (brow, A["L0_mix_b_out"]), (fb2, A["L0_ffn_b2"]),
                         (wr, A["L0_ffn_wr"].rearrange("d o -> (d o)")), (brc, A["L0_ffn_br"])):
                sp.dma_start(t[:, :], spread(a.rearrange("(o d) -> o d", o=1), 0, P)).then_inc(s_w, 16)
            sp.wait_ge(s_hm, 1)
            with nc.allow_non_contiguous_dma(reason="512 words"):
                sp.dma_start(hmap_d.rearrange("(a p) -> p a", p=P), hmI[:, :]).then_inc(s_hmd, 16)
            sp.wait_ge(s_hmd, 16)
            sp.dma_start(hrow[:, :], hmap_d.rearrange("(o a) -> o a", o=1)).then_inc(s_hrow, 16)
            sp.wait_ge(s_acc, 1)
            sp.dma_start(y_d.rearrange("(t p) d -> p t d", p=P), ACC[:, :, :]).then_inc(s_y, 16)
            sp.wait_ge(s_scd, 1)
            recv = rec_d.rearrange("r w -> (r w)")[0:NG * CH * P * RW].rearrange("(g p w) -> p g w", p=P, w=CH * RW)
            q = ceil_div(NG, 4)
            for a in range(0, NG, q):
                sp.dma_start(rec[:, a:a + q, :], recv[:, a:a + q, :]).then_inc(s_rec, 16)
            sp.wait_ge(s_added, 1)
            for t, a in ((wq, "wq"), (wo, "woT"), (w1s, "L0_ffn_w1"), (w2s, "L0_ffn_w2")):
                sp.dma_start(t, A[a].rearrange("(k p) n -> p k n", p=P)).then_inc(s_wf, 16)
            with sp.Fori(0, (NT - 2) // 2) as i:
                for u in range(2):
                    sp.wait_ge(a_x1, 2 * i + u + 1)
                    passed(sp, "sp")
                    sp.dma_start(xin[:, u, :], x_d[ds((2 * i + u) * P, P), :]).then_inc(a_xin[u], 16)
            sp.wait_ge(a_x1, NT - 1)
            sp.dma_start(xin[0:LAST, 0, :], x_d[xpart * P:N, :]).then_inc(a_xin[0], 16)
            sp.wait_ge(a_x1, NT)
            sp.dma_start(xin[0:LAST, 1, :], x_d[xpart * P:N, :]).then_inc(a_xin[1], 16)
            n7 = NB // 7
            with sp.Fori(0, n7 - 1) as i:
                for q in range(7):
                    sp.wait_ge(c_ot, 7 * i + q + 1)
                    passed(sp, "sp")
                    sp.dma_start(out[ds((7 * i + q) * P, P), :], ot[:, q, :]).then_inc(c_st[q], 16)
            for q in range(7):
                t = 7 * (n7 - 1) + q
                n = P if t < xpart else LAST
                sp.wait_ge(c_ot, t + 1)
                sp.dma_start(out[t * P:t * P + n, :], ot[0:n, q, :]).then_inc(c_st[q], 16)
            for q in range(7):
                sp.wait_ge(c_st[q], 16 * n7)

        @block.gpsimd
        def _(pool):
            pool.iota(iotaI[:, :], [[1, P]], base=0, channel_multiplier=0).then_inc(s_iota, 1)
            pool.iota(pidI[:, :], [[P, HI]], base=0, channel_multiplier=1).then_inc(s_iota, 1)
            pool.wait_ge(s_zero, 1)
            pool.dma_start(rec_d.rearrange("(p b) w -> p (b w)", p=P), zero).then_inc(s_scat, 16)
            pool.wait_ge(s_e, 1)
            with pool.Fori(0, NS // 2) as i:
                for u in range(2):
                    pool.wait_ge(s_o1, 2 * i + u + 1)
                    pool.wait_ge(s_cntp, 2 * i + u + 1)
                    passed(pool, "pool")
                    w = spread(ew[:, ds((2 * i + u) * SJ, SJ)].rearrange("p (j o) -> p j o", o=1), 2, NB)
                    pool.tensor_tensor(ohw[u], oh1[u], w, ALU.mult).then_inc(s_ow, 1)
            pool.sem_inc(s_wm, 2)
            pool.wait_ge(s_ridx, 1)
            with pool.Fori(0, NS) as s:
                for u in range(2):
                    pool.wait_ge(s_sub, 2 * s + u + 1)
                    pool.wait_ge(s_half, 2 * s + u + 1)
                    passed(pool, "pool")
                    w = spread(ew[:, ds(s * SJ + u * HJ, HJ)].rearrange("p (j o) -> p j o", o=1), 2, SUB)
                    pool.tensor_tensor(mv[u][:, :, :, 1], sub1h[u], w, ALU.mult).then_inc(s_wm, 1)
                pool.wait_ge(s_runc, s + 2)
                pool.wait_ge(s_sidx, s + 1)
                for k in range(HI):
                    pool.wait_ge(s_scat, 16 * (HI * s + k) + 16)
                    passed(pool, "pool")
                    pool.indirect_dma_start(rec_d, bass.IndirectOffsetOnAxis(sidx[:, k:k + 1], 0),
                                            sbuf[:, k * B * RW:(k + 1) * B * RW], None).then_inc(s_scat, 16)
            pool.wait_ge(s_scat, 16 * (HI * NS + 1))
            pool.sem_inc(s_scd, 1)
            pool.wait_ge(s_y, 16)
            with pool.Fori(0, NIT) as i:
                for u in range(UG):
                    pool.wait_ge(s_prep, UG * i + u + 1)
                    passed(pool, "pool")
                    for k in range(CH):
                        pool.indirect_dma_start(G[:, u % SLOTS, k, :], None, y_d,
                                                bass.IndirectOffsetOnAxis(gidx[:, u % SLOTS, k:k + 1], 0)
                                                ).then_inc(s_g[u % SLOTS], 16)

        @block.scalar
        def _(act):
            act.sem_inc(s_cntc, 2)
            act.sem_inc(s_runc, 1)
            act.sem_inc(b_tc, 2)
            act.sem_inc(c_g, 4)
            act.wait_ge(s_var, 1)
            act.activation(rstd[:, 0:NB], u49[:, :], ACT.Sqrt).then_inc(s_sqrt, 1)
            with act.Fori(0, NS // 2) as i:
                for u in range(2):
                    act.wait_ge(s_cntp, 2 * i + u + 3)
                    passed(act, "act")
                    act.copy(cnt[:, ds(2 * i + u, 1), :], bank[1 + u][:, 0:NB].rearrange("p (o h) -> p o h", o=1)).then_inc(s_cntc, 1)
            act.wait_ge(s_var, 2)
            act.activation(dinv[:, 0:NB], t49[:, :], ACT.Sqrt).then_inc(s_sqrt, 1)
            with act.Fori(0, NS) as s:
                act.wait_ge(s_runs, s + 1)
                act.wait_ge(s_scat, 16 * (HI * s) + 16)
                passed(act, "act")
                act.copy(sbuf[:, :], bank[3][:, 0:SUB * RW]).then_inc(s_runc, 1)
            act.wait_ge(s_acc, 1)
            act.wait_ge(s_scd, 1)
            with act.Fori(0, NB) as t:
                act.wait_ge(s_xTp, t + 1)
                passed(act, "act")
                act.copy(xs.rearrange("p (o d) -> p o d", o=1), X[:, ds(t, 1), :]).then_inc(s_xs, 1)
                act.wait_ge(s_xTp, t + 2)
                act.wait_ge(s_kvp, t + 1)
                passed(act, "act")
                act.copy(xT, bank[0][:, 0:D])
                act.copy(X[:, ds(t, 1), :], bank[0][:, 0:D].rearrange("p (o d) -> p o d", o=1)).then_inc(s_xT, 1)
                act.wait_ge(s_kvp, t + 2)
                act.wait_ge(s_pr, t + 1)
                act.wait_ge(s_dot, t + 1)
                passed(act, "act")
                act.activation(kvsq[:, 0:GD], bank[1][:, :], ACT.Square)
                act.activation(kvsq[:, GD:KV], bank[0][:, :], ACT.Square).then_inc(s_sq, 1)
                act.copy(vs, bank[0][:, :]).then_inc(s_vc, 1)
                act.wait_ge(s_pr, t + 2)
                passed(act, "act")
                act.activation(rr[:, :], pr[:, :], ACT.Sqrt).then_inc(s_sr, 1)
            act.wait_ge(s_m1, 1)
            for j in range(PAIRS):
                act.copy(Vh[:, j, :], bank[4 + j][:, 0:D])
            act.copy(WW[:, 0, :], bank[0][:, 0:D])
            act.copy(WW[:, 1, :], bank[3][:, 0:D]).then_inc(s_vh, 1)
            act.wait_ge(s_m2, 1)
            for m in range(DK):
                act.mul(Mx[:, m, :], bank[1 + m][:, 0:D], 1.0 / N).then_inc(s_mx, 1)
            act.wait_ge(s_b1, 1)
            with act.Fori(0, NT // 2) as i:
                for u in range(2):
                    act.wait_ge(a_tp, 2 * i + u + 1)
                    act.wait_ge(a_o, 2 * i + u + 1)
                    passed(act, "act")
                    act.copy(agT[:, u, :], bank[u][:, 0:D])
                    act.copy(xTs[:, u:u + 1, :], X[:, ds(2 * i + u, 1), :]).then_inc(a_T, 1)
                for u in range(2):
                    act.wait_ge(a_hp, 2 * i + u + 1)
                    passed(act, "act")
                    for m in range(DK):
                        ins = act.activation(hT[:, u, m * P:(m + 1) * P], bank[2 + u][:, m * P:(m + 1) * P], ACT.Relu,
                                             bias=b1c[:, m:m + 1])
                    ins.then_inc(a_h, 1)
            act.wait_ge(b_var, 1)
            act.activation(rstd[:, 0:NB], u49[:, :], ACT.Sqrt).then_inc(b_root, 1)
            with act.Fori(0, NT // 2) as i:
                for u in range(2):
                    act.wait_ge(b_tp, 2 * i + u + 3)
                    passed(act, "act")
                    act.copy(ACC[:, ds(2 * i + u, 1), :], bank[u][:, 0:D].rearrange("p (o d) -> p o d", o=1)).then_inc(b_tc, 1)
            with act.Fori(0, NB // 7) as i:
                for q, (nt, H1) in enumerate(((4, H1a), (3, H1b))):
                    act.wait_ge(c_y, 7 * i + 4 + 3 * q)
                    for f in range(FB):
                        act.wait_ge(c_h, (2 * i + q) * FB + f + 1)
                        passed(act, "act")
                        act.activation(H1[:, f, :], bank[f % 4][:, 0:nt * P], ACT.Gelu_apprx_tanh,
                                       bias=fb1[:, f:f + 1]).then_inc(c_g, 1)

        @block.tensor
        def _(pe):
            pe.sem_inc(s_cntp, 2)
            pe.sem_inc(s_h1, 2)
            pe.sem_inc(s_half, 2)
            pe.sem_inc(s_grp, 1)
            pe.sem_inc(s_xTp, 1)
            pe.sem_inc(s_kvp, 1)
            pe.sem_inc(s_dot, 1)
            pe.sem_inc(a_o, 2)
            pe.sem_inc(b_tp, 2)
            pe.sem_inc(c_y, 7)
            pe.wait_ge(s_const, 1)
            pe.matmul(bank[0][:, 0:NB], zcol[:, :], ones[:, 0:NB], start=True, stop=False, skip_group_check=True)
            with pe.Fori(0, NS // 2) as i:
                for u in range(2):
                    s = 2 * i + u
                    pe.wait_ge(s_o1, s + 1)
                    pe.wait_ge(s_cntc, s + 1)
                    for j in range(SJ):
                        pe.matmul(bank[1 + u][:, 0:NB], onesb[0:EP, :], oh1[u][:, j, :], start=(j == 0), stop=(j == SJ - 1))
                    pe.wait_ge(s_ow, s + 1)
                    for q in range(2):
                        pe.wait_ge(s_rl, 2 * s + q + 1)
                        for j in range(HJ):
                            ins = pe.matmul(bank[0][:, 0:NB], rl1h[q][:, j, :], ohw[u][:, q * HJ + j, :],
                                            start=False, stop=False, skip_group_check=True)
                        ins.then_inc(s_h1, 1)
                    pe.sem_inc(s_seen["pe"], 1)
                    pe.wait_ge(s_h1, 2 * s + 4)
                    pe.sem_inc(s_cntp, 1)
            pe.matmul(bank[0][:, 0:NB], zcol[:, :], ones[:, 0:NB], start=False, stop=True, skip_group_check=True).then_inc(s_deg, 1)
            with pe.Fori(0, NS) as s:
                pe.wait_ge(s_cn, s + 1)
                pe.matmul(bank[2][0:EP, 0:NB], strict[0:EP, 0:EP], cn[:, :], start=True, stop=True).then_inc(s_cross, 1)
                pe.wait_ge(s_runc, s + 1)
                for u in range(2):
                    pe.wait_ge(s_key, 2 * s + u + 1)
                    pe.wait_ge(s_lo, 2 * s + u + 1)
                    pe.wait_ge(s_wm, 2 * s + u + 3)
                    for j in range(HJ):
                        ins = pe.matmul(bank[3][:, 0:SUB * RW], lo1h[u][:, j, :], mv[u][:, j, :, :].rearrange("p a b -> p (a b)"),
                                        start=(u == 0 and j == 0), stop=(u == 1 and j == HJ - 1))
                    ins.then_inc(s_half, 1)
                pe.wait_ge(s_half, 2 * s + 4)
                pe.sem_inc(s_runs, 1)
            pe.wait_ge(s_w, 16 * 12)
            pe.wait_ge(s_wc, 1)

            def group(g, u, use):
                pe.wait_ge(s_g[u % SLOTS], 16 * CH * use)
                pe.wait_ge(s_prep, g + 1)
                for k in range(CH):
                    ins = pe.matmul(bank[3 + u % SLOTS][:, 0:D], OH[:, u % SLOTS, k, :], G[:, u % SLOTS, k, :],
                                    start=(k == 0), stop=(k == CH - 1))
                ins.then_inc(s_grp, 1)

            def kv_transpose(t):
                pe.wait_ge(s_xs, t + 1)
                for m in range(DK):
                    ins = pe.transpose(bank[0][:, m * P:(m + 1) * P], xs[:, m * P:(m + 1) * P], ident[:, :])
                ins.then_inc(s_xTp, 1)

            def kv_multiply(t):
                pe.wait_ge(s_xT, t + 1)
                pe.wait_ge(s_kn, t + 1)
                for b, o in ((1, 0), (0, GD)):
                    for k in range(DK):
                        ins = pe.matmul(bank[b][:, :], xT[:, k * P:(k + 1) * P], wkv[:, k, o:o + GD], start=(k == 0), stop=(k == DK - 1))
                ins.then_inc(s_kvp, 1)

            def kv_dots(t):
                pe.wait_ge(s_kn, t + 2)
                pe.wait_ge(s_vc, t + 1)
                for j in range(PAIRS):
                    ins = pe.matmul(bank[2][:, j * P:(j + 1) * P], kn[:, j * P:(j + 1) * P], vs[:, j * P:(j + 1) * P],
                                    start=False, stop=False, skip_group_check=True)
                ins.then_inc(s_dot, 1)

            pe.matmul(bank[2][:, 0:GD], zcol[:, :], wkv[:, 0, 0:GD], start=True, stop=False, skip_group_check=True)
            with pe.Fori(0, NB) as i:
                kv_transpose(i)
                for u in range(UG):
                    group(UG * i + u, u, 2 * i + u // SLOTS + 1)
                    if u == 1:
                        kv_multiply(i)
                    if u == 8:
                        kv_dots(i)
            for i in range(NB, NIT):
                for u in range(UG):
                    group(UG * i + u, u, 2 * i + u // SLOTS + 1)
            pe.matmul(bank[2][:, 0:GD], zcol[:, :], wkv[:, 0, 0:GD], start=False, stop=True, skip_group_check=True).then_inc(s_dot, 1)
            pe.wait_ge(s_added, 1)
            for kb, b in ((0, 0), (1, 3)):
                for k in range(DK):
                    pe.matmul(bank[b][:, 0:D], WT[:, k, kb * P:(kb + 1) * P], W1[:, k, :], start=(k == 0), stop=(k == DK - 1))
            for m in range(DK):
                for k in range(DK):
                    pe.matmul(bank[3][:, D + m:D + m + 1], W1[:, k, m * P:(m + 1) * P], bc[:, k:k + 1], start=(k == 0), stop=(k == DK - 1))
            pe.wait_ge(s_dd, 1)
            pe.wait_ge(s_wf, 16 * 4)
            for j in range(PAIRS):
                ins = pe.matmul(bank[4 + j][:, 0:D], dots[:, j, :], wq[:, j, :], start=True, stop=True)
            ins.then_inc(s_m1, 1)
            pe.wait_ge(s_vh, 1)
            for m in range(DK):
                for j in range(PAIRS):
                    ins = pe.matmul(bank[1 + m][:, 0:D], Vh[:, j, m * P:(m + 1) * P], wo[:, j, :], start=(j == 0), stop=(j == PAIRS - 1))
            ins.then_inc(s_m2, 1)
            pe.wait_ge(s_mx, DK)
            with pe.Fori(0, NT // 2) as i:
                for u in range(2):
                    pe.wait_ge(a_ag, 2 * i + u + 1)
                    for m in range(DK):
                        ins = pe.transpose(bank[u][:, m * P:(m + 1) * P], ag[:, u, m * P:(m + 1) * P], ident[:, :])
                    ins.then_inc(a_tp, 1)
                for u in range(2):
                    pe.wait_ge(a_T, 2 * i + u + 1)
                    for m in range(DK):
                        for k in range(DK):
                            ins = pe.matmul(bank[2 + u][:, m * P:(m + 1) * P], WW[:, k, m * P:(m + 1) * P],
                                            agT[:, u, k * P:(k + 1) * P], start=(k == 0), stop=(k == DK - 1))
                    ins.then_inc(a_hp, 1)
                for u in range(2):
                    pe.wait_ge(a_h, 2 * i + u + 1)
                    pe.wait_ge(a_x1, 2 * i + u + 1)
                    for k in range(DK):
                        pe.matmul(bank[4 + u][:, 0:D], hT[:, u, k * P:(k + 1) * P], W2[:, k, :], start=(k == 0), stop=False)
                    for k in range(DK):
                        ins = pe.matmul(bank[4 + u][:, 0:D], xTs[:, u, k * P:(k + 1) * P], Mx[:, k, :], start=False, stop=(k == DK - 1))
                    ins.then_inc(a_o, 1)
            with pe.Fori(0, NT // 2) as i:
                for u in range(2):
                    pe.wait_ge(b_xn, 2 * i + u + 1)
                    pe.wait_ge(b_tc, 2 * i + u + 1)
                    for m in range(DK):
                        ins = pe.transpose(bank[u][:, m * P:(m + 1) * P], xn2[:, u, m * P:(m + 1) * P], ident[:, :])
                    ins.then_inc(b_tp, 1)
            pe.wait_ge(b_tc, NT + 2)
            for n in range(2):
                with pe.Fori(0, 16) as i:
                    pe.wait_ge(k_cnt, 16 * n + i + 1)
                    pe.matmul(bank[7][:, 0:1], ones[:, :], tk[3][:, :], start=True, stop=True).then_inc(k_sum, 1)
            pe.wait_ge(k_cnt, 33)
            pe.matmul(bank[7][:, 0:1], ones[:, :], tk[3][:, :], start=True, stop=True)
            pe.matmul(bank[6][:, 0:NB], strict[:, :], eqm[:, :], start=True, stop=True)
            pe.matmul(bank[5][:, 0:NB], ones[:, :], eqm[:, :], start=True, stop=True).then_inc(k_sum, 1)
            pe.wait_ge(k_cnt, 34)
            with pe.Fori(0, NB // 7) as i:
                for q, (nt, H1) in enumerate(((4, H1a), (3, H1b))):
                    for f in range(FB):
                        pe.wait_ge(c_g, (2 * i + q) * FB + f + 1)
                        for k in range(DK):
                            ins = pe.matmul(bank[f % 4][:, 0:nt * P].rearrange("p (t n) -> p t n", n=P), w1s[:, k, f * P:(f + 1) * P],
                                            ACC[:, ds(7 * i + 4 * q, nt), k * P:(k + 1) * P], start=(k == 0), stop=(k == DK - 1))
                        ins.then_inc(c_h, 1)
                    pe.wait_ge(c_g, (2 * i + q + 1) * FB + 4)
                    for a in range(nt):
                        pe.wait_ge(c_free, 7 * i + 4 * q + a + 1)
                        for f in range(FB):
                            ins = pe.matmul(bank[4 + (4 * q + a) % 4][:, 0:D], H1[:, f, a * P:(a + 1) * P], w2s[:, f, :],
                                            start=(f == 0), stop=(f == FB - 1))
                        ins.then_inc(c_y, 1)

        @block.vector
        def _(dve):
            c = Chain(dve, s_dve)
            dve.memset(X[:, xpart:NT, :], 0.0).then_inc(s_xpad, 1)
            dve.memset(zero, 0.0).then_inc(s_zero, 1)
            dve.memset(ones[:, :], 1.0)
            dve.memset(zcol[:, :], 0.0)
            dve.memset(onesb[:, :], 1.0)
            dve.memset(dinv[:, NB:NT], 0.0)
            dve.memset(mvar[:, NB:NT, :], 0.0)
            dve.memset(rstd[:, NB:NT], 0.0)
            dve.memset(Fx[:, 0:1], 0.0)
            dve.sem_inc(a_x1, 2)
            dve.sem_inc(s_pr, 1)
            dve.sem_inc(s_kn, 1)
            dve.sem_inc(c_free, 3)
            dve.wait_ge(s_iota, 2)
            c.link(dve.tensor_copy(iota[:, :], iotaI[:, :]))
            c.link(dve.tensor_copy(pid[:, :], pidI[:, :]))
            c.link(dve.tensor_scalar(ident[:, :], iota[:, :], pid[:, 0:1], None, ALU.is_equal))
            c.link(dve.tensor_scalar(strict[:, :], iota[:, :], pid[:, 0:1], None, ALU.is_gt))
            dve.sem_inc(s_const, 1)
            dve.wait_ge(s_edges, 48)
            c.link(dve.tensor_scalar(tmpI, srcI, 7, None, ALU.arith_shift_right))
            c.link(dve.tensor_copy(hf, tmpI))
            c.link(dve.tensor_scalar(tmpI, srcI, P - 1, None, ALU.bitwise_and))
            c.link(dve.tensor_copy(rlof, tmpI))
            c.link(dve.tensor_scalar(tmpI, dstI, 7, None, ALU.logical_shift_left))
            c.link(dve.tensor_copy(keyf, tmpI))
            c.link(dve.tensor_tensor(keyf, keyf, rlof, ALU.add))
            dve.sem_inc(s_e, 1)

            def row_stats(src):
                with dve.Fori(0, NB) as t:
                    c.enter(t, 1)
                    c.mark(dve.bn_stats(row(st[:, ds(t, 1), :]), row(src[:, ds(t, 1), :])))
                c.leave(NB)
                c.wait()
                for t in range(NB):
                    ins = dve.bn_aggr(mvar[:, t, :], st[:, t, :])
                c.link(ins)
                c.link(dve.tensor_scalar(u49[:, :], mvar[:, 0:NB, 1], EPS, None, ALU.add))

            def inverse_root(r, v, tmp):
                c.link(dve.reciprocal(r, r))
                c.link(dve.tensor_tensor(tmp, r, r, ALU.mult))
                c.link(dve.tensor_tensor(tmp, tmp, v, ALU.mult))
                c.link(dve.tensor_scalar(tmp, tmp, -0.5, 1.5, ALU.mult, ALU.add))
                c.link(dve.tensor_tensor(r, r, tmp, ALU.mult))

            dve.wait_ge(s_x, 32)
            row_stats(X)
            dve.sem_inc(s_var, 1)
            dve.wait_ge(s_sqrt, 1)
            inverse_root(rstd[:, 0:NB], u49[:, :], v49[:, :])
            with dve.Fori(0, NB) as t:
                c.enter(t, 1)
                xv = row(X[:, ds(t, 1), :])
                c.mark(dve.tensor_scalar(xv, xv, mvar[:, ds(t, 1), 0], rstd[:, ds(t, 1)], ALU.subtract, ALU.mult))
            c.leave(NB)
            c.wait()
            with dve.Fori(0, NS // 2) as i:
                for u in range(2):
                    s = 2 * i + u
                    dve.wait_ge(s_cntp, s + 1)
                    hv = spread(hf[:, ds(s * SJ, SJ)].rearrange("p (j o) -> p j o", o=1), 2, NB)
                    iv = spread(iota[0:EP, 0:NB].rearrange("p (o h) -> p o h", o=1), 1, SJ)
                    dve.tensor_tensor(oh1[u], hv, iv, ALU.is_equal).then_inc(s_o1, 1)
                    for q in range(2):
                        dve.wait_ge(s_h1, 2 * s + q + 1)
                        rv = spread(rlof[:, ds(s * SJ + q * HJ, HJ)].rearrange("p (j o) -> p j o", o=1), 2, P)
                        iv = spread(iota[0:EP, :].rearrange("p (o h) -> p o h", o=1), 1, HJ)
                        dve.tensor_tensor(rl1h[q], rv, iv, ALU.is_equal).then_inc(s_rl, 1)
            dve.wait_ge(s_deg, 1)
            c.link(dve.tensor_scalar(u49[:, :], bank[0][:, 0:NB], 1.0, None, ALU.add))
            c.link(dve.tensor_scalar(sel[:, :], u49[:, :], 0.0, None, ALU.is_gt))
            c.link(dve.tensor_scalar(t49[:, :], u49[:, :], 1e-30, None, ALU.max))
            dve.sem_inc(s_var, 1)
            dve.wait_ge(s_cntc, NS + 2)
            dve.wait_ge(s_ow, NS)
            dve.wait_ge(s_scat, 16)
            flat = cnt.rearrange("p s h -> p (s h)")

            def ceil_shift(outf, tmp_i, inf, n):
                c.link(dve.tensor_scalar(tmp_i, inf, float(2 ** n - 1), None, ALU.add))
                c.link(dve.tensor_scalar(tmp_i, tmp_i, n, None, ALU.arith_shift_right))
                c.link(dve.tensor_copy(outf, tmp_i))

            def restart(major):
                c.link(dve.memset(keep, 1.0))
                c.link(dve.memset(keep.rearrange("p (a b) -> p a b", a=major)[:, :, 0:1], 0.0))

            ceil_shift(pcf, inc.bitcast(I32), flat, 4)
            pc3 = pcf.rearrange("p (s h) -> p s h", s=NS)
            restart(NS)
            c.link(dve.tensor_tensor_scan(inc, keep, pcf, 0.0, ALU.mult, ALU.add))
            inc3 = inc.rearrange("p (s h) -> p s h", s=NS)
            c.link(dve.tensor_tensor(lbx[:, :, 0:NB], inc3, pc3, ALU.subtract))
            c.link(dve.tensor_copy(lbx[:, :, NB:NB + 1], inc3[:, :, NB - 1:NB]))
            c.link(dve.tensor_copy(pcT, pc3.rearrange("p s h -> p h s")))
            restart(NB)
            c.link(dve.tensor_tensor_scan(inc, keep, pcT.rearrange("p h s -> p (h s)"), 0.0, ALU.mult, ALU.add))
            incT = inc.rearrange("p (h s) -> p h s", s=NS)
            ceil_shift(tpf[:, :], v49[:, :].bitcast(I32), incT[:, :, NS - 1], 5)
            c.link(dve.tensor_tensor_scan(ginc[:, :], ones[:, 0:NB], tpf[:, :], 0.0, ALU.mult, ALU.add))
            c.link(dve.tensor_tensor(tpf[:, :], ginc[:, :], tpf[:, :], ALU.subtract))
            c.link(dve.tensor_scalar(tpf[:, :], tpf[:, :], float(BPG), None, ALU.mult))
            c.link(dve.tensor_tensor(incT, incT, pcT, ALU.subtract))
            c.link(dve.tensor_tensor(incT, incT, spread(tpf[:, :].rearrange("p (h o) -> p h o", o=1), 2, NS), ALU.add))
            c.link(dve.tensor_tensor(big[:, :, 0:NB], incT.rearrange("p h s -> p s h"), lbx[:, :, 0:NB], ALU.subtract))
            c.link(dve.memset(big[:, :, NB:NB + 1], float(SPARE)))
            c.link(dve.tensor_copy(dlt[:, :, 0:1], big[:, :, 0:1]))
            c.link(dve.tensor_tensor(dlt[:, :, 1:NB + 1], big[:, :, 1:NB + 1], big[:, :, 0:NB], ALU.subtract))
            for k in range(HI):
                c.link(dve.scalar_tensor_tensor(big, lbx, pid[:, k:k + 1], dlt, ALU.is_le, ALU.mult))
                c.link(dve.tensor_reduce(ridxf[:, :], big, AX.X, ALU.add))
                c.link(dve.tensor_scalar(ridx[:, :, k], ridxf[:, :], pid[:, k:k + 1], None, ALU.add))
            for a in range(4):
                c.link(dve.tensor_scalar(hm[:, a:a + 1], pid[:, 0:1], float(a * P), None, ALU.add))
            for a in range(4):
                c.link(dve.tensor_scalar(hm49[:, a, :], ginc[:, :], hm[:, a:a + 1], None, ALU.is_le))
            c.link(dve.tensor_reduce(hm[:, :], hm49[:, :, :], AX.X, ALU.add))
            c.link(dve.tensor_copy(hmI[:, :], hm[:, :]))
            dve.sem_inc(s_hm, 1)
            dve.wait_ge(s_sqrt, 2)
            inverse_root(dinv[:, 0:NB], t49[:, :], u49[:, :])
            c.link(dve.tensor_tensor(dinv[:, 0:NB], dinv[:, 0:NB], sel[:, :], ALU.mult))
            c.link(dve.tensor_scalar(lbx, lbx, float(B), None, ALU.mult))
            c.link(dve.memset(Fx[:, 0:1], 0.0))
            dve.sem_inc(s_ridx, 1)
            F3 = Fx[:, 1:1 + NB * SJ].rearrange("p (h j) -> p h j", j=SJ)
            last = F3[:, :, SJ - 1]
            prev = Fx[:, 0:NB * SJ].rearrange("p (h j) -> p h j", j=SJ)[:, :, 0]
            with dve.Fori(0, NS) as s:
                c.enter(s, 14)
                hv = spread(hf[:, ds(s * SJ, SJ)].rearrange("p (o j) -> p o j", o=1), 1, NB)
                iv = spread(iota[0:EP, 0:NB].rearrange("p (h o) -> p h o", o=1), 2, SJ)
                c.link(dve.tensor_tensor(O2, hv, iv, ALU.is_equal))
                c.link(dve.tensor_tensor_scan(Fx[:, 1:1 + NB * SJ], spread(ones[0:EP, 0:1], 1, NB * SJ),
                                              O2.rearrange("p h j -> p (h j)"), 0.0, ALU.mult, ALU.add))
                dve.tensor_tensor(cn[:, :], last, prev, ALU.subtract).then_inc(s_cn, 1)
                dve.wait_ge(s_cross, s + 1)
                c.link(dve.scalar_tensor_tensor(A2[:, :], bank[2][0:EP, 0:NB], -1.0, prev, ALU.add, ALU.subtract))
                c.link(dve.tensor_tensor(A2[:, :], A2[:, :], row(lbx[0:EP, ds(s, 1), 0:NB]), ALU.add))
                c.link(dve.tensor_tensor(V2, F3, spread(A2[:, :].rearrange("p (h o) -> p h o", o=1), 2, SJ), ALU.add))
                c.link(dve.tensor_tensor(V2, V2, O2, ALU.mult))
                c.link(dve.tensor_reduce(posf[:, :], V2.rearrange("p h j -> p j h"), AX.X, ALU.add))
                c.link(dve.tensor_copy(posI[:, :], posf[:, :]))
                c.link(dve.tensor_scalar(poaI[:, :], posI[:, :], 4, P - 1, ALU.arith_shift_right, ALU.bitwise_and))
                c.link(dve.tensor_copy(lof[:, :], poaI[:, :]))
                c.link(dve.tensor_scalar(poaI[:, :], posI[:, :], 11, 4, ALU.arith_shift_right, ALU.logical_shift_left))
                c.link(dve.tensor_scalar(pobI[:, :], posI[:, :], B - 1, None, ALU.bitwise_and))
                c.link(dve.tensor_tensor(pobI[:, :], pobI[:, :], poaI[:, :], ALU.bitwise_or))
                c.link(dve.tensor_copy(subf[:, :], pobI[:, :]))
                for u in range(2):
                    dve.wait_ge(s_half, 2 * s + u + 1)
                    dve.wait_ge(s_wm, 2 * s + u + 1)
                    j0, j1 = u * HJ, (u + 1) * HJ
                    sv = spread(subf[:, j0:j1].rearrange("p (j o) -> p j o", o=1), 2, SUB)
                    iv = spread(iota[0:EP, 0:SUB].rearrange("p (o h) -> p o h", o=1), 1, HJ)
                    dve.tensor_tensor(sub1h[u], sv, iv, ALU.is_equal).then_inc(s_sub, 1)
                    lv = spread(lof[:, j0:j1].rearrange("p (j o) -> p j o", o=1), 2, P)
                    iv = spread(iota[0:EP, :].rearrange("p (o h) -> p o h", o=1), 1, HJ)
                    dve.tensor_tensor(lo1h[u], lv, iv, ALU.is_equal).then_inc(s_lo, 1)
                    dve.wait_ge(s_sub, 2 * s + u + 1)
                    kv = spread(keyf[:, ds(s * SJ + j0, HJ)].rearrange("p (j o) -> p j o", o=1), 2, SUB)
                    dve.tensor_tensor(mv[u][:, :, :, 0], sub1h[u], kv, ALU.mult).then_inc(s_key, 1)
                dve.wait_ge(s_scat, 16 * (HI * s) + 16)
                passed(dve, "dve")
                dve.tensor_copy(sidx[:, :].rearrange("p (o k) -> p o k", o=1), ridx[:, ds(s, 1), :]).then_inc(s_sidx, 1)
            c.leave(NS)
            dve.wait_ge(s_half, 2 * NS + 2)
            dve.wait_ge(s_wm, 2 * NS + 2)
            passed(dve, "dve")
            with dve.Fori(0, NT) as t:
                c.enter(t, 1)
                c.mark(dve.tensor_scalar(row(ACC[:, ds(t, 1), :]), row(X[:, ds(t, 1), :]), dinv[:, ds(t, 1)], None, ALU.mult))
            c.leave(NT)
            c.wait()
            dve.sem_inc(s_acc, 1)
            dve.wait_ge(s_w, 16 * 12)
            w3 = kvf.rearrange("p (h w) -> p h w", w=HW)
            wm = wmean[:, :]
            c.link(dve.tensor_reduce(wm, w3, AX.X, ALU.add))
            c.link(dve.tensor_scalar(wm, wm, 1.0 / HW, None, ALU.mult))
            c.link(dve.tensor_tensor(w3, w3, spread(wm.rearrange("p (h o) -> p h o", o=1), 2, HW), ALU.subtract))
            dve.sem_inc(s_wc, 1)
            dve.wait_ge(s_rec, 64)
            r4 = rec.rearrange("p g (c w) -> p g c w", w=RW)
            c.link(dve.memset(cidx[:, NG:, :], 0.0))
            c.link(dve.memset(rlo[:, NG:, :], 0.0))
            c.link(dve.memset(rec[:, NG:, :], 0.0))
            rloI = rlo_i
            c.link(dve.tensor_copy(cidxI[:, 0:NG, :], r4[:, 0:NG, :, 0]))
            c.link(dve.tensor_scalar(rloI[:, 0:NG, :], cidxI[:, 0:NG, :], P - 1, None, ALU.bitwise_and))
            c.link(dve.tensor_copy(rlo[:, 0:NG, :], rloI[:, 0:NG, :]))
            c.link(dve.tensor_scalar(cidxI[:, 0:NG, :], cidxI[:, 0:NG, :], 7, None, ALU.arith_shift_right))
            dve.wait_ge(s_hrow, 16)
            dve.wait_ge(s_y, 16)
            dve.sem_inc(s_seen["dve"], 1)

            def prep(g, slot):
                for k in range(CH):
                    dve.tensor_scalar(OH[:, slot, k, :], iota[:, :], rlo[:, ds(g, 1), k],
                                      recw[:, ds(g, 1), k], ALU.is_equal, ALU.mult)
                dve.tensor_copy(gidx[:, slot:slot + 1, :], cidxI[:, ds(g, 1), :]).then_inc(s_prep, 1)

            def add_group(g, slot):
                h = dve.value_load(hrow[0:1, ds(g, 1)], min_val=0, max_val=NB)
                a = row(ACC[:, ds(h, 1), :])
                c.wait()
                dve.wait_ge(s_grp, g + 2)
                c.mark(dve.tensor_tensor(a, a, bank[3 + slot][:, 0:D], ALU.add))

            for g in range(SLOTS - 1):
                prep(g, g)

            def body(i, with_kv):
                for u in range(UG):
                    g = UG * i + u
                    dve.wait_ge(s_grp, g + 1)
                    prep(g + SLOTS - 1, (u + SLOTS - 1) % SLOTS)
                    add_group(g, u % SLOTS)
                    if with_kv and u == 4:
                        dve.wait_ge(s_sq, i + 1)
                        c.link(dve.tensor_reduce(ss[:, :], kvsq.rearrange("p (h w) -> p h w", w=HW), AX.X, ALU.add))
                        c.link(dve.tensor_scalar(ss[:, :], ss[:, :], 1.0 / HW, EPS, ALU.mult, ALU.add))
                        c.link(dve.tensor_tensor(pr[:, :], ss[:, 0:HEADS], ss[:, HEADS:], ALU.mult))
                        dve.sem_inc(s_pr, 1)
                    if with_kv and u == 6:
                        dve.wait_ge(s_sr, i + 1)
                        inverse_root(rr[:, :], pr[:, :], r2[:, :])
                        dve.wait_ge(s_dot, i + 1)
                        dve.tensor_tensor(kn.rearrange("p (h w) -> p h w", w=HW), bank[1][:, :].rearrange("p (h w) -> p h w", w=HW),
                                          spread(rr[:, :].rearrange("p (h o) -> p h o", o=1), 2, HW), ALU.mult).then_inc(s_kn, 1)

            with dve.Fori(0, NB) as i:
                c.enter(i, UG + 8)
                body(i, True)
            c.leave(NB)
            for i in range(NB, NIT):
                body(i, False)
            c.wait()
            dve.wait_ge(s_dot, NB + 2)
            dve.sem_inc(s_added, 1)
            c.link(dve.memset(dots, 0.0))
            for j in range(PAIRS):
                for q in range(2):
                    r0, r1 = q * HW, (q + 1) * HW
                    ins = dve.tensor_copy(dots[r0:r1, j, r0:r1], bank[2][r0:r1, j * P + r0:j * P + r1])
                    c.mark(ins)
            c.wait()
            dve.sem_inc(s_dd, 1)
            c.link(dve.tensor_tensor(b2o[:, :], b2o[:, :], brow[:, :], ALU.add))
            dve.wait_ge(s_vh, 1)
            c.link(dve.tensor_tensor(b1c[:, :], b1c[:, :], bank[3][:, D:D + DK], ALU.add))
            dve.sem_inc(s_b1, 1)
            with dve.Fori(0, NT // 2) as i:
                c.enter(i, 4)
                for u in range(2):
                    t = 2 * i + u
                    dve.tensor_scalar(ag[:, u, :], row(ACC[:, ds(t, 1), :]), dinv[:, ds(t, 1)], None, ALU.mult).then_inc(a_ag, 1)
                for u in range(2):
                    t = 2 * i + u
                    dve.wait_ge(a_xin[u], 16 * i + 16)
                    c.link(dve.tensor_tensor(xin[:, u, :], xin[:, u, :], b2o[:, :], ALU.add))
                    dve.wait_ge(a_o, t + 3)
                    c.link(dve.tensor_tensor(row(ACC[:, ds(t, 1), :]), bank[4 + u][:, 0:D], xin[:, u, :], ALU.add))
                    dve.sem_inc(a_x1, 1)
            c.leave(NT // 2)
            row_stats(ACC)
            dve.sem_inc(b_var, 1)
            dve.wait_ge(b_root, 1)
            inverse_root(rstd[:, 0:NB], u49[:, :], v49[:, :])
            with dve.Fori(0, NT // 2) as i:
                c.enter(i, 6)
                for u in range(2):
                    t = 2 * i + u
                    dve.wait_ge(b_tp, t + 1)
                    c.link(dve.tensor_scalar(xn2[:, u, :], row(ACC[:, ds(t, 1), :]), mvar[:, ds(t, 1), 0], rstd[:, ds(t, 1)],
                                             ALU.subtract, ALU.mult))
                    dve.tensor_tensor(row(X[:, ds(t, 1), :]), row(ACC[:, ds(t, 1), :]), xn2[:, u, :], ALU.add).then_inc(b_xn, 1)
                    c.link(dve.tensor_tensor_reduce(yt[:, u, :], xn2[:, u, :], wr[:, :], 1.0, 0.0, ALU.mult, ALU.add, wcol[:, :]))
                    dve.sem_inc(s_seen["dve"], 1)
                    c.link(dve.tensor_copy(wt[:, ds(t, 1)], wcol[:, :]))
            c.leave(NT // 2)
            c.link(dve.tensor_scalar(wt[:, 0:NB], wt[:, 0:NB], brc[:, 0:1], None, ALU.add))
            bits = wt[:, 0:NB].bitcast(I32)
            c.link(dve.tensor_scalar(keyI[:, :], bits, 31, 0x7FFFFFFF, ALU.arith_shift_right, ALU.bitwise_and))
            c.link(dve.tensor_tensor(keyI[:, :], keyI[:, :], bits, ALU.bitwise_xor))
            c.link(dve.tensor_scalar(kbI[:, :], keyI[:, :], 16, None, ALU.arith_shift_right))
            c.link(dve.tensor_scalar(khi[:, :], kbI[:, :], 32768.0, None, ALU.add))
            c.link(dve.tensor_scalar(kbI[:, :], keyI[:, :], 0xFFFF, None, ALU.bitwise_and))
            c.link(dve.tensor_copy(klo[:, :], kbI[:, :]))
            c.link(dve.tensor_scalar(tk[4][:, :], pid[:, 0:1], float(LAST), None, ALU.is_lt))
            c.link(dve.tensor_scalar(tk[5][:, :], tk[4][:, :], -1.0, None, ALU.add))
            c.link(dve.tensor_scalar(khi[:, xpart:NB], khi[:, xpart:NB], tk[4][:, :], tk[5][:, :], ALU.mult, ALU.add))
            top, bit, cand, cntc, ge, need = (t[:, :] for t in tk)

            def search(values, n):
                c.link(dve.memset(top, 0.0))
                c.link(dve.memset(bit, 32768.0))
                with dve.Fori(0, 16) as i:
                    c.enter(i, 6)
                    c.link(dve.tensor_tensor(cand, top, bit, ALU.add))
                    c.link(dve.tensor_scalar(gtm[:, :], values, cand, None, ALU.is_ge))
                    c.link(dve.tensor_reduce(cntc, gtm[:, :], AX.X, ALU.add))
                    dve.sem_inc(k_cnt, 1)
                    dve.wait_ge(k_sum, 16 * n + i + 1)
                    c.link(dve.tensor_scalar(ge, bank[7][:, 0:1], float(TOP), bit, ALU.is_ge, ALU.mult))
                    c.link(dve.tensor_tensor(top, top, ge, ALU.add))
                    c.link(dve.tensor_scalar(bit, bit, 0.5, None, ALU.mult))
                c.leave(16)

            search(khi[:, :], 0)
            c.link(dve.tensor_scalar(gtm[:, :], khi[:, :], top, 65537.0, ALU.is_gt, ALU.mult))
            c.link(dve.tensor_scalar(eqm[:, :], khi[:, :], top, None, ALU.is_equal))
            c.link(dve.tensor_scalar(klo[:, :], klo[:, :], 1.0, None, ALU.add))
            c.link(dve.tensor_tensor(comb[:, :], klo[:, :], eqm[:, :], ALU.mult))
            c.link(dve.tensor_tensor(comb[:, :], comb[:, :], gtm[:, :], ALU.add))
            c.link(dve.tensor_scalar(comb[:, :], comb[:, :], -1.0, None, ALU.add))
            search(comb[:, :], 1)
            c.link(dve.tensor_scalar(eqm[:, :], comb[:, :], top, None, ALU.is_equal))
            c.link(dve.tensor_scalar(sel[:, :], comb[:, :], top, None, ALU.is_gt))
            c.link(dve.tensor_reduce(cntc, sel[:, :], AX.X, ALU.add))
            dve.sem_inc(k_cnt, 1)
            dve.wait_ge(k_sum, 33)
            c.link(dve.tensor_scalar(need, bank[7][:, 0:1], -1.0, float(TOP), ALU.mult, ALU.add))
            c.link(dve.tensor_copy(v49[:, :], bank[5][:, 0:NB]))
            c.link(dve.tensor_tensor_scan(u49[:, :], ones[:, 0:NB], v49[:, :], 0.0, ALU.mult, ALU.add))
            c.link(dve.tensor_tensor(u49[:, :], u49[:, :], v49[:, :], ALU.subtract))
            c.link(dve.tensor_tensor(u49[:, :], u49[:, :], bank[6][:, 0:NB], ALU.add))
            dve.sem_inc(k_cnt, 1)
            c.link(dve.tensor_scalar(u49[:, :], u49[:, :], need, None, ALU.is_lt))
            c.link(dve.tensor_tensor(u49[:, :], u49[:, :], eqm[:, :], ALU.mult))
            c.link(dve.tensor_tensor(sel[:, :], sel[:, :], u49[:, :], ALU.add))
            c.link(dve.tensor_tensor(wsel[:, :], wt[:, 0:NB], sel[:, :], ALU.mult))

            def finish(i, first):
                for q in range(7):
                    t = 7 * i + q
                    if not first:
                        dve.wait_ge(c_st[q], 16 * i)
                    dve.wait_ge(c_y, t + 8)
                    passed(dve, "dve")
                    dve.tensor_tensor(ot[:, q, :], bank[4 + q % 4][:, 0:D], fb2[:, :], ALU.add).then_inc(c_free, 1)
                    dve.wait_ge(c_free, t + 4)
                    dve.scalar_tensor_tensor(ot[:, q, :], ot[:, q, :], wsel[:, ds(t, 1)], row(X[:, ds(t, 1), :]),
                                             ALU.mult, ALU.add).then_inc(c_ot, 1)

            finish(0, True)
            with dve.Fori(1, NB // 7) as i:
                finish(i, False)


_INS = ['x', 'src', 'dst', 'edge_weight', 'L0_gnn_b', 'L0_gnn_W1', 'L0_gnn_b1', 'L0_gnn_W2', 'L0_gnn_b2',
        'L0_mix_b_out', 'L0_ffn_wr', 'L0_ffn_br', 'L0_ffn_w1', 'L0_ffn_b1', 'L0_ffn_w2', 'L0_ffn_b2']


def kernel(**inputs):
    import numpy as _np
    import concourse.bacc as _bacc
    from concourse import mybir as _mybir
    from concourse.bass_utils import run_bass_kernel_spmd as _run

    nc = _bacc.Bacc("TRN2", target_bir_lowering=False, num_devices=1)
    qkv = _np.asarray(inputs['L0_mix_w_qkv'])
    inner = qkv.shape[0] // 3
    laid = {name: _np.asarray(inputs[name]) for name in _INS}
    laid['wq'] = qkv[:inner]
    laid['kvT'] = qkv[inner:].T
    laid['woT'] = _np.asarray(inputs['L0_mix_w_out']).T
    laid['WT'] = _np.asarray(inputs['L0_gnn_W']).T
    arrays, aps = {}, {}
    for name, a in laid.items():
        a = _np.ascontiguousarray(a)
        arrays[f"in_{name}_dram"] = a
        aps[name] = nc.dram_tensor(f"in_{name}_dram", a.shape, _mybir.dt.from_np(a.dtype), kind="ExternalInput").ap()
    out = nc.dram_tensor("out_0_dram", laid['x'].shape, _mybir.dt.float32, kind="ExternalOutput").ap()
    gps_layer(nc, aps, out)
    r = _run(nc, [arrays], core_ids=[0])
    return r.results[0]["out_0_dram"]
```

```python
from contextlib import ExitStack

import concourse.bass as bass
from concourse import mybir

ALU = mybir.AluOpType
ACT = mybir.ActivationFunctionType
AX = mybir.AxisListType
F32 = mybir.dt.float32
BF16 = mybir.dt.bfloat16
I32 = mybir.dt.int32
ds = bass.ds

P = 128
EPS = 1e-5


def ceil_div(a, b):
    return -(-a // b)


def spread(v, axis, n):
    shape = list(v.shape)
    shape[axis] = n
    return v.broadcast_to(shape)


class Chain:

    def __init__(self, eng, sem):
        self.eng, self.sem, self.base, self.k, self.i, self.per = eng, sem, 0, 0, None, 0

    def mark(self, ins):
        self.k += 1
        ins.then_inc(self.sem, 1)

    def wait(self):
        at = self.base + self.k
        self.eng.wait_ge(self.sem, at if self.i is None else self.i * self.per + at)

    def link(self, ins):
        self.mark(ins)
        self.wait()

    def enter(self, i, per):
        self.base, self.k, self.i, self.per = self.base + self.k, 0, i, per

    def leave(self, n):
        assert self.k == self.per, (self.k, self.per)
        self.base, self.k, self.i = self.base + n * self.per, 0, None


def gps_layer(nc, A, out):
    x_d, src_d, dst_d, ew_d = A["x"], A["src"], A["dst"], A["edge_weight"]
    N, D = x_d.shape
    E = src_d.shape[0]
    NB = ceil_div(N, P)
    NT = NB + NB % 2
    LAST = N - (NB - 1) * P
    DK = D // P
    EP = 125
    EC = E // EP
    SJ = 40
    NS = EC // SJ
    HJ = SJ // 2
    B = 16
    BL = B.bit_length() - 1
    RW = 2
    HI = ceil_div(ceil_div(EP * SJ + NB * (B - 1), B), P)
    SUB = HI * B
    WP = 3
    CH = 2
    BPG = CH * P // B
    SLOTS = 5
    UG = 2 * SLOTS
    runs_max = (E + NS * NB * (B - 1)) // B
    groups_max = (runs_max + NB * (BPG - 1)) // BPG
    NG = ceil_div(groups_max, UG) * UG
    NIT = NG // UG
    CT = ceil_div(NG * CH, P)
    SPARE = CT * P * P // B
    RUNS = SPARE + HI * P
    HG = ceil_div(NG, P)
    assert E == EP * EC and EC == SJ * NS and NIT >= NB and NB < P and NT == NB + 1 and NB % 7 == 0 and CT * P >= (NG + SLOTS - 1) * CH and NS % 2 == 0
    GD = A["woT"].shape[0]
    KV = 2 * GD
    HW = 64
    HEADS = GD // HW
    PAIRS = GD // P
    F = A["L0_ffn_w1"].shape[1]
    FB = F // P
    TOP = max(1, N // 2) - 1

    y_d = nc.dram_tensor("y_table", [NB * P, D], F32, kind="Internal").ap()
    rec_d = nc.dram_tensor("records", [RUNS, B * RW], F32, kind="Internal").ap()
    hmap_d = nc.dram_tensor("block_of_group", [HG * P], I32, kind="Internal").ap()

    with ExitStack() as ctx:
        def sb(name, shape, dt=F32):
            return ctx.enter_context(nc.sbuf_tensor(name, shape, dt))

        def sem(name):
            return ctx.enter_context(nc.semaphore(name))

        bank = [ctx.enter_context(nc.psum_tensor(f"bank{i}", [P, 512], F32)) for i in range(8)]

        X = sb("X", [P, NT, D])
        ACC = sb("ACC", [P, NT, D])
        AR = sb("AR", [P, 18304])
        accf = ACC[:, :, :].rearrange("p t d -> p (t d)")

        def cut(base, start, shape, rows=P):
            n = 1
            for s in shape:
                n *= s
            v = base[0:rows, start:start + n]
            if len(shape) == 2:
                v = v.rearrange("p (a b) -> p a b", a=shape[0])
            if len(shape) == 3:
                v = v.rearrange("p (a b c) -> p a b c", a=shape[0], b=shape[1])
            return v, start + n

        def cutb(base, start, shape, rows=P):
            n = 1
            for q in shape:
                n *= q
            v = base[0:rows, start:start + n // 2].bitcast(BF16)
            names = "abcd"[:len(shape)]
            if len(shape) > 1:
                v = v.rearrange(f"p ({' '.join(names)}) -> p {' '.join(names)}", **dict(zip(names[:-1], shape)))
            return v, start + n // 2

        o = 0
        hfb, o = cutb(AR, o, [EC], EP)
        keyp = []
        for _ in range(WP):
            v, o = cutb(AR, o, [EC], EP)
            keyp.append(v)
        rlob = keyp[WP - 1]
        wp = []
        for _ in range(WP):
            v, o = cutb(AR, o, [EC], EP)
            wp.append(v)
        iotaL, o = cutb(AR, o, [P, SJ], EP)
        zero, _ = cut(AR, o, [RUNS // P * B * RW])
        lbx, o = cut(AR, o, [NS, NB + 1])
        o_dead = o
        dlt, o = cut(AR, o, [NS, NB + 1])
        cnt, o = cut(AR, o, [NS, NB])
        ys, o = cut(AR, o, [2, D])
        Z, o = cut(AR, o, [NB, SJ], EP)
        o_sort = o
        assert RUNS // P * B * RW <= 2 * NS * (NB + 1)
        o = 0
        srcI = accf[0:EP, 0:EC].bitcast(I32)
        dstI = accf[0:EP, EC:2 * EC].bitcast(I32)
        tmpI = accf[0:EP, 2 * EC:3 * EC].bitcast(I32)
        ew = accf[0:EP, 3 * EC:4 * EC]
        o = 0
        oh1, ohw, rl1h = [], [], []
        for _ in range(2):
            v, o = cutb(accf, o, [NB, SJ], EP)
            oh1.append(v)
        for _ in range(2):
            v, o = cutb(accf, o, [WP, NB, SJ], EP)
            ohw.append(v)
        for _ in range(2):
            v, o = cutb(accf, o, [P, HJ], EP)
            rl1h.append(v)
        assert o <= NT * D
        o = 0
        pcf, o = cut(accf, o, [NS * NB])
        pcT, o = cut(accf, o, [NB, NS])
        inc, o = cut(accf, o, [NS * NB])
        keep, o = cut(accf, o, [NS * NB])
        big, o = cut(accf, o, [NS, NB + 1])
        hm49, o = cut(accf, o, [HG, NB])
        assert o <= NT * D
        o = 0
        O2, lo1h, sub1h = [], [], []
        for _ in range(2):
            v, o = cutb(accf, o, [NB, SJ], EP)
            O2.append(v)
        F3, o = cut(accf, o, [NB, SJ], EP)
        for _ in range(2):
            v, o = cutb(accf, o, [P, HJ], EP)
            lo1h.append(v)
        for _ in range(2):
            v, o = cutb(accf, o, [SUB, HJ], EP)
            sub1h.append(v)
        mv1, o = cutb(accf, o, [WP, RW, SUB * HJ], EP)
        assert o <= NT * D
        mv0, o = cutb(AR, o_dead, [WP, RW, SUB * HJ], EP)
        assert o <= o_dead + NS * (2 * NB + 1)
        mv = [v.rearrange("p m w (s j) -> p m w s j", j=HJ) for v in (mv0, mv1)]
        o = 0
        rec, o = cut(AR, o, [CT, P, RW])
        cidx, o = cut(AR, o, [CT * P])
        rlo, o = cut(AR, o, [CT * P])
        recw, o = cut(AR, o, [CT * P])
        cidxI, rloI = cidx.bitcast(I32), rlo.bitcast(I32)
        G, o = cut(AR, o, [SLOTS, CH, D])
        OH, o = cut(AR, o, [SLOTS, CH, P])
        kvsq, o = cut(AR, o, [KV])
        kn, o = cut(AR, o, [GD])
        vs, o = cut(AR, o, [GD])
        xs, o = cut(AR, o, [D])
        xT, o = cut(AR, o, [D])
        o_gather = o
        o = 0
        w1s, o = cut(AR, o, [DK, F])
        w2s, o = cut(AR, o, [FB, D])
        wq, o = cut(AR, o, [PAIRS, D])
        wo, o = cut(AR, o, [PAIRS, D])
        ot, o = cut(AR, o, [7, D])
        yt, o = cut(AR, o, [2, D])
        H1a, o = cut(AR, o, [FB, 4 * P])
        H1b, o2 = cut(AR, o, [FB, 3 * P])
        assert o2 <= 18304, o2
        ag, o = cut(AR, o, [2, D])
        agT, o = cut(AR, o, [2, D])
        hT, o = cut(AR, o, [2, D])
        xTs, o = cut(AR, o, [2, D])
        xin, o = cut(AR, o, [2, D])
        xn2, o = cut(AR, o, [2, D])
        assert o <= o2

        assert max(o_sort, o_gather) + HG * P <= 18304
        hrow = AR[0:1, 18304 - HG * P:18304].bitcast(I32)

        wkv = sb("wkv", [P, DK, KV])
        WT = sb("WT", [P, DK, D])
        W1 = sb("W1", [P, DK, D])
        W2 = sb("W2", [P, DK, D])
        WW = sb("WW", [P, DK, D])
        kvf = wkv[:, :, :].rearrange("p k n -> p (k n)")
        dots, o = cut(kvf, 0, [PAIRS, P])
        Vh, o = cut(kvf, o, [PAIRS, D])
        Mx, o = cut(kvf, o, [DK, D])
        assert o <= DK * KV
        bc = sb("bc", [P, DK])
        b1c = sb("b1c", [P, DK])
        fb1 = sb("fb1", [P, FB])
        b2o = sb("b2o", [P, D])
        brow = sb("brow", [P, D])
        fb2 = sb("fb2", [P, D])
        wr = sb("wr", [P, D])
        brc = sb("brc", [P, 1])
        iotaI = sb("iotaI", [P, P], I32)
        iota = sb("iota", [P, P])
        pidI = sb("pidI", [P, HI], I32)
        pid = sb("pid", [P, HI])
        ident = sb("ident", [P, P])
        strict = sb("strict", [P, P])
        ones = sb("ones", [P, P])
        onesb = sb("onesb", [P, P], BF16)
        befb = sb("befb", [P, 2, P], BF16)
        iotab = sb("iotab", [P, P], BF16)
        zcol = sb("zcol", [P, P])
        st = sb("st", [P, NB, 6])
        mvar = sb("mvar", [P, NT, 2])
        rstd = sb("rstd", [P, NT])
        t49 = sb("t49", [P, NB])
        v49 = sb("v49", [P, NB])
        u49 = sb("u49", [P, NB])
        dinv = sb("dinv", [P, NT])
        wcol = sb("wcol", [P, 1])
        wmean = sb("wmean", [P, DK * 2 * HEADS])
        ginc = sb("ginc", [P, NB])
        tpf = sb("tpf", [P, NB])
        ridx = sb("ridx", [P, NS, HI], I32)
        ridxf = sb("ridxf", [P, NS])
        hm = sb("hm", [P, HG])
        hmI = sb("hmI", [P, HG], I32)
        A2 = sb("A2", [EP, 2, NB + 1])
        posf = sb("posf", [EP, SJ])
        posI = sb("posI", [EP, SJ], I32)
        poaI = sb("poaI", [EP, SJ], I32)
        pobI = sb("pobI", [EP, SJ], I32)
        lof = sb("lof", [EP, SJ])
        subf = sb("subf", [EP, SJ])
        sidx = sb("sidx", [P, 2, HI], I32)
        sbuf = sb("sbuf", [P, 2, SUB * RW])
        nmr = sb("nmr", [P, NB])
        gidx = sb("gidx", [P, SLOTS, CH], I32)
        ss = sb("ss", [P, 2 * HEADS])
        pr = sb("pr", [P, HEADS])
        rr = sb("rr", [P, HEADS])
        r2 = sb("r2", [P, HEADS])
        wt = sb("wt", [P, NT])
        keyI = sb("keyI", [P, NB], I32)
        kbI = sb("kbI", [P, NB], I32)
        khi = sb("khi", [P, NB])
        klo = sb("klo", [P, NB])
        comb = sb("comb", [P, NB])
        gtm = sb("gtm", [P, NB])
        eqm = sb("eqm", [P, NB])
        tk = [sb(f"tk{i}", [P, 1]) for i in range(6)]
        wsel = sb("wsel", [P, NB])
        sel = sb("sel", [P, NB])


        s_x, s_xpad, s_edges, s_w, s_wf = sem("x_loaded"), sem("x_padded"), sem("edges_loaded"), sem("weights_loaded"), sem("tail_weights_loaded")
        s_iota, s_zero, s_const, s_rk = sem("iota_done"), sem("zeros_ready"), sem("constants_ready"), sem("record_keys_copied")
        s_dve = sem("dve_chain")
        s_var, s_sqrt = sem("variances_ready"), sem("roots_taken")
        s_e = sem("edge_fields_ready")
        s_o1, s_ow, s_rl = sem("block_onehots"), sem("weighted_onehots"), sem("row_onehots")
        s_cntp, s_cntc, s_h1 = sem("cells_counted"), sem("cell_counts_copied"), sem("row_onehots_used")
        s_deg = sem("degrees_summed")
        s_ridx, s_hm, s_hmd, s_hrow = sem("run_places_ready"), sem("group_blocks_ready"), sem("group_blocks_stored"), sem("group_blocks_loaded")
        s_o2, s_cross = sem("edge_block_onehots"), sem("partition_prefixes")
        s_sub, s_key, s_wm, s_lo = sem("run_onehots"), sem("keys_placed"), sem("edge_weights_placed"), sem("lane_onehots")
        s_half, s_runs, s_runc = sem("halves_multiplied"), sem("runs_summed"), sem("runs_copied")
        s_sidx, s_scat, s_scd = sem("run_indices"), sem("records_written"), sem("scatters_over")
        s_acc, s_rec, s_ln = sem("acc_started"), sem("records_loaded"), sem("ln_scales_ready")
        s_xn, s_dinv, s_yt = sem("xn_ready"), sem("dinv_ready"), sem("table_tile_ready")
        s_y = [sem("table_stored_0"), sem("table_stored_1")]
        s_rt, s_rw = sem("records_transposed"), sem("record_weights_copied")
        s_prep, s_grp, s_added = sem("groups_prepared"), sem("groups_multiplied"), sem("all_groups_added")
        s_g = [sem(f"rows_gathered_{i}") for i in range(SLOTS)]
        s_seen = {e: sem(f"waits_passed_{e}") for e in ("pool", "pe", "act", "dve", "sp")}
        s_xs, s_xTp, s_xT, s_kvp, s_vc = sem("xn_staged"), sem("xn_transposed"), sem("xnT_copied"), sem("kv_multiplied"), sem("v_copied")
        s_sq, s_pr, s_sr, s_kn, s_dot = sem("kv_squared"), sem("norm_products"), sem("norm_roots"), sem("k_scaled"), sem("dots_summed")
        s_wc, s_dd, s_m1, s_vh, s_m2, s_mx = (sem(n) for n in ("kv_weights_centred", "dots_copied", "mixer_half", "mixer_half_copied", "mixer_whole", "mixer_copied"))
        s_b1 = sem("hidden_bias_ready")
        a_ag, a_tp, a_T, a_hp, a_h, a_o, a_x1 = (sem("a_" + n) for n in ("scaled", "transposed", "copied", "hidden", "relu", "summed", "x1"))
        a_xin = [sem("a_x_loaded_0"), sem("a_x_loaded_1")]
        b_var, b_root, b_xn, b_tp, b_tc = (sem("b_" + n) for n in ("variances", "roots", "normalised", "transposed", "copied"))
        k_cnt, k_sum = sem("k_counted"), sem("k_summed")
        c_h, c_g, c_y, c_free, c_ot = (sem("c_" + n) for n in ("hidden", "gelu", "out", "bank_read", "tile_ready"))
        c_st = [sem(f"c_stored_{i}") for i in range(7)]

        def passed(eng, name):
            eng.sem_inc(s_seen[name], 1)

        def row(v):
            return v.rearrange("p o d -> p (o d)")

        block = ctx.enter_context(nc.Block())
        xpart = NB - 1

        @block.sync
        def _(sp):
            sp.dma_start(srcI, src_d.rearrange("(p j) -> p j", p=EP)).then_inc(s_edges, 16)
            sp.dma_start(dstI, dst_d.rearrange("(p j) -> p j", p=EP)).then_inc(s_edges, 16)
            sp.dma_start(ew, ew_d.rearrange("(p j) -> p j", p=EP)).then_inc(s_edges, 16)
            sp.dma_start(X[:, 0:xpart, :], x_d[0:xpart * P, :].rearrange("(t p) d -> p t d", p=P)).then_inc(s_x, 16)
            sp.wait_ge(s_xpad, 1)
            sp.dma_start(X[0:LAST, xpart, :], x_d[xpart * P:N, :]).then_inc(s_x, 16)
            for t, a in ((wkv, "kvT"), (WT, "WT"), (W1, "L0_gnn_W1"), (W2, "L0_gnn_W2")):
                sp.dma_start(t[:, :, :], A[a].rearrange("(k p) n -> p k n", p=P)).then_inc(s_w, 16)
            with nc.allow_non_contiguous_dma(reason="a few hundred words of biases"):
                sp.dma_start(bc[:, :], A["L0_gnn_b"].rearrange("(k p) -> p k", p=P)).then_inc(s_w, 16)
                sp.dma_start(b1c[:, :], A["L0_gnn_b1"].rearrange("(k p) -> p k", p=P)).then_inc(s_w, 16)
                sp.dma_start(fb1[:, :], A["L0_ffn_b1"].rearrange("(k p) -> p k", p=P)).then_inc(s_w, 16)
            for t, a in ((b2o, A["L0_gnn_b2"]), (brow, A["L0_mix_b_out"]), (fb2, A["L0_ffn_b2"]),
                         (wr, A["L0_ffn_wr"].rearrange("d o -> (d o)")), (brc, A["L0_ffn_br"])):
                sp.dma_start(t[:, :], spread(a.rearrange("(o d) -> o d", o=1), 0, P)).then_inc(s_w, 16)
            sp.wait_ge(s_hm, 1)
            with nc.allow_non_contiguous_dma(reason="1024 words"):
                sp.dma_start(hmap_d.rearrange("(p a) -> p a", p=P), hmI[:, :]).then_inc(s_hmd, 16)
            sp.wait_ge(s_hmd, 16)
            sp.dma_start(hrow[:, :], hmap_d.rearrange("(o a) -> o a", o=1)).then_inc(s_hrow, 16)
            def table(t, u):
                sp.wait_ge(s_yt, t + 1)
                passed(sp, "sp")
                sp.dma_start(y_d[ds(t * P, P), :], ys[:, u, :]).then_inc(s_y[u], 16)

            with sp.Fori(0, NB // 2) as i:
                for u in range(2):
                    table(2 * i + u, u)
            sp.wait_ge(s_yt, NB)
            sp.dma_start(y_d[(NB - 1) * P:NB * P, :], ys[:, 0, :]).then_inc(s_y[0], 16)
            sp.wait_ge(s_scd, 1)
            recv = rec_d[0:SPARE, :].rearrange("(p t) w -> p (t w)", p=P)
            sp.dma_start(rec.rearrange("p t r w -> p (t r w)"), recv).then_inc(s_rec, 16)
            sp.wait_ge(s_added, 1)
            for t, a in ((wq, "wq"), (wo, "woT"), (w1s, "L0_ffn_w1"), (w2s, "L0_ffn_w2")):
                sp.dma_start(t, A[a].rearrange("(k p) n -> p k n", p=P)).then_inc(s_wf, 16)
            with sp.Fori(0, (NT - 2) // 2) as i:
                for u in range(2):
                    sp.wait_ge(a_x1, 2 * i + u + 1)
                    passed(sp, "sp")
                    sp.dma_start(xin[:, u, :], x_d[ds((2 * i + u) * P, P), :]).then_inc(a_xin[u], 16)
            sp.wait_ge(a_x1, NT - 1)
            sp.dma_start(xin[0:LAST, 0, :], x_d[xpart * P:N, :]).then_inc(a_xin[0], 16)
            sp.wait_ge(a_x1, NT)
            sp.dma_start(xin[0:LAST, 1, :], x_d[xpart * P:N, :]).then_inc(a_xin[1], 16)
            n7 = NB // 7
            with sp.Fori(0, n7 - 1) as i:
                for q in range(7):
                    sp.wait_ge(c_ot, 7 * i + q + 1)
                    passed(sp, "sp")
                    sp.dma_start(out[ds((7 * i + q) * P, P), :], ot[:, q, :]).then_inc(c_st[q], 16)
            for q in range(7):
                t = 7 * (n7 - 1) + q
                n = P if t < xpart else LAST
                sp.wait_ge(c_ot, t + 1)
                sp.dma_start(out[t * P:t * P + n, :], ot[0:n, q, :]).then_inc(c_st[q], 16)
            for q in range(7):
                sp.wait_ge(c_st[q], 16 * n7)

        @block.gpsimd
        def _(pool):
            pool.iota(iotaI[:, :], [[1, P]], base=0, channel_multiplier=0).then_inc(s_iota, 1)
            pool.iota(pidI[:, :], [[P, HI]], base=0, channel_multiplier=1).then_inc(s_iota, 1)
            pool.wait_ge(s_zero, 1)
            pool.dma_start(rec_d.rearrange("(p b) w -> p (b w)", p=P), zero).then_inc(s_scat, 16)
            pool.wait_ge(s_e, 1)
            with pool.Fori(0, NS // 2) as i:
                for u in range(2):
                    pool.wait_ge(s_o1, 2 * i + u + 1)
                    pool.wait_ge(s_cntp, 2 * i + u + 1)
                    passed(pool, "pool")
                    w = spread(wp[2][:, ds((2 * i + u) * SJ, SJ)].rearrange("p (o j) -> p o j", o=1), 1, NB)
                    pool.tensor_tensor(ohw[u][:, 2, :, :], oh1[u], w, ALU.mult).then_inc(s_ow, 1)
            pool.wait_ge(s_ridx, 1)

            def place(s, u, m):
                w = spread(wp[m][:, ds(s * SJ + u * HJ, HJ)].rearrange("p (o j) -> p o j", o=1), 1, SUB)
                return pool.tensor_tensor(mv[u][:, m, 1, :, :], sub1h[u], w, ALU.mult)

            def scatter(s, b, k):
                if k == 0:
                    pool.wait_ge(s_runc, s + 3)
                    pool.wait_ge(s_sidx, s + 1)
                pool.wait_ge(s_scat, 16 * (HI * s + k) + 16)
                passed(pool, "pool")
                pool.indirect_dma_start(rec_d, bass.IndirectOffsetOnAxis(sidx[:, b, k:k + 1], 0),
                                        sbuf[:, b, k * B * RW:(k + 1) * B * RW], None).then_inc(s_scat, 16)

            def sort_step(s, b, scattering):
                for u in range(2):
                    pool.wait_ge(s_sub, 2 * s + u + 1)
                    pool.wait_ge(s_half, 2 * s + u + 1)
                    passed(pool, "pool")
                    place(s, u, 1)
                    if scattering:
                        scatter(s - 1, 1 - b, u)
                    place(s, u, 2).then_inc(s_wm, 1)
                if scattering:
                    for k in range(2, HI):
                        scatter(s - 1, 1 - b, k)

            sort_step(0, 0, False)
            with pool.Fori(0, NS // 2 - 1) as i:
                sort_step(2 * i + 1, 1, True)
                sort_step(2 * i + 2, 0, True)
            sort_step(NS - 1, 1, True)
            for k in range(HI):
                scatter(NS - 1, 1, k)
            pool.wait_ge(s_scat, 16 * (HI * NS + 1))
            pool.sem_inc(s_scd, 1)
            pool.wait_ge(s_y[0], 16 * (NB // 2 + 1))
            pool.wait_ge(s_y[1], 16 * (NB // 2))
            with pool.Fori(0, NIT) as i:
                for u in range(UG):
                    pool.wait_ge(s_prep, UG * i + u + 1)
                    passed(pool, "pool")
                    for k in range(CH):
                        pool.indirect_dma_start(G[:, u % SLOTS, k, :], None, y_d,
                                                bass.IndirectOffsetOnAxis(gidx[:, u % SLOTS, k:k + 1], 0)
                                                ).then_inc(s_g[u % SLOTS], 16)

        @block.scalar
        def _(act):
            act.sem_inc(s_cntc, 2)
            act.sem_inc(s_runc, 2)
            act.sem_inc(b_tc, 2)
            act.sem_inc(c_g, 4)
            act.wait_ge(s_var, 1)
            act.activation(rstd[:, 0:NB], u49[:, :], ACT.Sqrt).then_inc(s_sqrt, 1)
            act.wait_ge(s_ln, 1)
            with act.Fori(0, NB) as t:
                xv = row(X[:, ds(t, 1), :])
                act.activation(xv, xv, ACT.Identity, bias=nmr[:, ds(t, 1)], scale=rstd[:, ds(t, 1)]).then_inc(s_xn, 1)
            with act.Fori(0, NS // 2) as i:
                for u in range(2):
                    act.wait_ge(s_cntp, 2 * i + u + 3)
                    passed(act, "act")
                    act.copy(cnt[:, ds(2 * i + u, 1), :], bank[1 + u][:, 0:NB].rearrange("p (o h) -> p o h", o=1)).then_inc(s_cntc, 1)
            act.wait_ge(s_var, 2)
            act.activation(dinv[:, 0:NB], t49[:, :], ACT.Sqrt).then_inc(s_sqrt, 1)
            act.wait_ge(s_dinv, 1)

            def tile(t, u):
                act.mul(ys[:, u, :], row(X[:, ds(t, 1), :]), dinv[:, ds(t, 1)]).then_inc(s_yt, 1)

            for u in range(2):
                tile(u, u)
            with act.Fori(1, NB // 2) as i:
                for u in range(2):
                    act.wait_ge(s_y[u], 16 * i)
                    passed(act, "act")
                    tile(2 * i + u, u)
            act.wait_ge(s_y[0], 16 * (NB // 2))
            tile(NB - 1, 0)

            def copy_runs(s, b, waiting):
                act.wait_ge(s_runs, s + 1)
                if waiting:
                    act.wait_ge(s_scat, 16 * (HI * (s - 1)) + 16)
                passed(act, "act")
                act.copy(sbuf[:, b, :].rearrange("p (s w) -> p w s", w=RW),
                         bank[3 + b][:, 0:SUB * RW].rearrange("p (w s) -> p w s", w=RW)).then_inc(s_runc, 1)

            copy_runs(0, 0, False)
            with act.Fori(0, NS // 2 - 1) as i:
                copy_runs(2 * i + 1, 1, True)
                copy_runs(2 * i + 2, 0, True)
            copy_runs(NS - 1, 1, True)
            act.wait_ge(s_half, 2 * NS + 2)
            act.wait_ge(s_scd, 1)
            with act.Fori(NT // 2, NT) as t:
                act.mul(row(ACC[:, ds(t, 1), :]), row(X[:, ds(t, 1), :]), dinv[:, ds(t, 1)]).then_inc(s_acc, 1)
            act.wait_ge(s_rt, 2)
            for b in range(ceil_div(CT, 4)):
                n = min(4, CT - 4 * b)
                act.copy(recw.rearrange("p (c t) -> p t c", t=CT)[:, 4 * b:4 * b + n, :],
                         bank[4 + b][:, 0:n * P].rearrange("p (t c) -> p t c", t=n)).then_inc(s_rw, 1)
            act.wait_ge(s_acc, NT // 2 + 1)
            act.wait_ge(s_scd, 1)
            with act.Fori(0, NB) as t:
                act.wait_ge(s_xTp, t + 1)
                passed(act, "act")
                act.copy(xs.rearrange("p (o d) -> p o d", o=1), X[:, ds(t, 1), :]).then_inc(s_xs, 1)
                act.wait_ge(s_xTp, t + 2)
                act.wait_ge(s_kvp, t + 1)
                passed(act, "act")
                act.copy(xT, bank[0][:, 0:D])
                act.copy(X[:, ds(t, 1), :], bank[0][:, 0:D].rearrange("p (o d) -> p o d", o=1)).then_inc(s_xT, 1)
                act.wait_ge(s_kvp, t + 2)
                act.wait_ge(s_pr, t + 1)
                act.wait_ge(s_dot, t + 1)
                passed(act, "act")
                act.activation(kvsq[:, 0:GD], bank[1][:, :], ACT.Square)
                act.activation(kvsq[:, GD:KV], bank[0][:, :], ACT.Square).then_inc(s_sq, 1)
                act.copy(vs, bank[0][:, :]).then_inc(s_vc, 1)
                act.wait_ge(s_pr, t + 2)
                passed(act, "act")
                act.activation(rr[:, :], pr[:, :], ACT.Sqrt).then_inc(s_sr, 1)
            act.wait_ge(s_m1, 1)
            for j in range(PAIRS):
                act.copy(Vh[:, j, :], bank[4 + j][:, 0:D])
            act.copy(WW[:, 0, :], bank[0][:, 0:D])
            act.copy(WW[:, 1, :], bank[3][:, 0:D]).then_inc(s_vh, 1)
            act.wait_ge(s_m2, 1)
            for m in range(DK):
                act.mul(Mx[:, m, :], bank[1 + m][:, 0:D], 1.0 / N).then_inc(s_mx, 1)
            act.wait_ge(s_b1, 1)
            with act.Fori(0, NT // 2) as i:
                for u in range(2):
                    act.wait_ge(a_tp, 2 * i + u + 1)
                    act.wait_ge(a_o, 2 * i + u + 1)
                    passed(act, "act")
                    act.copy(agT[:, u, :], bank[u][:, 0:D])
                    act.copy(xTs[:, u:u + 1, :], X[:, ds(2 * i + u, 1), :]).then_inc(a_T, 1)
                for u in range(2):
                    act.wait_ge(a_hp, 2 * i + u + 1)
                    passed(act, "act")
                    for m in range(DK):
                        ins = act.activation(hT[:, u, m * P:(m + 1) * P], bank[2 + u][:, m * P:(m + 1) * P], ACT.Relu,
                                             bias=b1c[:, m:m + 1])
                    ins.then_inc(a_h, 1)
            act.wait_ge(b_var, 1)
            act.activation(rstd[:, 0:NB], u49[:, :], ACT.Sqrt).then_inc(b_root, 1)
            with act.Fori(0, NT // 2) as i:
                for u in range(2):
                    act.wait_ge(b_tp, 2 * i + u + 3)
                    passed(act, "act")
                    act.copy(ACC[:, ds(2 * i + u, 1), :], bank[u][:, 0:D].rearrange("p (o d) -> p o d", o=1)).then_inc(b_tc, 1)
            with act.Fori(0, NB // 7) as i:
                for q, (nt, H1) in enumerate(((4, H1a), (3, H1b))):
                    act.wait_ge(c_y, 7 * i + 4 + 3 * q)
                    for f in range(FB):
                        act.wait_ge(c_h, (2 * i + q) * FB + f + 1)
                        passed(act, "act")
                        act.activation(H1[:, f, :], bank[f % 4][:, 0:nt * P], ACT.Gelu_apprx_tanh,
                                       bias=fb1[:, f:f + 1]).then_inc(c_g, 1)

        @block.tensor
        def _(pe):
            pe.sem_inc(s_cntp, 2)
            pe.sem_inc(s_h1, 2)
            pe.sem_inc(s_half, 2)
            kvz = spread(ones[:, 0:1], 1, WP * NB)
            pe.sem_inc(s_grp, 1)
            pe.sem_inc(s_xTp, 1)
            pe.sem_inc(s_kvp, 1)
            pe.sem_inc(s_dot, 1)
            pe.sem_inc(a_o, 2)
            pe.sem_inc(b_tp, 2)
            pe.sem_inc(c_y, 7)
            pe.wait_ge(s_const, 1)
            pe.matmul(bank[0][:, 0:WP * NB], zcol[:, :], kvz, start=True, stop=False, skip_group_check=True)
            with pe.Fori(0, NS // 2) as i:
                for u in range(2):
                    s = 2 * i + u
                    pe.wait_ge(s_o1, s + 1)
                    pe.wait_ge(s_cntc, s + 1)
                    for j in range(SJ):
                        pe.matmul(bank[1 + u][:, 0:NB], onesb[0:EP, :], oh1[u][:, :, j], start=(j == 0), stop=(j == SJ - 1))
                    pe.wait_ge(s_ow, 2 * s + 2)
                    for q in range(2):
                        pe.wait_ge(s_rl, 2 * s + q + 1)
                        for j in range(HJ):
                            ins = pe.matmul(bank[0][:, 0:WP * NB].rearrange("p (m h) -> p m h", m=WP), rl1h[q][:, :, j],
                                            ohw[u][:, :, :, q * HJ + j], start=False, stop=False, skip_group_check=True)
                        ins.then_inc(s_h1, 1)
                    pe.sem_inc(s_seen["pe"], 1)
                    pe.wait_ge(s_h1, 2 * s + 4)
                    pe.sem_inc(s_cntp, 1)
            pe.matmul(bank[0][:, 0:WP * NB], zcol[:, :], kvz, start=False, stop=True, skip_group_check=True).then_inc(s_deg, 1)

            def cross(s, b):
                pe.wait_ge(s_o2, s + 1)
                for q in range(2):
                    for j in range(SJ):
                        ins = pe.matmul(bank[2][0:EP, q * NB:(q + 1) * NB], befb[0:EP, q, 0:EP], O2[b][:, :, j],
                                        start=(j == 0), stop=(j == SJ - 1))
                ins.then_inc(s_cross, 1)

            def sort_runs(s, b, more):
                if more:
                    cross(s + 1, 1 - b)
                pe.wait_ge(s_runc, s + 1)
                for u in range(2):
                    pe.wait_ge(s_key, 2 * s + u + 1)
                    pe.wait_ge(s_wm, 2 * s + u + 1)
                    for j in range(HJ):
                        for m in range(WP):
                            ins = pe.matmul(bank[3 + b][:, 0:SUB * RW].rearrange("p (w s) -> p w s", w=RW), lo1h[u][:, :, j],
                                            mv[u][:, m, :, :, j],
                                            start=(u == 0 and j == 0 and m == 0), stop=(u == 1 and j == HJ - 1 and m == WP - 1))
                    ins.then_inc(s_half, 1)
                pe.wait_ge(s_half, 2 * s + 4)
                pe.sem_inc(s_runs, 1)

            cross(0, 0)
            with pe.Fori(0, NS // 2 - 1) as i:
                sort_runs(2 * i, 0, True)
                sort_runs(2 * i + 1, 1, True)
            sort_runs(NS - 2, 0, True)
            sort_runs(NS - 1, 1, False)
            pe.wait_ge(s_rec, 16)
            pe.wait_ge(s_runc, NS + 2)
            for w in range(RW):
                for t in range(CT):
                    ins = pe.transpose(bank[4 * w + t // 4][:, t % 4 * P:(t % 4 + 1) * P], rec[:, t, :, w], ident[:, :])
                ins.then_inc(s_rt, 1)
            pe.wait_ge(s_rk, ceil_div(CT, 4))
            pe.wait_ge(s_rw, ceil_div(CT, 4))
            pe.wait_ge(s_w, 16 * 12)
            pe.wait_ge(s_wc, 1)

            def group(g, u, use):
                pe.wait_ge(s_g[u % SLOTS], 16 * CH * use)
                pe.wait_ge(s_prep, g + 1)
                for k in range(CH):
                    ins = pe.matmul(bank[3 + u % SLOTS][:, 0:D], OH[:, u % SLOTS, k, :], G[:, u % SLOTS, k, :],
                                    start=(k == 0), stop=(k == CH - 1))
                ins.then_inc(s_grp, 1)

            def kv_transpose(t):
                pe.wait_ge(s_xs, t + 1)
                for m in range(DK):
                    ins = pe.transpose(bank[0][:, m * P:(m + 1) * P], xs[:, m * P:(m + 1) * P], ident[:, :])
                ins.then_inc(s_xTp, 1)

            def kv_multiply(t):
                pe.wait_ge(s_xT, t + 1)
                pe.wait_ge(s_kn, t + 1)
                for b, o in ((1, 0), (0, GD)):
                    for k in range(DK):
                        ins = pe.matmul(bank[b][:, :], xT[:, k * P:(k + 1) * P], wkv[:, k, o:o + GD], start=(k == 0), stop=(k == DK - 1))
                ins.then_inc(s_kvp, 1)

            def kv_dots(t):
                pe.wait_ge(s_kn, t + 2)
                pe.wait_ge(s_vc, t + 1)
                for j in range(PAIRS):
                    ins = pe.matmul(bank[2][:, j * P:(j + 1) * P], kn[:, j * P:(j + 1) * P], vs[:, j * P:(j + 1) * P],
                                    start=False, stop=False, skip_group_check=True)
                ins.then_inc(s_dot, 1)

            pe.matmul(bank[2][:, 0:GD], zcol[:, :], wkv[:, 0, 0:GD], start=True, stop=False, skip_group_check=True)
            with pe.Fori(0, NB) as i:
                kv_transpose(i)
                for u in range(UG):
                    group(UG * i + u, u, 2 * i + u // SLOTS + 1)
                    if u == 1:
                        kv_multiply(i)
                    if u == 8:
                        kv_dots(i)
            with pe.Fori(NB, NIT) as i:
                for u in range(UG):
                    group(UG * i + u, u, 2 * i + u // SLOTS + 1)
            pe.matmul(bank[2][:, 0:GD], zcol[:, :], wkv[:, 0, 0:GD], start=False, stop=True, skip_group_check=True).then_inc(s_dot, 1)
            pe.wait_ge(s_added, 1)
            for kb, b in ((0, 0), (1, 3)):
                for k in range(DK):
                    pe.matmul(bank[b][:, 0:D], WT[:, k, kb * P:(kb + 1) * P], W1[:, k, :], start=(k == 0), stop=(k == DK - 1))
            for m in range(DK):
                for k in range(DK):
                    pe.matmul(bank[3][:, D + m:D + m + 1], W1[:, k, m * P:(m + 1) * P], bc[:, k:k + 1], start=(k == 0), stop=(k == DK - 1))
            pe.wait_ge(s_dd, 1)
            pe.wait_ge(s_wf, 16 * 4)
            for j in range(PAIRS):
                ins = pe.matmul(bank[4 + j][:, 0:D], dots[:, j, :], wq[:, j, :], start=True, stop=True)
            ins.then_inc(s_m1, 1)
            pe.wait_ge(s_vh, 1)
            for m in range(DK):
                for j in range(PAIRS):
                    ins = pe.matmul(bank[1 + m][:, 0:D], Vh[:, j, m * P:(m + 1) * P], wo[:, j, :], start=(j == 0), stop=(j == PAIRS - 1))
            ins.then_inc(s_m2, 1)
            pe.wait_ge(s_mx, DK)
            with pe.Fori(0, NT // 2) as i:
                for u in range(2):
                    pe.wait_ge(a_ag, 2 * i + u + 1)
                    for m in range(DK):
                        ins = pe.transpose(bank[u][:, m * P:(m + 1) * P], ag[:, u, m * P:(m + 1) * P], ident[:, :])
                    ins.then_inc(a_tp, 1)
                for u in range(2):
                    pe.wait_ge(a_T, 2 * i + u + 1)
                    for m in range(DK):
                        for k in range(DK):
                            ins = pe.matmul(bank[2 + u][:, m * P:(m + 1) * P], WW[:, k, m * P:(m + 1) * P],
                                            agT[:, u, k * P:(k + 1) * P], start=(k == 0), stop=(k == DK - 1))
                    ins.then_inc(a_hp, 1)
                for u in range(2):
                    pe.wait_ge(a_h, 2 * i + u + 1)
                    pe.wait_ge(a_x1, 2 * i + u + 1)
                    for k in range(DK):
                        pe.matmul(bank[4 + u][:, 0:D], hT[:, u, k * P:(k + 1) * P], W2[:, k, :], start=(k == 0), stop=False)
                    for k in range(DK):
                        ins = pe.matmul(bank[4 + u][:, 0:D], xTs[:, u, k * P:(k + 1) * P], Mx[:, k, :], start=False, stop=(k == DK - 1))
                    ins.then_inc(a_o, 1)
            with pe.Fori(0, NT // 2) as i:
                for u in range(2):
                    pe.wait_ge(b_xn, 2 * i + u + 1)
                    pe.wait_ge(b_tc, 2 * i + u + 1)
                    for m in range(DK):
                        ins = pe.transpose(bank[u][:, m * P:(m + 1) * P], xn2[:, u, m * P:(m + 1) * P], ident[:, :])
                    ins.then_inc(b_tp, 1)
            pe.wait_ge(b_tc, NT + 2)
            for n in range(2):
                with pe.Fori(0, 16) as i:
                    pe.wait_ge(k_cnt, 16 * n + i + 1)
                    pe.matmul(bank[7][:, 0:1], ones[:, :], tk[3][:, :], start=True, stop=True).then_inc(k_sum, 1)
            pe.wait_ge(k_cnt, 33)
            pe.matmul(bank[7][:, 0:1], ones[:, :], tk[3][:, :], start=True, stop=True)
            pe.matmul(bank[6][:, 0:NB], strict[:, :], eqm[:, :], start=True, stop=True)
            pe.matmul(bank[5][:, 0:NB], ones[:, :], eqm[:, :], start=True, stop=True).then_inc(k_sum, 1)
            pe.wait_ge(k_cnt, 34)
            with pe.Fori(0, NB // 7) as i:
                for q, (nt, H1) in enumerate(((4, H1a), (3, H1b))):
                    for f in range(FB):
                        pe.wait_ge(c_g, (2 * i + q) * FB + f + 1)
                        for k in range(DK):
                            ins = pe.matmul(bank[f % 4][:, 0:nt * P].rearrange("p (t n) -> p t n", n=P), w1s[:, k, f * P:(f + 1) * P],
                                            ACC[:, ds(7 * i + 4 * q, nt), k * P:(k + 1) * P], start=(k == 0), stop=(k == DK - 1))
                        ins.then_inc(c_h, 1)
                    pe.wait_ge(c_g, (2 * i + q + 1) * FB + 4)
                    for a in range(nt):
                        pe.wait_ge(c_free, 7 * i + 4 * q + a + 1)
                        for f in range(FB):
                            ins = pe.matmul(bank[4 + (4 * q + a) % 4][:, 0:D], H1[:, f, a * P:(a + 1) * P], w2s[:, f, :],
                                            start=(f == 0), stop=(f == FB - 1))
                        ins.then_inc(c_y, 1)

        @block.vector
        def _(dve):
            c = Chain(dve, s_dve)
            dve.memset(X[:, xpart:NT, :], 0.0).then_inc(s_xpad, 1)
            dve.memset(zero, 0.0).then_inc(s_zero, 1)
            dve.memset(ones[:, :], 1.0)
            dve.memset(zcol[:, :], 0.0)
            dve.memset(onesb[:, :], 1.0)
            dve.memset(dinv[:, NB:NT], 0.0)
            dve.memset(mvar[:, NB:NT, :], 0.0)
            dve.memset(rstd[:, NB:NT], 0.0)
            dve.memset(A2[:, :, 0:1], 0.0)
            dve.sem_inc(a_x1, 2)
            dve.sem_inc(s_pr, 1)
            dve.sem_inc(s_kn, 1)
            dve.sem_inc(c_free, 3)
            dve.wait_ge(s_iota, 2)
            c.link(dve.tensor_copy(iota[:, :], iotaI[:, :]))
            c.link(dve.tensor_copy(pid[:, :], pidI[:, :]))
            c.link(dve.tensor_scalar(ident[:, :], iota[:, :], pid[:, 0:1], None, ALU.is_equal))
            c.link(dve.tensor_scalar(strict[:, :], iota[:, :], pid[:, 0:1], None, ALU.is_gt))
            c.link(dve.tensor_scalar(befb[:, 0, :], iota[:, :], pid[:, 0:1], None, ALU.is_gt))
            c.link(dve.tensor_scalar(befb[:, 1, :], iota[:, :], pid[:, 0:1], None, ALU.is_ge))
            c.link(dve.tensor_copy(iotab[:, :], iota[:, :]))
            c.link(dve.tensor_copy(iotaL, spread(iotab[0:EP, :].rearrange("p (h o) -> p h o", o=1), 2, SJ)))
            dve.sem_inc(s_const, 1)
            dve.wait_ge(s_edges, 48)
            c.link(dve.tensor_scalar(tmpI, srcI, 7, None, ALU.arith_shift_right))
            c.link(dve.tensor_copy(hfb, tmpI))
            c.link(dve.tensor_scalar(tmpI, srcI, P - 1, None, ALU.bitwise_and))
            c.link(dve.tensor_copy(rlob, tmpI))
            c.link(dve.tensor_scalar(tmpI, dstI, 7, 14, ALU.arith_shift_right, ALU.logical_shift_left))
            c.link(dve.tensor_copy(keyp[0], tmpI))
            c.link(dve.tensor_scalar(tmpI, dstI, P - 1, 7, ALU.bitwise_and, ALU.logical_shift_left))
            c.link(dve.tensor_copy(keyp[1], tmpI))
            c.link(dve.tensor_copy(wp[0], ew))
            c.link(dve.tensor_tensor(ew, ew, wp[0], ALU.subtract))
            c.link(dve.tensor_copy(wp[1], ew))
            c.link(dve.tensor_tensor(ew, ew, wp[1], ALU.subtract))
            c.link(dve.tensor_copy(wp[2], ew))
            dve.sem_inc(s_e, 1)

            def row_stats(src):
                with dve.Fori(0, NB) as t:
                    c.enter(t, 1)
                    c.mark(dve.bn_stats(row(st[:, ds(t, 1), :]), row(src[:, ds(t, 1), :])))
                c.leave(NB)
                c.wait()
                for t in range(NB):
                    ins = dve.bn_aggr(mvar[:, t, :], st[:, t, :])
                c.link(ins)
                c.link(dve.tensor_scalar(u49[:, :], mvar[:, 0:NB, 1], EPS, None, ALU.add))

            def inverse_root(r, v, tmp):
                c.link(dve.reciprocal(r, r))
                c.link(dve.tensor_tensor(tmp, r, r, ALU.mult))
                c.link(dve.tensor_tensor(tmp, tmp, v, ALU.mult))
                c.link(dve.tensor_scalar(tmp, tmp, -0.5, 1.5, ALU.mult, ALU.add))
                c.link(dve.tensor_tensor(r, r, tmp, ALU.mult))

            dve.wait_ge(s_x, 32)
            row_stats(X)
            dve.sem_inc(s_var, 1)
            dve.wait_ge(s_sqrt, 1)
            inverse_root(rstd[:, 0:NB], u49[:, :], v49[:, :])
            c.link(dve.scalar_tensor_tensor(nmr[:, :], mvar[:, 0:NB, 0], -1.0, rstd[:, 0:NB], ALU.mult, ALU.mult))
            dve.sem_inc(s_ln, 1)

            def by_edge(v, at, n, classes):
                return spread(v[:, ds(at, n)].rearrange("p (o j) -> p o j", o=1), 1, classes)

            with dve.Fori(0, NS // 2) as i:
                for u in range(2):
                    s = 2 * i + u
                    dve.wait_ge(s_cntp, s + 1)
                    dve.tensor_tensor(oh1[u], by_edge(hfb, s * SJ, SJ, NB), iotaL[:, 0:NB, :], ALU.is_equal).then_inc(s_o1, 1)
                    for q in range(2):
                        dve.wait_ge(s_h1, 2 * s + q + 1)
                        dve.tensor_tensor(rl1h[q], by_edge(rlob, s * SJ + q * HJ, HJ, P), iotaL[:, :, 0:HJ], ALU.is_equal).then_inc(s_rl, 1)
                        if q == 0:
                            dve.wait_ge(s_o1, s + 1)
                            for m in range(2):
                                ins = dve.tensor_tensor(ohw[u][:, m, :, :], oh1[u], by_edge(wp[m], s * SJ, SJ, NB), ALU.mult)
                            ins.then_inc(s_ow, 1)
            dve.wait_ge(s_deg, 1)
            c.link(dve.tensor_reduce(u49[:, :], bank[0][:, 0:WP * NB].rearrange("p (m h) -> p h m", m=WP), AX.X, ALU.add))
            c.link(dve.tensor_scalar(u49[:, :], u49[:, :], 1.0, None, ALU.add))
            c.link(dve.tensor_scalar(sel[:, :], u49[:, :], 0.0, None, ALU.is_gt))
            c.link(dve.tensor_scalar(t49[:, :], u49[:, :], 1e-30, None, ALU.max))
            dve.sem_inc(s_var, 1)
            dve.wait_ge(s_cntc, NS + 2)
            dve.wait_ge(s_ow, 2 * NS)
            dve.wait_ge(s_scat, 16)
            flat = cnt.rearrange("p s h -> p (s h)")

            def ceil_shift(outf, tmp_i, inf, n):
                c.link(dve.tensor_scalar(tmp_i, inf, float(2 ** n - 1), None, ALU.add))
                c.link(dve.tensor_scalar(tmp_i, tmp_i, n, None, ALU.arith_shift_right))
                c.link(dve.tensor_copy(outf, tmp_i))

            def restart(major):
                c.link(dve.memset(keep, 1.0))
                c.link(dve.memset(keep.rearrange("p (a b) -> p a b", a=major)[:, :, 0:1], 0.0))

            ceil_shift(pcf, inc.bitcast(I32), flat, BL)
            pc3 = pcf.rearrange("p (s h) -> p s h", s=NS)
            restart(NS)
            c.link(dve.tensor_tensor_scan(inc, keep, pcf, 0.0, ALU.mult, ALU.add))
            inc3 = inc.rearrange("p (s h) -> p s h", s=NS)
            c.link(dve.tensor_tensor(lbx[:, :, 0:NB], inc3, pc3, ALU.subtract))
            c.link(dve.tensor_copy(lbx[:, :, NB:NB + 1], inc3[:, :, NB - 1:NB]))
            c.link(dve.tensor_copy(pcT, pc3.rearrange("p s h -> p h s")))
            restart(NB)
            c.link(dve.tensor_tensor_scan(inc, keep, pcT.rearrange("p h s -> p (h s)"), 0.0, ALU.mult, ALU.add))
            incT = inc.rearrange("p (h s) -> p h s", s=NS)
            ceil_shift(tpf[:, :], v49[:, :].bitcast(I32), incT[:, :, NS - 1], BPG.bit_length() - 1)
            c.link(dve.tensor_tensor_scan(ginc[:, :], ones[:, 0:NB], tpf[:, :], 0.0, ALU.mult, ALU.add))
            c.link(dve.tensor_tensor(tpf[:, :], ginc[:, :], tpf[:, :], ALU.subtract))
            c.link(dve.tensor_scalar(tpf[:, :], tpf[:, :], float(BPG), None, ALU.mult))
            c.link(dve.tensor_tensor(incT, incT, pcT, ALU.subtract))
            c.link(dve.tensor_tensor(incT, incT, spread(tpf[:, :].rearrange("p (h o) -> p h o", o=1), 2, NS), ALU.add))
            c.link(dve.tensor_tensor(big[:, :, 0:NB], incT.rearrange("p h s -> p s h"), lbx[:, :, 0:NB], ALU.subtract))
            c.link(dve.memset(big[:, :, NB:NB + 1], float(SPARE)))
            c.link(dve.tensor_copy(dlt[:, :, 0:1], big[:, :, 0:1]))
            c.link(dve.tensor_tensor(dlt[:, :, 1:NB + 1], big[:, :, 1:NB + 1], big[:, :, 0:NB], ALU.subtract))
            for k in range(HI):
                c.link(dve.scalar_tensor_tensor(big, lbx, pid[:, k:k + 1], dlt, ALU.is_le, ALU.mult))
                c.link(dve.tensor_reduce(ridxf[:, :], big, AX.X, ALU.add))
                c.link(dve.tensor_scalar(ridx[:, :, k], ridxf[:, :], pid[:, k:k + 1], None, ALU.add))
            for a in range(HG):
                c.link(dve.tensor_scalar(hm[:, a:a + 1], pid[:, 0:1], float(HG), float(a), ALU.mult, ALU.add))
            for a in range(HG):
                c.link(dve.tensor_scalar(hm49[:, a, :], ginc[:, :], hm[:, a:a + 1], None, ALU.is_le))
            c.link(dve.tensor_reduce(hm[:, :], hm49[:, :, :], AX.X, ALU.add))
            c.link(dve.tensor_copy(hmI[:, :], hm[:, :]))
            dve.sem_inc(s_hm, 1)
            dve.wait_ge(s_sqrt, 2)
            inverse_root(dinv[:, 0:NB], t49[:, :], u49[:, :])
            c.link(dve.tensor_tensor(dinv[:, 0:NB], dinv[:, 0:NB], sel[:, :], ALU.mult))
            dve.wait_ge(s_xn, NB)
            dve.sem_inc(s_dinv, 1)
            c.link(dve.tensor_scalar(lbx, lbx, float(B), -1.0, ALU.mult, ALU.add))
            c.link(dve.memset(Z, 0.0))
            dve.sem_inc(s_ridx, 1)

            def rank_onehots(s, b):
                dve.tensor_tensor(O2[b], by_edge(hfb, s * SJ, SJ, NB), iotaL[:, 0:NB, :], ALU.is_equal).then_inc(s_o2, 1)

            def rank(s, b, waiting):
                dve.wait_ge(s_cross, s + 1)
                l2 = spread(lbx[0:EP, ds(s, 1), 0:NB], 1, 2)
                c.link(dve.tensor_tensor(A2[:, :, 1:], bank[2][0:EP, 0:2 * NB].rearrange("p (q h) -> p q h", q=2), l2, ALU.add))
                c.link(dve.tensor_tensor(Z[:, :, 0], A2[:, 0, 1:], A2[:, 1, 0:NB], ALU.subtract))
                f1 = F3.rearrange("p h j -> p (h j)")
                c.link(dve.tensor_tensor_scan(f1, Z.rearrange("p h j -> p (h j)"), O2[b].rearrange("p h j -> p (h j)"),
                                              0.0, ALU.add, ALU.add))
                c.link(dve.tensor_tensor(F3, F3, O2[b], ALU.mult))
                c.link(dve.tensor_reduce(posf[:, :], F3.rearrange("p h j -> p j h"), AX.X, ALU.add))
                c.link(dve.tensor_copy(posI[:, :], posf[:, :]))
                c.link(dve.tensor_scalar(poaI[:, :], posI[:, :], BL, P - 1, ALU.arith_shift_right, ALU.bitwise_and))
                c.link(dve.tensor_copy(lof[:, :], poaI[:, :]))
                c.link(dve.tensor_scalar(poaI[:, :], posI[:, :], BL + 7, BL, ALU.arith_shift_right, ALU.logical_shift_left))
                c.link(dve.tensor_scalar(pobI[:, :], posI[:, :], B - 1, None, ALU.bitwise_and))
                c.link(dve.tensor_tensor(pobI[:, :], pobI[:, :], poaI[:, :], ALU.bitwise_or))
                c.link(dve.tensor_copy(subf[:, :], pobI[:, :]))
                if waiting:
                    dve.wait_ge(s_scat, 16 * (HI * (s - 1)) + 16)
                passed(dve, "dve")
                dve.tensor_copy(sidx[:, b:b + 1, :], ridx[:, ds(s, 1), :]).then_inc(s_sidx, 1)

            def place_runs(s, b, more):
                if more:
                    rank_onehots(s + 1, 1 - b)
                for u in range(2):
                    dve.wait_ge(s_half, 2 * s + u + 1)
                    sv = spread(subf[:, u * HJ:(u + 1) * HJ].rearrange("p (o j) -> p o j", o=1), 1, SUB)
                    dve.tensor_tensor(sub1h[u], sv, iotaL[:, 0:SUB, 0:HJ], ALU.is_equal).then_inc(s_sub, 1)
                    lv = spread(lof[:, u * HJ:(u + 1) * HJ].rearrange("p (o j) -> p o j", o=1), 1, P)
                    dve.tensor_tensor(lo1h[u], lv, iotaL[:, :, 0:HJ], ALU.is_equal)
                    dve.wait_ge(s_sub, 2 * s + u + 1)
                    at = s * SJ + u * HJ
                    for m in range(WP):
                        ins = dve.tensor_tensor(mv[u][:, m, 0, :, :], sub1h[u], by_edge(keyp[m], at, HJ, SUB), ALU.mult)
                        if m == 0:
                            dve.tensor_tensor(mv[u][:, 0, 1, :, :], sub1h[u], by_edge(wp[0], at, HJ, SUB), ALU.mult)
                    ins.then_inc(s_key, 1)
                if more:
                    dve.wait_ge(s_key, 2 * s + 2)
                    rank(s + 1, 1 - b, True)

            rank_onehots(0, 0)
            rank(0, 0, False)
            with dve.Fori(0, NS // 2 - 1) as i:
                c.enter(i, 24)
                place_runs(2 * i, 0, True)
                place_runs(2 * i + 1, 1, True)
            c.leave(NS // 2 - 1)
            place_runs(NS - 2, 0, True)
            place_runs(NS - 1, 1, False)
            dve.wait_ge(s_half, 2 * NS + 2)
            dve.wait_ge(s_wm, 2 * NS)
            passed(dve, "dve")
            with dve.Fori(0, NT // 2) as t:
                c.enter(t, 1)
                c.mark(dve.tensor_scalar(row(ACC[:, ds(t, 1), :]), row(X[:, ds(t, 1), :]), dinv[:, ds(t, 1)], None, ALU.mult))
            c.leave(NT // 2)
            c.wait()
            dve.sem_inc(s_acc, 1)
            dve.wait_ge(s_w, 16 * 12)
            w3 = kvf.rearrange("p (h w) -> p h w", w=HW)
            wm = wmean[:, :]
            c.link(dve.tensor_reduce(wm, w3, AX.X, ALU.add))
            c.link(dve.tensor_scalar(wm, wm, 1.0 / HW, None, ALU.mult))
            c.link(dve.tensor_tensor(w3, w3, spread(wm.rearrange("p (h o) -> p h o", o=1), 2, HW), ALU.subtract))
            dve.sem_inc(s_wc, 1)
            dve.wait_ge(s_rt, 1)
            for b in range(ceil_div(CT, 4)):
                n = min(4, CT - 4 * b)
                ins = dve.tensor_copy(cidxI.rearrange("p (c t) -> p t c", t=CT)[:, 4 * b:4 * b + n, :],
                                      bank[b][:, 0:n * P].rearrange("p (t c) -> p t c", t=n))
                ins.then_inc(s_rk, 1)
            dve.wait_ge(s_rk, ceil_div(CT, 4))
            c.link(dve.tensor_scalar(rloI, cidxI, P - 1, None, ALU.bitwise_and))
            c.link(dve.tensor_copy(rlo, rloI))
            c.link(dve.tensor_scalar(cidxI, cidxI, 7, None, ALU.arith_shift_right))
            dve.wait_ge(s_hrow, 16)
            dve.wait_ge(s_rw, ceil_div(CT, 4))
            dve.wait_ge(s_acc, NT // 2 + 1)
            dve.sem_inc(s_seen["dve"], 1)

            def prep(g, slot):
                for k in range(CH):
                    dve.tensor_scalar(OH[:, slot, k, :], iota[:, :], rlo[:, ds(CH * g + k, 1)],
                                      recw[:, ds(CH * g + k, 1)], ALU.is_equal, ALU.mult)
                dve.tensor_copy(gidx[:, slot, :], cidxI[:, ds(CH * g, CH)]).then_inc(s_prep, 1)

            def add_group(g, slot):
                h = dve.value_load(hrow[0:1, ds(g, 1)], min_val=0, max_val=NB)
                a = row(ACC[:, ds(h, 1), :])
                c.wait()
                dve.wait_ge(s_grp, g + 2)
                c.mark(dve.tensor_tensor(a, a, bank[3 + slot][:, 0:D], ALU.add))

            for g in range(SLOTS - 1):
                prep(g, g)

            def body(i, with_kv):
                for u in range(UG):
                    g = UG * i + u
                    dve.wait_ge(s_grp, g + 1)
                    prep(g + SLOTS - 1, (u + SLOTS - 1) % SLOTS)
                    add_group(g, u % SLOTS)
                    if with_kv and u == 4:
                        dve.wait_ge(s_sq, i + 1)
                        c.link(dve.tensor_reduce(ss[:, :], kvsq.rearrange("p (h w) -> p h w", w=HW), AX.X, ALU.add))
                        c.link(dve.tensor_scalar(ss[:, :], ss[:, :], 1.0 / HW, EPS, ALU.mult, ALU.add))
                        c.link(dve.tensor_tensor(pr[:, :], ss[:, 0:HEADS], ss[:, HEADS:], ALU.mult))
                        dve.sem_inc(s_pr, 1)
                    if with_kv and u == 6:
                        dve.wait_ge(s_sr, i + 1)
                        inverse_root(rr[:, :], pr[:, :], r2[:, :])
                        dve.wait_ge(s_dot, i + 1)
                        dve.tensor_tensor(kn.rearrange("p (h w) -> p h w", w=HW), bank[1][:, :].rearrange("p (h w) -> p h w", w=HW),
                                          spread(rr[:, :].rearrange("p (h o) -> p h o", o=1), 2, HW), ALU.mult).then_inc(s_kn, 1)

            with dve.Fori(0, NB) as i:
                c.enter(i, UG + 8)
                body(i, True)
            c.leave(NB)
            with dve.Fori(NB, NIT) as i:
                c.enter(i - NB, UG)
                body(i, False)
            c.leave(NIT - NB)
            c.wait()
            dve.wait_ge(s_dot, NB + 2)
            dve.sem_inc(s_added, 1)
            c.link(dve.memset(dots, 0.0))
            for j in range(PAIRS):
                for q in range(2):
                    r0, r1 = q * HW, (q + 1) * HW
                    ins = dve.tensor_copy(dots[r0:r1, j, r0:r1], bank[2][r0:r1, j * P + r0:j * P + r1])
                    c.mark(ins)
            c.wait()
            dve.sem_inc(s_dd, 1)
            c.link(dve.tensor_tensor(b2o[:, :], b2o[:, :], brow[:, :], ALU.add))
            dve.wait_ge(s_vh, 1)
            c.link(dve.tensor_tensor(b1c[:, :], b1c[:, :], bank[3][:, D:D + DK], ALU.add))
            dve.sem_inc(s_b1, 1)
            with dve.Fori(0, NT // 2) as i:
                c.enter(i, 4)
                for u in range(2):
                    t = 2 * i + u
                    dve.tensor_scalar(ag[:, u, :], row(ACC[:, ds(t, 1), :]), dinv[:, ds(t, 1)], None, ALU.mult).then_inc(a_ag, 1)
                for u in range(2):
                    t = 2 * i + u
                    dve.wait_ge(a_xin[u], 16 * i + 16)
                    c.link(dve.tensor_tensor(xin[:, u, :], xin[:, u, :], b2o[:, :], ALU.add))
                    dve.wait_ge(a_o, t + 3)
                    c.link(dve.tensor_tensor(row(ACC[:, ds(t, 1), :]), bank[4 + u][:, 0:D], xin[:, u, :], ALU.add))
                    dve.sem_inc(a_x1, 1)
            c.leave(NT // 2)
            row_stats(ACC)
            dve.sem_inc(b_var, 1)
            dve.wait_ge(b_root, 1)
            inverse_root(rstd[:, 0:NB], u49[:, :], v49[:, :])
            with dve.Fori(0, NT // 2) as i:
                c.enter(i, 6)
                for u in range(2):
                    t = 2 * i + u
                    dve.wait_ge(b_tp, t + 1)
                    c.link(dve.tensor_scalar(xn2[:, u, :], row(ACC[:, ds(t, 1), :]), mvar[:, ds(t, 1), 0], rstd[:, ds(t, 1)],
                                             ALU.subtract, ALU.mult))
                    dve.tensor_tensor(row(X[:, ds(t, 1), :]), row(ACC[:, ds(t, 1), :]), xn2[:, u, :], ALU.add).then_inc(b_xn, 1)
                    c.link(dve.tensor_tensor_reduce(yt[:, u, :], xn2[:, u, :], wr[:, :], 1.0, 0.0, ALU.mult, ALU.add, wcol[:, :]))
                    dve.sem_inc(s_seen["dve"], 1)
                    c.link(dve.tensor_copy(wt[:, ds(t, 1)], wcol[:, :]))
            c.leave(NT // 2)
            c.link(dve.tensor_scalar(wt[:, 0:NB], wt[:, 0:NB], brc[:, 0:1], None, ALU.add))
            bits = wt[:, 0:NB].bitcast(I32)
            c.link(dve.tensor_scalar(keyI[:, :], bits, 31, 0x7FFFFFFF, ALU.arith_shift_right, ALU.bitwise_and))
            c.link(dve.tensor_tensor(keyI[:, :], keyI[:, :], bits, ALU.bitwise_xor))
            c.link(dve.tensor_scalar(kbI[:, :], keyI[:, :], 16, None, ALU.arith_shift_right))
            c.link(dve.tensor_scalar(khi[:, :], kbI[:, :], 32768.0, None, ALU.add))
            c.link(dve.tensor_scalar(kbI[:, :], keyI[:, :], 0xFFFF, None, ALU.bitwise_and))
            c.link(dve.tensor_copy(klo[:, :], kbI[:, :]))
            c.link(dve.tensor_scalar(tk[4][:, :], pid[:, 0:1], float(LAST), None, ALU.is_lt))
            c.link(dve.tensor_scalar(tk[5][:, :], tk[4][:, :], -1.0, None, ALU.add))
            c.link(dve.tensor_scalar(khi[:, xpart:NB], khi[:, xpart:NB], tk[4][:, :], tk[5][:, :], ALU.mult, ALU.add))
            top, bit, cand, cntc, ge, need = (t[:, :] for t in tk)

            def search(values, n):
                c.link(dve.memset(top, 0.0))
                c.link(dve.memset(bit, 32768.0))
                with dve.Fori(0, 16) as i:
                    c.enter(i, 6)
                    c.link(dve.tensor_tensor(cand, top, bit, ALU.add))
                    c.link(dve.tensor_scalar(gtm[:, :], values, cand, None, ALU.is_ge))
                    c.link(dve.tensor_reduce(cntc, gtm[:, :], AX.X, ALU.add))
                    dve.sem_inc(k_cnt, 1)
                    dve.wait_ge(k_sum, 16 * n + i + 1)
                    c.link(dve.tensor_scalar(ge, bank[7][:, 0:1], float(TOP), bit, ALU.is_ge, ALU.mult))
                    c.link(dve.tensor_tensor(top, top, ge, ALU.add))
                    c.link(dve.tensor_scalar(bit, bit, 0.5, None, ALU.mult))
                c.leave(16)

            search(khi[:, :], 0)
            c.link(dve.tensor_scalar(gtm[:, :], khi[:, :], top, 65537.0, ALU.is_gt, ALU.mult))
            c.link(dve.tensor_scalar(eqm[:, :], khi[:, :], top, None, ALU.is_equal))
            c.link(dve.tensor_scalar(klo[:, :], klo[:, :], 1.0, None, ALU.add))
            c.link(dve.tensor_tensor(comb[:, :], klo[:, :], eqm[:, :], ALU.mult))
            c.link(dve.tensor_tensor(comb[:, :], comb[:, :], gtm[:, :], ALU.add))
            c.link(dve.tensor_scalar(comb[:, :], comb[:, :], -1.0, None, ALU.add))
            search(comb[:, :], 1)
            c.link(dve.tensor_scalar(eqm[:, :], comb[:, :], top, None, ALU.is_equal))
            c.link(dve.tensor_scalar(sel[:, :], comb[:, :], top, None, ALU.is_gt))
            c.link(dve.tensor_reduce(cntc, sel[:, :], AX.X, ALU.add))
            dve.sem_inc(k_cnt, 1)
            dve.wait_ge(k_sum, 33)
            c.link(dve.tensor_scalar(need, bank[7][:, 0:1], -1.0, float(TOP), ALU.mult, ALU.add))
            c.link(dve.tensor_copy(v49[:, :], bank[5][:, 0:NB]))
            c.link(dve.tensor_tensor_scan(u49[:, :], ones[:, 0:NB], v49[:, :], 0.0, ALU.mult, ALU.add))
            c.link(dve.tensor_tensor(u49[:, :], u49[:, :], v49[:, :], ALU.subtract))
            c.link(dve.tensor_tensor(u49[:, :], u49[:, :], bank[6][:, 0:NB], ALU.add))
            dve.sem_inc(k_cnt, 1)
            c.link(dve.tensor_scalar(u49[:, :], u49[:, :], need, None, ALU.is_lt))
            c.link(dve.tensor_tensor(u49[:, :], u49[:, :], eqm[:, :], ALU.mult))
            c.link(dve.tensor_tensor(sel[:, :], sel[:, :], u49[:, :], ALU.add))
            c.link(dve.tensor_tensor(wsel[:, :], wt[:, 0:NB], sel[:, :], ALU.mult))

            def finish(i, first):
                for q in range(7):
                    t = 7 * i + q
                    if not first:
                        dve.wait_ge(c_st[q], 16 * i)
                    dve.wait_ge(c_y, t + 8)
                    passed(dve, "dve")
                    dve.tensor_tensor(ot[:, q, :], bank[4 + q % 4][:, 0:D], fb2[:, :], ALU.add).then_inc(c_free, 1)
                    dve.wait_ge(c_free, t + 4)
                    dve.scalar_tensor_tensor(ot[:, q, :], ot[:, q, :], wsel[:, ds(t, 1)], row(X[:, ds(t, 1), :]),
                                             ALU.mult, ALU.add).then_inc(c_ot, 1)

            finish(0, True)
            with dve.Fori(1, NB // 7) as i:
                finish(i, False)


_INS = ['x', 'src', 'dst', 'edge_weight', 'L0_gnn_b', 'L0_gnn_W1', 'L0_gnn_b1', 'L0_gnn_W2', 'L0_gnn_b2',
        'L0_mix_b_out', 'L0_ffn_wr', 'L0_ffn_br', 'L0_ffn_w1', 'L0_ffn_b1', 'L0_ffn_w2', 'L0_ffn_b2']


def kernel(**inputs):
    import numpy as _np
    import concourse.bacc as _bacc
    from concourse import mybir as _mybir
    from concourse.bass_utils import run_bass_kernel_spmd as _run

    nc = _bacc.Bacc("TRN2", target_bir_lowering=False, num_devices=1)
    qkv = _np.asarray(inputs['L0_mix_w_qkv'])
    inner = qkv.shape[0] // 3
    laid = {name: _np.asarray(inputs[name]) for name in _INS}
    laid['wq'] = qkv[:inner]
    laid['kvT'] = qkv[inner:].T
    laid['woT'] = _np.asarray(inputs['L0_mix_w_out']).T
    laid['WT'] = _np.asarray(inputs['L0_gnn_W']).T
    arrays, aps = {}, {}
    for name, a in laid.items():
        a = _np.ascontiguousarray(a)
        arrays[f"in_{name}_dram"] = a
        aps[name] = nc.dram_tensor(f"in_{name}_dram", a.shape, _mybir.dt.from_np(a.dtype), kind="ExternalInput").ap()
    out = nc.dram_tensor("out_0_dram", laid['x'].shape, _mybir.dt.float32, kind="ExternalOutput").ap()
    gps_layer(nc, aps, out)
    r = _run(nc, [arrays], core_ids=[0])
    return r.results[0]["out_0_dram"]
```

```python
from contextlib import ExitStack

import concourse.bass as bass
from concourse import mybir

ALU = mybir.AluOpType
ACT = mybir.ActivationFunctionType
AX = mybir.AxisListType
F32 = mybir.dt.float32
BF16 = mybir.dt.bfloat16
I32 = mybir.dt.int32
ds = bass.ds

P = 128
EPS = 1e-5


def ceil_div(a, b):
    return -(-a // b)


def spread(v, axis, n):
    shape = list(v.shape)
    shape[axis] = n
    return v.broadcast_to(shape)


class Chain:

    def __init__(self, eng, sem):
        self.eng, self.sem, self.base, self.k, self.i, self.per = eng, sem, 0, 0, None, 0

    def mark(self, ins):
        self.k += 1
        ins.then_inc(self.sem, 1)

    def wait(self):
        at = self.base + self.k
        self.eng.wait_ge(self.sem, at if self.i is None else self.i * self.per + at)

    def link(self, ins):
        self.mark(ins)
        self.wait()

    def enter(self, i, per):
        self.base, self.k, self.i, self.per = self.base + self.k, 0, i, per

    def leave(self, n):
        assert self.k == self.per, (self.k, self.per)
        self.base, self.k, self.i = self.base + n * self.per, 0, None


def gps_layer(nc, A, out):
    x_d, src_d, dst_d, ew_d = A["x"], A["src"], A["dst"], A["edge_weight"]
    N, D = x_d.shape
    E = src_d.shape[0]
    NB = ceil_div(N, P)
    NT = NB + NB % 2
    LAST = N - (NB - 1) * P
    DK = D // P
    EP = 125
    EC = E // EP
    SJ = 40
    NS = EC // SJ
    HJ = SJ // 2
    B = 8
    BL = B.bit_length() - 1
    ROUND = 1.5 * 2 ** 23
    RW = 2
    HI = ceil_div(ceil_div(EP * SJ + NB * (B - 1), B), P)
    HR = HI // 2
    SUB = HI * B
    WP = 3
    WD = 2
    CH = 2
    BPG = CH * P // B
    SLOTS = 5
    SB = 5
    UG = 2 * SLOTS
    runs_max = (E + NS * NB * (B - 1)) // B
    groups_max = (runs_max + NB * (BPG - 1)) // BPG
    NG = ceil_div(groups_max, UG) * UG
    NIT = NG // UG
    CT = ceil_div(NG * CH, P)
    SPARE = CT * P * P // B
    RUNS = SPARE + HI * P
    PK = 2
    HG = ceil_div(NG, PK * P) * PK
    assert E == EP * EC and EC == SJ * NS and NS % 2 == 0 and HI % 2 == 0
    assert NT == NB + 1 and NB % 7 == 0 and NB < 64 and NIT > NB + NB // 2
    assert CT * P >= (NG + SLOTS - 1) * CH and UG % PK == 0
    GD = A["woT"].shape[0]
    KV = 2 * GD
    HW = 64
    HEADS = GD // HW
    PAIRS = GD // P
    F = A["L0_ffn_w1"].shape[1]
    FB = F // P
    SR = 4
    SD = 8
    TOP = max(1, N // 2) - 1

    y_d = nc.dram_tensor("y_table", [NB * P, D], F32, kind="Internal").ap()
    rec_d = [nc.dram_tensor(f"records_{i}", [RUNS, B * RW], F32, kind="Internal").ap() for i in range(2)]
    hmap_d = nc.dram_tensor("block_of_group", [HG // PK * P], I32, kind="Internal").ap()

    with ExitStack() as ctx:
        def sb(name, shape, dt=F32):
            return ctx.enter_context(nc.sbuf_tensor(name, shape, dt))

        def sem(name):
            return ctx.enter_context(nc.semaphore(name))

        bank = [ctx.enter_context(nc.psum_tensor(f"bank{i}", [P, 512], F32)) for i in range(8)]

        X = sb("X", [P, NT, D])
        ACC = sb("ACC", [P, NT, D])
        AR = sb("AR", [P, 18304])
        accf = ACC[:, :, :].rearrange("p t d -> p (t d)")

        def cut(base, start, shape, rows=P):
            n = 1
            for s in shape:
                n *= s
            v = base[0:rows, start:start + n]
            if len(shape) == 2:
                v = v.rearrange("p (a b) -> p a b", a=shape[0])
            if len(shape) == 3:
                v = v.rearrange("p (a b c) -> p a b c", a=shape[0], b=shape[1])
            return v, start + n

        def cutb(base, start, shape, rows=P):
            n = 1
            for q in shape:
                n *= q
            v = base[0:rows, start:start + n // 2].bitcast(BF16)
            names = "abcd"[:len(shape)]
            if len(shape) > 1:
                v = v.rearrange(f"p ({' '.join(names)}) -> p {' '.join(names)}", **dict(zip(names[:-1], shape)))
            return v, start + n // 2

        o = 0
        hfb, o = cutb(AR, o, [EC], EP)
        keyp = []
        for _ in range(WP):
            v, o = cutb(AR, o, [EC], EP)
            keyp.append(v)
        rlob = keyp[WP - 1]
        wp = []
        for _ in range(WP):
            v, o = cutb(AR, o, [EC], EP)
            wp.append(v)
        iotaL, o = cutb(AR, o, [P, SJ], EP)
        zero, _ = cut(AR, o, [RUNS // P * B * RW])
        lbx, o = cut(AR, o, [NS, NB + 1])
        o_dead = o
        dlt, o = cut(AR, o, [NS, NB + 1])
        cnt, o = cut(AR, o, [NS, NB])
        ys, o = cut(AR, o, [2, D])
        lt, o = cutb(AR, o, [HJ, P], EP)
        o_sort = o
        assert RUNS // P * B * RW <= 2 * NS * (NB + 1)
        o = 0
        srcI = accf[0:EP, 0:EC].bitcast(I32)
        dstI = accf[0:EP, EC:2 * EC].bitcast(I32)
        tmpI = accf[0:EP, 2 * EC:3 * EC].bitcast(I32)
        ew = accf[0:EP, 3 * EC:4 * EC]
        o = 0
        oh1, ohw, rl1h = [], [], []
        for _ in range(2):
            v, o = cutb(accf, o, [NB, SJ], EP)
            oh1.append(v)
        for _ in range(2):
            v, o = cutb(accf, o, [WP, NB, SJ], EP)
            ohw.append(v)
        for _ in range(2):
            v, o = cutb(accf, o, [P, HJ], EP)
            rl1h.append(v)
        assert o <= NT * D
        o = 0
        pcf, o = cut(accf, o, [NS * NB])
        pcT, o = cut(accf, o, [NB, NS])
        inc, o = cut(accf, o, [NS * NB])
        keep, o = cut(accf, o, [NS * NB])
        big, o = cut(accf, o, [NS, NB + 1])
        hm49, o = cut(accf, o, [HG, NB])
        assert o <= NT * D
        o = 0
        O2, lo1h, sub1h = [], [], []
        for _ in range(2):
            v, o = cutb(accf, o, [NB, SJ], EP)
            O2.append(v)
        F3, o = cut(accf, o, [NB, SJ], EP)
        Z, o = cut(accf, o, [NB, SJ], EP)
        for _ in range(2):
            v, o = cutb(accf, o, [P, HJ], EP)
            lo1h.append(v)
        for _ in range(2):
            v, o = cutb(accf, o, [SUB, HJ], EP)
            sub1h.append(v)
        mv1, o = cutb(accf, o, [WP, RW, SUB * HJ], EP)
        assert o <= NT * D
        mv0, o = cutb(AR, o_dead, [WP, RW, SUB * HJ], EP)
        assert o <= o_dead + NS * (2 * NB + 1)
        mv = [v.rearrange("p m w (s j) -> p m w s j", j=HJ) for v in (mv0, mv1)]
        o = 0
        rec, o = cut(AR, o, [CT, P, RW])
        cidx, o = cut(AR, o, [CT * P])
        rlo, o = cut(AR, o, [CT * P])
        recw, o = cut(AR, o, [CT * P])
        cidxI, rloI = cidx.bitcast(I32), rlo.bitcast(I32)
        rec1, _ = cut(AR, o, [CT, P, RW])
        G, o = cut(AR, o, [SLOTS, CH, D])
        OH, o = cut(AR, o, [SLOTS, CH, P])
        xin, _ = cut(AR, o, [2, D])
        xTs, _ = cut(AR, o + 2 * D, [2, D])
        kvsq, o = cut(AR, o, [KV])
        kn, o = cut(AR, o, [GD])
        vs, o = cut(AR, o, [GD])
        xs, o = cut(AR, o, [D])
        xT, o = cut(AR, o, [D])
        wq, o = cut(AR, o, [PAIRS, D])
        wo, o = cut(AR, o, [PAIRS, D])
        o_gather = o
        o = 0
        w1s, o = cut(AR, o, [DK, F])
        w2s, o = cut(AR, o, [FB, D])
        ot, o = cut(AR, o, [7, D])
        x1s, o = cut(AR, o, [2, D])
        xn2, o = cut(AR, o, [2, D])
        prod, o = cut(AR, o, [2, D])
        H1a, o = cut(AR, o, [FB, 4 * P])
        H1b, o2 = cut(AR, o, [FB, 3 * P])
        assert o2 <= 18304, o2
        ag, o = cut(AR, o, [2, D])
        agT, o = cut(AR, o, [2, D])
        hT, o = cut(AR, o, [2, D])
        assert o <= o2

        assert max(o_sort, o_gather) + HG // PK * P <= 18304
        hrow = AR[0:1, 18304 - HG // PK * P:18304].bitcast(I32)

        wkv = sb("wkv", [P, DK, KV])
        WT = sb("WT", [P, DK, D])
        W1 = sb("W1", [P, DK, D])
        W2 = sb("W2", [P, DK, D])
        WW = sb("WW", [P, DK, D])
        kvf = wkv[:, :, :].rearrange("p k n -> p (k n)")
        dots, o = cut(kvf, 0, [PAIRS, P])
        Vh, o = cut(kvf, o, [PAIRS, D])
        Mx, o = cut(kvf, o, [DK, D])
        assert o <= DK * KV
        bc = sb("bc", [P, DK])
        b1c = sb("b1c", [P, DK])
        fb1 = sb("fb1", [P, FB])
        b2o = sb("b2o", [P, D])
        brow = sb("brow", [P, D])
        fb2 = sb("fb2", [P, D])
        wr = sb("wr", [P, D])
        brc = sb("brc", [P, 1])
        iotaI = sb("iotaI", [P, P], I32)
        iota = sb("iota", [P, P])
        pidI = sb("pidI", [P, 1 + HI], I32)
        pid = sb("pid", [P, 1 + HI])
        ident = sb("ident", [P, P])
        strict = sb("strict", [P, P])
        ones = sb("ones", [P, P])
        onesb = sb("onesb", [P, P], BF16)
        befb = sb("befb", [P, 2, P], BF16)
        iotab = sb("iotab", [P, P], BF16)
        zcol = sb("zcol", [P, P])
        st = sb("st", [P, NB, 6])
        mvar = sb("mvar", [P, NT, 2])
        rstd = sb("rstd", [P, NT])
        t49 = sb("t49", [P, NB])
        v49 = sb("v49", [P, NB])
        u49 = sb("u49", [P, NB])
        dinv = sb("dinv", [P, NT])
        wmean = sb("wmean", [P, DK * 2 * HEADS])
        ginc = sb("ginc", [P, NB])
        tpf = sb("tpf", [P, NB])
        ridx = sb("ridx", [P, NS, HI], I32)
        ridxf = sb("ridxf", [P, NS])
        hm = sb("hm", [P, HG])
        hmI = sb("hmI", [P, HG // PK], I32)
        A2 = sb("A2", [EP, 2, NB + 1])
        posf = sb("posf", [EP, SJ])
        posd = sb("posd", [EP, SJ])
        lob = sb("lob", [EP, SJ], BF16)
        nlo = sb("nlo", [EP, 2, SJ])
        subb = sb("subb", [EP, SJ], BF16)
        sidx = sb("sidx", [P, 2, HI], I32)
        sbuf = sb("sbuf", [P, 2, SUB * RW])
        nmr = sb("nmr", [P, NB])
        gidx = sb("gidx", [P, SLOTS, CH], I32)
        ss = sb("ss", [P, 2 * HEADS])
        pr = sb("pr", [P, HEADS])
        rr = sb("rr", [P, HEADS])
        r2 = sb("r2", [P, HEADS])
        wt = sb("wt", [P, NT])
        st2 = sb("st2", [P, 2, 6])
        mv2 = sb("mv2", [P, 2, 2])
        v2 = sb("v2", [P, 2])
        r2v = sb("r2v", [P, 2])
        t2 = sb("t2", [P, 2])
        wcol = sb("wcol", [P, 2])
        steps = sb("steps", [P, SD, SR])
        cand = sb("cand", [P, SR])
        cnts = sb("cnts", [P, SR])
        reach = sb("reach", [P, SR, NB])
        keyI = sb("keyI", [P, NB], I32)
        kbI = sb("kbI", [P, NB], I32)
        khi = sb("khi", [P, NB])
        klo = sb("klo", [P, NB])
        comb = sb("comb", [P, NB])
        gtm = sb("gtm", [P, NB])
        eqm = sb("eqm", [P, NB])
        tk = [sb(f"tk{i}", [P, 1]) for i in range(5)]
        wsel = sb("wsel", [P, NB])
        sel = sb("sel", [P, NB])

        s_wq = sem("mixer_weights_loaded")
        s_x, s_xpad, s_edges = sem("x_loaded"), sem("x_padded"), sem("edges_loaded")
        s_w, s_wf = sem("weights_loaded"), sem("tail_weights_loaded")
        s_iota, s_zero, s_const, s_rk = sem("iota_done"), sem("zeros_ready"), sem("constants_ready"), sem("record_keys_copied")
        s_dve = sem("dve_chain")
        s_var, s_sqrt = sem("variances_ready"), sem("roots_taken")
        s_e = sem("edge_fields_ready")
        s_o1, s_ow, s_rl = sem("block_onehots"), sem("weighted_onehots"), sem("row_onehots")
        s_cntp, s_cntc, s_h1 = sem("cells_counted"), sem("cell_counts_copied"), sem("row_onehots_used")
        s_deg = sem("degrees_summed")
        s_ridx, s_hm = sem("run_places_ready"), sem("group_blocks_ready")
        s_hmd, s_hrow = sem("group_blocks_stored"), sem("group_blocks_loaded")
        s_o2, s_cross, s_scan, s_rank = (sem(n) for n in ("edge_block_onehots", "partition_prefixes", "ranks_scanned", "ranks_masked"))
        s_sub, s_key, s_wm = sem("run_onehots"), sem("keys_placed"), sem("edge_weights_placed")
        s_lo = sem("lane_onehots_second_half")
        s_split, s_dist = sem("ranks_split"), sem("lane_distances")
        s_half, s_runs, s_runc = sem("halves_multiplied"), sem("runs_summed"), sem("runs_copied")
        s_sidx, s_scd = sem("run_indices"), sem("scatters_over")
        s_scat = [sem("records_written_0"), sem("records_written_1")]
        s_acc, s_rec, s_ln = sem("acc_started"), sem("records_loaded"), sem("ln_scales_ready")
        s_xn, s_dinv, s_yt = sem("xn_ready"), sem("dinv_ready"), sem("table_tile_ready")
        s_y = [sem("table_stored_0"), sem("table_stored_1")]
        s_rt, s_rw, s_merged = sem("records_transposed"), sem("record_weights_copied"), sem("records_merged")
        s_sum = sem("groups_added")
        s_prep, s_grp, s_added = sem("groups_prepared"), sem("groups_multiplied"), sem("all_groups_added")
        s_g = [sem(f"rows_gathered_{i}") for i in range(SLOTS)]
        s_seen = {e: sem(f"waits_passed_{e}") for e in ("pool", "pe", "act", "dve", "sp")}
        s_xs, s_xTp, s_xT, s_kvp, s_vc = sem("xn_staged"), sem("xn_transposed"), sem("xnT_copied"), sem("kv_multiplied"), sem("v_copied")
        s_sq, s_pr, s_sr, s_kn, s_dot = sem("kv_squared"), sem("norm_products"), sem("norm_roots"), sem("k_scaled"), sem("dots_summed")
        s_wc, s_dd, s_m1 = sem("kv_weights_centred"), sem("dots_copied"), sem("mixer_half")
        s_vh, s_m2, s_mx = sem("mixer_half_copied"), sem("mixer_whole"), sem("mixer_copied")
        s_ww, s_b1 = sem("gnn_weights_multiplied"), sem("gnn_weights_copied")
        m_x = [sem("m_x_loaded_0"), sem("m_x_loaded_1")]
        m_xT, m_p, m_done = sem("m_xnT_copied"), sem("m_multiplied"), sem("m_added")
        a_sum = sem("a_x1_plus_ln")
        a_ag, a_tp, a_T, a_hp, a_h, a_o, a_x1 = (sem("a_" + n) for n in ("scaled", "transposed", "copied", "hidden", "relu", "summed", "x1"))
        b_var, b_root, b_xn, b_tp, b_tc = (sem("b_" + n) for n in ("variances", "roots", "normalised", "transposed", "copied"))
        k_cnt, k_sum = sem("k_counted"), sem("k_summed")
        c_h, c_g, c_y, c_free, c_ot = (sem("c_" + n) for n in ("hidden", "gelu", "out", "bank_read", "tile_ready"))
        c_st = [sem(f"c_stored_{i}") for i in range(7)]

        def passed(eng, name):
            eng.sem_inc(s_seen[name], 1)

        def row(v):
            return v.rearrange("p o d -> p (o d)")

        MIX = (1, 6)
        MIX_READ = (3, 8)
        YB = (4, 5, 6, 4, 5, 6, 5)

        block = ctx.enter_context(nc.Block())
        xpart = NB - 1

        @block.sync
        def _(sp):
            sp.dma_start(srcI, src_d.rearrange("(p j) -> p j", p=EP)).then_inc(s_edges, 16)
            sp.dma_start(dstI, dst_d.rearrange("(p j) -> p j", p=EP)).then_inc(s_edges, 16)
            sp.dma_start(ew, ew_d.rearrange("(p j) -> p j", p=EP)).then_inc(s_edges, 16)
            sp.dma_start(X[:, 0:xpart, :], x_d[0:xpart * P, :].rearrange("(t p) d -> p t d", p=P)).then_inc(s_x, 16)
            sp.wait_ge(s_xpad, 1)
            sp.dma_start(X[0:LAST, xpart, :], x_d[xpart * P:N, :]).then_inc(s_x, 16)
            for t, a in ((wkv, "kvT"), (WT, "WT"), (W1, "L0_gnn_W1"), (W2, "L0_gnn_W2")):
                sp.dma_start(t[:, :, :], A[a].rearrange("(k p) n -> p k n", p=P)).then_inc(s_w, 16)
            with nc.allow_non_contiguous_dma(reason="a few hundred words of biases"):
                sp.dma_start(bc[:, :], A["L0_gnn_b"].rearrange("(k p) -> p k", p=P)).then_inc(s_w, 16)
                sp.dma_start(b1c[:, :], A["L0_gnn_b1"].rearrange("(k p) -> p k", p=P)).then_inc(s_w, 16)
                sp.dma_start(fb1[:, :], A["L0_ffn_b1"].rearrange("(k p) -> p k", p=P)).then_inc(s_w, 16)
            for t, a in ((b2o, A["L0_gnn_b2"]), (brow, A["L0_mix_b_out"]), (fb2, A["L0_ffn_b2"]),
                         (wr, A["L0_ffn_wr"].rearrange("d o -> (d o)")), (brc, A["L0_ffn_br"])):
                sp.dma_start(t[:, :], spread(a.rearrange("(o d) -> o d", o=1), 0, P)).then_inc(s_w, 16)
            sp.wait_ge(s_hm, 1)
            with nc.allow_non_contiguous_dma(reason="512 words"):
                sp.dma_start(hmap_d.rearrange("(p a) -> p a", p=P), hmI[:, :]).then_inc(s_hmd, 16)
            sp.wait_ge(s_hmd, 16)
            sp.dma_start(hrow[:, :], hmap_d.rearrange("(o a) -> o a", o=1)).then_inc(s_hrow, 16)
            def table(t, u):
                sp.wait_ge(s_yt, t + 1)
                passed(sp, "sp")
                sp.dma_start(y_d[ds(t * P, P), :], ys[:, u, :]).then_inc(s_y[u], 16)

            with sp.Fori(0, NB // 2) as i:
                for u in range(2):
                    table(2 * i + u, u)
            sp.wait_ge(s_yt, NB)
            sp.dma_start(y_d[(NB - 1) * P:NB * P, :], ys[:, 0, :]).then_inc(s_y[0], 16)
            sp.wait_ge(s_scd, 1)
            for r, to in enumerate((rec, rec1)):
                sp.dma_start(to.rearrange("p t r w -> p (t r w)"),
                             rec_d[r][0:SPARE, :].rearrange("(p t) w -> p (t w)", p=P)).then_inc(s_rec, 16)
            for t, a in ((wq, "wq"), (wo, "woT")):
                sp.dma_start(t, A[a].rearrange("(k p) n -> p k n", p=P)).then_inc(s_wq, 16)
            sp.wait_ge(s_mx, DK)
            with sp.Fori(0, NB // 2) as i:
                for u in range(2):
                    sp.wait_ge(m_done, 2 * i + u + 1)
                    passed(sp, "sp")
                    sp.dma_start(xin[:, u, :], x_d[ds((2 * i + u) * P, P), :]).then_inc(m_x[u], 16)
            sp.wait_ge(m_done, NB)
            sp.dma_start(xin[0:LAST, 0, :], x_d[xpart * P:N, :]).then_inc(m_x[0], 16)
            sp.wait_ge(s_added, 1)
            for t, a in ((w1s, "L0_ffn_w1"), (w2s, "L0_ffn_w2")):
                sp.dma_start(t, A[a].rearrange("(k p) n -> p k n", p=P)).then_inc(s_wf, 16)
            n7 = NB // 7
            with sp.Fori(0, n7 - 1) as i:
                for q in range(7):
                    sp.wait_ge(c_ot, 7 * i + q + 1)
                    passed(sp, "sp")
                    sp.dma_start(out[ds((7 * i + q) * P, P), :], ot[:, q, :]).then_inc(c_st[q], 16)
            for q in range(7):
                t = 7 * (n7 - 1) + q
                n = P if t < xpart else LAST
                sp.wait_ge(c_ot, t + 1)
                sp.dma_start(out[t * P:t * P + n, :], ot[0:n, q, :]).then_inc(c_st[q], 16)
            for q in range(7):
                sp.wait_ge(c_st[q], 16 * n7)

        @block.gpsimd
        def _(pool):
            pool.iota(iotaI[:, :], [[1, P]], base=0, channel_multiplier=0).then_inc(s_iota, 1)
            pool.iota(pidI[:, 0:1], [[1, 1]], base=0, channel_multiplier=1).then_inc(s_iota, 1)
            pool.iota(pidI[:, 1:], [[1, HI]], base=0, channel_multiplier=HI).then_inc(s_iota, 1)
            pool.wait_ge(s_zero, 1)
            for r in range(2):
                pool.dma_start(rec_d[r].rearrange("(p b) w -> p (b w)", p=P), zero).then_inc(s_scat[r], 16)
            pool.wait_ge(s_e, 1)
            with pool.Fori(0, NS // 2) as i:
                for u in range(2):
                    pool.wait_ge(s_o1, 2 * i + u + 1)
                    pool.wait_ge(s_cntp, 2 * i + u + 1)
                    passed(pool, "pool")
                    w = spread(wp[2][:, ds((2 * i + u) * SJ, SJ)].rearrange("p (o j) -> p o j", o=1), 1, NB)
                    pool.tensor_tensor(ohw[u][:, 2, :, :], oh1[u], w, ALU.mult).then_inc(s_ow, 1)
            pool.wait_ge(s_ridx, 1)

            def place(s, u, m):
                w = spread(wp[m][:, ds(s * SJ + u * HJ, HJ)].rearrange("p (o j) -> p o j", o=1), 1, SUB)
                return pool.tensor_tensor(mv[u][:, m, 1, :, :], sub1h[u], w, ALU.mult)

            def scatter(s, b, k):
                if k == 0:
                    pool.wait_ge(s_runc, s + 3)
                    pool.wait_ge(s_sidx, s + 1)
                pool.wait_ge(s_scat[k % 2], 16 * (HR * s + k // 2) + 16)
                passed(pool, "pool")
                pool.indirect_dma_start(rec_d[k % 2], bass.IndirectOffsetOnAxis(sidx[:, b, k:k + 1], 0),
                                        sbuf[:, b, k * B * RW:(k + 1) * B * RW], None).then_inc(s_scat[k % 2], 16)

            H2 = ceil_div(HI, 2)

            def mask(s, b):
                pool.wait_ge(s_scan, s + 1)
                pool.tensor_tensor(F3, F3, O2[b], ALU.mult).then_inc(s_rank, 1)

            def sort_step(s, b, scattering, more):
                for u in range(2):
                    pool.wait_ge(s_sub, 2 * s + u + 1)
                    pool.wait_ge(s_half, 2 * s + u + 1)
                    passed(pool, "pool")
                    for m in range(WD, WP):
                        ins = place(s, u, m)
                    ins.then_inc(s_wm, 1)
                    if scattering:
                        for k in range(u * H2, HI if u else H2):
                            scatter(s - 1, 1 - b, k)
                            if u == 0 and more and k == 0:
                                mask(s + 1, 1 - b)
                    elif u == 0:
                        mask(s + 1, 1 - b)

            mask(0, 0)
            sort_step(0, 0, False, True)
            with pool.Fori(0, NS // 2 - 1) as i:
                sort_step(2 * i + 1, 1, True, True)
                sort_step(2 * i + 2, 0, True, True)
            sort_step(NS - 1, 1, True, False)
            for k in range(HI):
                scatter(NS - 1, 1, k)
            for r in range(2):
                pool.wait_ge(s_scat[r], 16 * (HR * NS + 1))
            pool.sem_inc(s_scd, 1)
            pool.wait_ge(s_y[0], 16 * (NB // 2 + 1))
            pool.wait_ge(s_y[1], 16 * (NB // 2))
            with pool.Fori(0, NIT) as i:
                for u in range(UG):
                    pool.wait_ge(s_prep, UG * i + u + 1)
                    passed(pool, "pool")
                    for k in range(CH):
                        pool.indirect_dma_start(G[:, u % SLOTS, k, :], None, y_d,
                                                bass.IndirectOffsetOnAxis(gidx[:, u % SLOTS, k:k + 1], 0)
                                                ).then_inc(s_g[u % SLOTS], 16)
            pool.sem_inc(a_sum, 2)
            with pool.Fori(0, NT // 2) as i:
                for u in range(2):
                    pool.wait_ge(b_xn, 2 * i + u + 1)
                    passed(pool, "pool")
                    pool.tensor_tensor(row(X[:, ds(2 * i + u, 1), :]), x1s[:, u, :], xn2[:, u, :], ALU.add).then_inc(a_sum, 1)

        @block.scalar
        def _(act):
            act.sem_inc(s_cntc, 2)
            act.sem_inc(s_runc, 2)
            act.sem_inc(b_tc, 2)
            act.sem_inc(c_g, 4)
            act.sem_inc(c_free, 2)
            with act.Fori(0, NS // 2) as i:
                for u in range(2):
                    act.wait_ge(s_cntp, 2 * i + u + 3)
                    passed(act, "act")
                    act.copy(cnt[:, ds(2 * i + u, 1), :], bank[1 + u][:, 0:NB].rearrange("p (o h) -> p o h", o=1)).then_inc(s_cntc, 1)
            act.wait_ge(s_var, 1)
            act.activation(rstd[:, 0:NB], u49[:, :], ACT.Sqrt).then_inc(s_sqrt, 1)
            act.wait_ge(s_var, 2)
            act.activation(dinv[:, 0:NB], t49[:, :], ACT.Sqrt).then_inc(s_sqrt, 1)
            act.wait_ge(s_ln, 1)
            with act.Fori(0, NB) as t:
                xv = row(X[:, ds(t, 1), :])
                act.activation(xv, xv, ACT.Identity, bias=nmr[:, ds(t, 1)], scale=rstd[:, ds(t, 1)]).then_inc(s_xn, 1)
            act.wait_ge(s_dinv, 1)

            def tile(t, u):
                act.mul(ys[:, u, :], row(X[:, ds(t, 1), :]), dinv[:, ds(t, 1)]).then_inc(s_yt, 1)

            for u in range(2):
                tile(u, u)
            with act.Fori(1, NB // 2) as i:
                for u in range(2):
                    act.wait_ge(s_y[u], 16 * i)
                    passed(act, "act")
                    tile(2 * i + u, u)
            act.wait_ge(s_y[0], 16 * (NB // 2))
            tile(NB - 1, 0)

            def copy_runs(s, b, waiting):
                act.wait_ge(s_runs, s + 1)
                if waiting:
                    for r in range(2):
                        act.wait_ge(s_scat[r], 16 * (HR * (s - 1)) + 16)
                passed(act, "act")
                act.copy(sbuf[:, b, :].rearrange("p (s w) -> p w s", w=RW),
                         bank[3 + b][:, 0:SUB * RW].rearrange("p (w s) -> p w s", w=RW)).then_inc(s_runc, 1)

            def lanes(s, b):
                act.wait_ge(s_split, s + 1)
                act.wait_ge(s_half, 2 * s + 2)
                passed(act, "act")
                for j in range(HJ):
                    ins = act.activation(lt[:, j, :], iota[0:EP, :], ACT.Abs, bias=nlo[:, b, HJ + j:HJ + j + 1])
                ins.then_inc(s_dist, 1)
                act.wait_ge(s_dist, s + 1)
                act.activation(lo1h[1].rearrange("p l j -> p j l"), lt, ACT.Relu, bias=ones[0:EP, 0:1], scale=-1.0).then_inc(s_lo, 1)

            lanes(0, 0)
            copy_runs(0, 0, False)
            with act.Fori(0, NS // 2 - 1) as i:
                lanes(2 * i + 1, 1)
                copy_runs(2 * i + 1, 1, True)
                lanes(2 * i + 2, 0)
                copy_runs(2 * i + 2, 0, True)
            lanes(NS - 1, 1)
            copy_runs(NS - 1, 1, True)
            act.wait_ge(s_half, 2 * NS + 2)
            act.wait_ge(s_scd, 1)
            with act.Fori(NT // 2, NT) as t:
                act.mul(row(ACC[:, ds(t, 1), :]), row(X[:, ds(t, 1), :]), dinv[:, ds(t, 1)]).then_inc(s_acc, 1)
            act.wait_ge(s_rt, 2)
            for b in range(ceil_div(CT, 4)):
                n = min(4, CT - 4 * b)
                act.copy(recw.rearrange("p (c t) -> p t c", t=CT)[:, 4 * b:4 * b + n, :],
                         bank[4 + b][:, 0:n * P].rearrange("p (t c) -> p t c", t=n)).then_inc(s_rw, 1)
            act.wait_ge(s_acc, NT // 2 + 1)
            act.wait_ge(s_scd, 1)
            with act.Fori(0, NB) as t:
                act.wait_ge(s_xTp, t + 1)
                passed(act, "act")
                act.copy(xs.rearrange("p (o d) -> p o d", o=1), X[:, ds(t, 1), :]).then_inc(s_xs, 1)
                act.wait_ge(s_xTp, t + 2)
                act.wait_ge(s_kvp, t + 1)
                passed(act, "act")
                act.copy(xT, bank[0][:, 0:D])
                act.copy(X[:, ds(t, 1), :], bank[0][:, 0:D].rearrange("p (o d) -> p o d", o=1)).then_inc(s_xT, 1)
                act.wait_ge(s_kvp, t + 2)
                act.wait_ge(s_pr, t + 1)
                act.wait_ge(s_dot, t + 1)
                passed(act, "act")
                act.activation(kvsq[:, 0:GD], bank[1][:, :], ACT.Square)
                act.activation(kvsq[:, GD:KV], bank[0][:, :], ACT.Square).then_inc(s_sq, 1)
                act.copy(vs, bank[0][:, :]).then_inc(s_vc, 1)
                act.wait_ge(s_pr, t + 2)
                passed(act, "act")
                act.activation(rr[:, :], pr[:, :], ACT.Sqrt).then_inc(s_sr, 1)
            act.wait_ge(s_m1, 1)
            for j in range(PAIRS):
                act.copy(Vh[:, j, :], bank[j // 2][:, j % 2 * D:(j % 2 + 1) * D]).then_inc(s_vh, 1)
            act.wait_ge(s_m2, 1)
            for m in range(DK):
                act.mul(Mx[:, m, :], bank[2][:, m * D:(m + 1) * D], 1.0 / N).then_inc(s_mx, 1)
            act.wait_ge(s_ww, 1)
            act.copy(WW[:, 0, :], bank[0][:, 0:D])
            act.copy(WW[:, 1, :], bank[1][:, 0:D])
            for m in range(DK):
                act.activation(b1c[:, m:m + 1], bank[1][:, D + m:D + m + 1], ACT.Identity, bias=b1c[:, m:m + 1]).then_inc(s_b1, 1)
            with act.Fori(0, NB // 2) as i:
                for u in range(2):
                    act.wait_ge(m_p, 2 * i + u + 1)
                    passed(act, "act")
                    act.copy(xTs[:, u:u + 1, :], X[:, ds(2 * i + u, 1), :]).then_inc(m_xT, 1)
            act.wait_ge(m_p, NB)
            act.copy(xTs[:, 0, :], X[:, xpart, :]).then_inc(m_xT, 1)
            act.wait_ge(s_added, 1)

            def scale(i):
                for u in range(2):
                    t = 2 * i + u
                    act.mul(ag[:, u, :], row(ACC[:, ds(t, 1), :]), dinv[:, ds(t, 1)]).then_inc(a_ag, 1)

            def aggregate(i):
                for u in range(2):
                    act.wait_ge(a_tp, 2 * i + u + 1)
                    act.copy(agT[:, u, :], bank[u][:, 0:D]).then_inc(a_T, 1)

            def hidden(i):
                for u in range(2):
                    act.wait_ge(a_hp, 2 * i + u + 1)
                    act.wait_ge(a_o, 2 * i + u + 1)
                    passed(act, "act")
                    for m in range(DK):
                        ins = act.activation(hT[:, u, m * P:(m + 1) * P], bank[2 + u][:, m * P:(m + 1) * P], ACT.Relu,
                                             bias=b1c[:, m:m + 1])
                    ins.then_inc(a_h, 1)

            def transposed(i):
                for u in range(2):
                    act.wait_ge(b_tp, 2 * i + u + 3)
                    passed(act, "act")
                    act.copy(ACC[:, ds(2 * i + u, 1), :], bank[6 + u][:, 0:D].rearrange("p (o d) -> p o d", o=1)).then_inc(b_tc, 1)

            def root(i):
                act.wait_ge(b_var, i + 1)
                act.activation(r2v[:, :], v2[:, :], ACT.Sqrt).then_inc(b_root, 1)

            n2 = NT // 2
            scale(0)
            aggregate(0)
            scale(1)
            hidden(0)
            aggregate(1)
            scale(2)
            root(0)
            with act.Fori(1, n2 - 2) as i:
                hidden(i)
                aggregate(i + 1)
                scale(i + 2)
                transposed(i - 1)
                root(i)
            hidden(n2 - 2)
            aggregate(n2 - 1)
            transposed(n2 - 3)
            root(n2 - 2)
            hidden(n2 - 1)
            transposed(n2 - 2)
            root(n2 - 1)
            transposed(n2 - 1)

            def ffn(i, first):
                for q, (nt, H1) in enumerate(((4, H1a), (3, H1b))):
                    for f in range(FB):
                        act.wait_ge(c_h, (2 * i + q) * FB + f + 1)
                        passed(act, "act")
                        act.activation(H1[:, f, :], bank[f % 4][:, 0:nt * P], ACT.Gelu_apprx_tanh,
                                       bias=fb1[:, f:f + 1]).then_inc(c_g, 1)
                    for a in range(4 * q, 4 * q + nt):
                        act.wait_ge(c_y, 7 * i + a + 1)
                        if not first:
                            act.wait_ge(c_st[a], 16 * i)
                        passed(act, "act")
                        act.copy(ot[:, a, :], bank[YB[a]][:, 0:D]).then_inc(c_free, 1)

            act.wait_ge(b_xn, NT)
            ffn(0, True)
            with act.Fori(1, NB // 7) as i:
                ffn(i, False)

        @block.tensor
        def _(pe):
            pe.sem_inc(s_cntp, 2)
            pe.sem_inc(s_h1, 2)
            pe.sem_inc(s_half, 2)
            kvz = spread(ones[:, 0:1], 1, WP * NB)
            pe.sem_inc(s_grp, 1)
            pe.sem_inc(s_xTp, 1)
            pe.sem_inc(s_kvp, 1)
            pe.sem_inc(s_dot, 1)
            pe.sem_inc(a_o, 2)
            pe.sem_inc(m_p, 2)
            pe.sem_inc(b_tp, 2)
            pe.wait_ge(s_const, 1)
            pe.matmul(bank[0][:, 0:WP * NB], zcol[:, :], kvz, start=True, stop=False, skip_group_check=True)
            with pe.Fori(0, NS // 2) as i:
                for u in range(2):
                    s = 2 * i + u
                    pe.wait_ge(s_o1, s + 1)
                    pe.wait_ge(s_cntc, s + 1)
                    for j in range(SJ):
                        pe.matmul(bank[1 + u][:, 0:NB], onesb[0:EP, :], oh1[u][:, :, j], start=(j == 0), stop=(j == SJ - 1))
                    pe.wait_ge(s_ow, 2 * s + 2)
                    for q in range(2):
                        pe.wait_ge(s_rl, 2 * s + q + 1)
                        for j in range(HJ):
                            ins = pe.matmul(bank[0][:, 0:WP * NB].rearrange("p (m h) -> p m h", m=WP), rl1h[q][:, :, j],
                                            ohw[u][:, :, :, q * HJ + j], start=False, stop=False, skip_group_check=True)
                        ins.then_inc(s_h1, 1)
                    pe.sem_inc(s_seen["pe"], 1)
                    pe.wait_ge(s_h1, 2 * s + 4)
                    pe.sem_inc(s_cntp, 1)
            pe.matmul(bank[0][:, 0:WP * NB], zcol[:, :], kvz, start=False, stop=True, skip_group_check=True).then_inc(s_deg, 1)

            def cross(s, b):
                pe.wait_ge(s_o2, s + 1)
                for q in range(2):
                    for j in range(SJ):
                        ins = pe.matmul(bank[2][0:EP, q * NB:(q + 1) * NB], befb[0:EP, q, 0:EP], O2[b][:, :, j],
                                        start=(j == 0), stop=(j == SJ - 1))
                ins.then_inc(s_cross, 1)

            def sort_runs(s, b, more):
                pe.wait_ge(s_runc, s + 1)
                for u in range(2):
                    pe.wait_ge(s_key, 2 * s + u + 1)
                    pe.wait_ge(s_wm, 2 * s + u + 1)
                    if u == 1:
                        pe.wait_ge(s_lo, s + 1)
                    for j in range(HJ):
                        for m in range(WP):
                            ins = pe.matmul(bank[3 + b][:, 0:SUB * RW].rearrange("p (w s) -> p w s", w=RW), lo1h[u][:, :, j],
                                            mv[u][:, m, :, :, j],
                                            start=(u == 0 and j == 0 and m == 0), stop=(u == 1 and j == HJ - 1 and m == WP - 1))
                    ins.then_inc(s_half, 1)
                    if u == 0 and more:
                        cross(s + 2, b)
                pe.wait_ge(s_half, 2 * s + 4)
                pe.sem_inc(s_runs, 1)

            cross(0, 0)
            cross(1, 1)
            with pe.Fori(0, NS // 2 - 1) as i:
                sort_runs(2 * i, 0, True)
                sort_runs(2 * i + 1, 1, True)
            sort_runs(NS - 2, 0, False)
            sort_runs(NS - 1, 1, False)
            pe.wait_ge(s_merged, 1)
            pe.wait_ge(s_runc, NS + 2)
            for w in range(RW):
                for t in range(CT):
                    ins = pe.transpose(bank[4 * w + t // 4][:, t % 4 * P:(t % 4 + 1) * P], rec[:, t, :, w], ident[:, :])
                ins.then_inc(s_rt, 1)
            pe.wait_ge(s_rk, ceil_div(CT, 4))
            pe.wait_ge(s_rw, ceil_div(CT, 4))
            pe.wait_ge(s_w, 16 * 12)
            pe.wait_ge(s_wc, 1)

            def group(g, u, use):
                pe.wait_ge(s_g[u % SLOTS], 16 * CH * use)
                pe.wait_ge(s_prep, g + 1)
                pe.wait_ge(s_sum, g + 1)
                for k in range(CH):
                    ins = pe.matmul(bank[3 + u % SB][:, 0:D], OH[:, u % SLOTS, k, :], G[:, u % SLOTS, k, :],
                                    start=(k == 0), stop=(k == CH - 1))
                ins.then_inc(s_grp, 1)

            def kv_transpose(t):
                pe.wait_ge(s_xs, t + 1)
                for m in range(DK):
                    ins = pe.transpose(bank[0][:, m * P:(m + 1) * P], xs[:, m * P:(m + 1) * P], ident[:, :])
                ins.then_inc(s_xTp, 1)

            def kv_multiply(t):
                pe.wait_ge(s_xT, t + 1)
                pe.wait_ge(s_kn, t + 1)
                for b, o in ((1, 0), (0, GD)):
                    for k in range(DK):
                        ins = pe.matmul(bank[b][:, :], xT[:, k * P:(k + 1) * P], wkv[:, k, o:o + GD], start=(k == 0), stop=(k == DK - 1))
                ins.then_inc(s_kvp, 1)

            def kv_dots(t):
                pe.wait_ge(s_kn, t + 2)
                pe.wait_ge(s_vc, t + 1)
                for j in range(PAIRS):
                    ins = pe.matmul(bank[2][:, j * P:(j + 1) * P], kn[:, j * P:(j + 1) * P], vs[:, j * P:(j + 1) * P],
                                    start=False, stop=False, skip_group_check=True)
                ins.then_inc(s_dot, 1)

            pe.matmul(bank[2][:, 0:GD], zcol[:, :], wkv[:, 0, 0:GD], start=True, stop=False, skip_group_check=True)
            with pe.Fori(0, NB) as i:
                kv_transpose(i)
                for u in range(UG):
                    group(UG * i + u, u, 2 * i + u // SLOTS + 1)
                    if u == UG // 10:
                        kv_multiply(i)
                    if u == UG * 4 // 5:
                        kv_dots(i)
            pe.matmul(bank[2][:, 0:GD], zcol[:, :], wkv[:, 0, 0:GD], start=False, stop=True, skip_group_check=True).then_inc(s_dot, 1)
            pe.wait_ge(s_dd, 1)
            pe.wait_ge(s_wq, 32)
            for j in range(PAIRS):
                ins = pe.matmul(bank[j // 2][:, j % 2 * D:(j % 2 + 1) * D], dots[:, j, :], wq[:, j, :], start=True, stop=True)
            ins.then_inc(s_m1, 1)
            pe.wait_ge(s_vh, PAIRS)
            for m in range(DK):
                for j in range(PAIRS):
                    ins = pe.matmul(bank[2][:, m * D:(m + 1) * D], Vh[:, j, m * P:(m + 1) * P], wo[:, j, :],
                                    start=(j == 0), stop=(j == PAIRS - 1))
            ins.then_inc(s_m2, 1)
            for kb in range(DK):
                for k in range(DK):
                    pe.matmul(bank[kb][:, 0:D], WT[:, k, kb * P:(kb + 1) * P], W1[:, k, :], start=(k == 0), stop=(k == DK - 1))
            for m in range(DK):
                for k in range(DK):
                    ins = pe.matmul(bank[1][:, D + m:D + m + 1], W1[:, k, m * P:(m + 1) * P], bc[:, k:k + 1],
                                    start=(k == 0), stop=(k == DK - 1))
            ins.then_inc(s_ww, 1)

            def mix(t, b):
                pe.wait_ge(m_xT, t + 1)
                pe.wait_ge(m_done, t + 1)
                for k in range(DK):
                    ins = pe.matmul(bank[b][:, 0:D], xTs[:, b, k * P:(k + 1) * P], Mx[:, k, :], start=(k == 0), stop=(k == DK - 1))
                ins.then_inc(m_p, 1)

            with pe.Fori(0, NB // 2) as i:
                for u in range(UG):
                    group(UG * (i + NB) + u, u, 2 * (i + NB) + u // SLOTS + 1)
                    if u in MIX:
                        b = MIX.index(u)
                        if b == 0:
                            pe.wait_ge(s_b1, DK)
                        mix(2 * i + b, b)
            mix(NB - 1, 0)
            with pe.Fori(NB + NB // 2, NIT) as i:
                for u in range(UG):
                    group(UG * i + u, u, 2 * i + u // SLOTS + 1)
            pe.wait_ge(s_added, 1)

            def aggregate(i):
                for u in range(2):
                    pe.wait_ge(a_ag, 2 * i + u + 1)
                    for m in range(DK):
                        ins = pe.transpose(bank[u][:, m * P:(m + 1) * P], ag[:, u, m * P:(m + 1) * P], ident[:, :])
                    ins.then_inc(a_tp, 1)

            def hidden(i):
                for u in range(2):
                    pe.wait_ge(a_T, 2 * i + u + 1)
                    for m in range(DK):
                        for k in range(DK):
                            ins = pe.matmul(bank[2 + u][:, m * P:(m + 1) * P], WW[:, k, m * P:(m + 1) * P],
                                            agT[:, u, k * P:(k + 1) * P], start=(k == 0), stop=(k == DK - 1))
                    ins.then_inc(a_hp, 1)

            def rows(i):
                for u in range(2):
                    pe.wait_ge(a_h, 2 * i + u + 1)
                    pe.wait_ge(a_x1, 2 * i + u + 1)
                    for k in range(DK):
                        ins = pe.matmul(bank[4 + u][:, 0:D], hT[:, u, k * P:(k + 1) * P], W2[:, k, :], start=(k == 0), stop=(k == DK - 1))
                    ins.then_inc(a_o, 1)

            def transposes(i):
                for u in range(2):
                    pe.wait_ge(b_xn, 2 * i + u + 1)
                    pe.wait_ge(b_tc, 2 * i + u + 1)
                    for m in range(DK):
                        ins = pe.transpose(bank[6 + u][:, m * P:(m + 1) * P], xn2[:, u, m * P:(m + 1) * P], ident[:, :])
                    ins.then_inc(b_tp, 1)

            n2 = NT // 2
            aggregate(0)
            hidden(0)
            aggregate(1)
            rows(0)
            with pe.Fori(1, n2 - 1) as i:
                hidden(i)
                aggregate(i + 1)
                rows(i)
                transposes(i - 1)
            hidden(n2 - 1)
            rows(n2 - 1)
            transposes(n2 - 2)
            transposes(n2 - 1)
            pe.wait_ge(b_tc, NT + 2)
            pe.wait_ge(s_wf, 32)

            def count(n):
                pe.wait_ge(k_cnt, n + 1)
                pe.matmul(bank[7][:, 0:SR], ones[:, :], cnts[:, :], start=True, stop=True).then_inc(k_sum, 1)

            def ffn(i, first):
                for q, (nt, H1) in enumerate(((4, H1a), (3, H1b))):
                    for f in range(FB):
                        pe.wait_ge(c_g, (2 * i + q) * FB + f + 1)
                        for k in range(DK):
                            ins = pe.matmul(bank[f % 4][:, 0:nt * P].rearrange("p (t n) -> p t n", n=P), w1s[:, k, f * P:(f + 1) * P],
                                            ACC[:, ds(7 * i + 4 * q, nt), k * P:(k + 1) * P], start=(k == 0), stop=(k == DK - 1))
                        ins.then_inc(c_h, 1)
                        if first:
                            count(q * FB + f)
                    pe.wait_ge(c_g, (2 * i + q + 1) * FB + 4)
                    for a in range(4 * q, 4 * q + nt):
                        pe.wait_ge(c_free, 7 * i + a + 1)
                        for f in range(FB):
                            ins = pe.matmul(bank[YB[a]][:, 0:D], H1[:, f, (a - 4 * q) * P:(a - 4 * q + 1) * P], w2s[:, f, :],
                                            start=(f == 0), stop=(f == FB - 1))
                        ins.then_inc(c_y, 1)
                if first:
                    ties(2 * SD)

            def ties(n):
                pe.wait_ge(k_cnt, n + 1)
                pe.matmul(bank[7][:, 0:1], ones[:, :], cnts[:, 0:1], start=True, stop=True)
                pe.matmul(bank[7][:, P:P + NB], strict[:, :], eqm[:, :], start=True, stop=True)
                pe.matmul(bank[7][:, 2 * P:2 * P + NB], ones[:, :], eqm[:, :], start=True, stop=True).then_inc(k_sum, 1)

            ffn(0, True)
            with pe.Fori(1, NB // 7) as i:
                ffn(i, False)

        @block.vector
        def _(dve):
            c = Chain(dve, s_dve)
            dve.memset(X[:, xpart:NT, :], 0.0).then_inc(s_xpad, 1)
            dve.memset(zero, 0.0).then_inc(s_zero, 1)
            dve.memset(ones[:, :], 1.0)
            dve.memset(zcol[:, :], 0.0)
            dve.memset(onesb[:, :], 1.0)
            dve.memset(dinv[:, NB:NT], 0.0)
            dve.memset(mvar[:, NB:NT, :], 0.0)
            dve.memset(rstd[:, NB:NT], 0.0)
            dve.memset(A2[:, :, 0:1], 0.0)
            dve.sem_inc(a_x1, 2)
            dve.sem_inc(m_done, 2)
            dve.sem_inc(s_pr, 1)
            dve.sem_inc(s_sum, SB)
            dve.sem_inc(s_kn, 1)
            dve.wait_ge(s_iota, 3)
            c.link(dve.tensor_copy(iota[:, :], iotaI[:, :]))
            c.link(dve.tensor_copy(pid[:, :], pidI[:, :]))
            c.link(dve.tensor_scalar(ident[:, :], iota[:, :], pid[:, 0:1], None, ALU.is_equal))
            c.link(dve.tensor_scalar(strict[:, :], iota[:, :], pid[:, 0:1], None, ALU.is_gt))
            c.link(dve.tensor_scalar(befb[:, 0, :], iota[:, :], pid[:, 0:1], None, ALU.is_gt))
            c.link(dve.tensor_scalar(befb[:, 1, :], iota[:, :], pid[:, 0:1], None, ALU.is_ge))
            c.link(dve.tensor_copy(iotab[:, :], iota[:, :]))
            c.link(dve.tensor_copy(iotaL, spread(iotab[0:EP, :].rearrange("p (h o) -> p h o", o=1), 2, SJ)))
            for i in range(SD):
                c.mark(dve.tensor_scalar(steps[:, i, :], iota[:, 0:SR], float(SR ** (SD - 1 - i)), None, ALU.mult))
            dve.sem_inc(s_const, 1)
            dve.wait_ge(s_edges, 48)
            c.link(dve.tensor_scalar(tmpI, srcI, 7, None, ALU.arith_shift_right))
            c.link(dve.tensor_copy(hfb, tmpI))
            c.link(dve.tensor_scalar(tmpI, srcI, P - 1, None, ALU.bitwise_and))
            c.link(dve.tensor_copy(rlob, tmpI))
            c.link(dve.tensor_scalar(tmpI, dstI, 7, 14, ALU.arith_shift_right, ALU.logical_shift_left))
            c.link(dve.tensor_copy(keyp[0], tmpI))
            c.link(dve.tensor_scalar(tmpI, dstI, P - 1, 7, ALU.bitwise_and, ALU.logical_shift_left))
            c.link(dve.tensor_copy(keyp[1], tmpI))
            c.link(dve.tensor_copy(wp[0], ew))
            c.link(dve.tensor_tensor(ew, ew, wp[0], ALU.subtract))
            c.link(dve.tensor_copy(wp[1], ew))
            c.link(dve.tensor_tensor(ew, ew, wp[1], ALU.subtract))
            c.link(dve.tensor_copy(wp[2], ew))
            dve.sem_inc(s_e, 1)

            def row_stats(src):
                with dve.Fori(0, NB) as t:
                    c.enter(t, 1)
                    c.mark(dve.bn_stats(row(st[:, ds(t, 1), :]), row(src[:, ds(t, 1), :])))
                c.leave(NB)
                c.wait()
                for t in range(NB):
                    ins = dve.bn_aggr(mvar[:, t, :], st[:, t, :])
                c.link(ins)
                c.link(dve.tensor_scalar(u49[:, :], mvar[:, 0:NB, 1], EPS, None, ALU.add))

            def inverse_root(r, v, tmp):
                c.link(dve.reciprocal(r, r))
                c.link(dve.tensor_tensor(tmp, r, r, ALU.mult))
                c.link(dve.tensor_tensor(tmp, tmp, v, ALU.mult))
                c.link(dve.tensor_scalar(tmp, tmp, -0.5, 1.5, ALU.mult, ALU.add))
                c.link(dve.tensor_tensor(r, r, tmp, ALU.mult))

            def by_edge(v, at, n, classes):
                return spread(v[:, ds(at, n)].rearrange("p (o j) -> p o j", o=1), 1, classes)

            with dve.Fori(0, NS // 2) as i:
                for u in range(2):
                    s = 2 * i + u
                    dve.wait_ge(s_cntp, s + 1)
                    dve.tensor_tensor(oh1[u], by_edge(hfb, s * SJ, SJ, NB), iotaL[:, 0:NB, :], ALU.is_equal).then_inc(s_o1, 1)
                    for q in range(2):
                        dve.wait_ge(s_h1, 2 * s + q + 1)
                        dve.tensor_tensor(rl1h[q], by_edge(rlob, s * SJ + q * HJ, HJ, P), iotaL[:, :, 0:HJ], ALU.is_equal).then_inc(s_rl, 1)
                        if q == 0:
                            dve.wait_ge(s_o1, s + 1)
                            for m in range(2):
                                ins = dve.tensor_tensor(ohw[u][:, m, :, :], oh1[u], by_edge(wp[m], s * SJ, SJ, NB), ALU.mult)
                            ins.then_inc(s_ow, 1)
            dve.wait_ge(s_x, 32)
            row_stats(X)
            dve.sem_inc(s_var, 1)
            dve.wait_ge(s_sqrt, 1)
            inverse_root(rstd[:, 0:NB], u49[:, :], v49[:, :])
            c.link(dve.scalar_tensor_tensor(nmr[:, :], mvar[:, 0:NB, 0], -1.0, rstd[:, 0:NB], ALU.mult, ALU.mult))
            dve.sem_inc(s_ln, 1)
            dve.wait_ge(s_deg, 1)
            c.link(dve.tensor_reduce(u49[:, :], bank[0][:, 0:WP * NB].rearrange("p (m h) -> p h m", m=WP), AX.X, ALU.add))
            c.link(dve.tensor_scalar(u49[:, :], u49[:, :], 1.0, None, ALU.add))
            c.link(dve.tensor_scalar(sel[:, :], u49[:, :], 0.0, None, ALU.is_gt))
            c.link(dve.tensor_scalar(t49[:, :], u49[:, :], 1e-30, None, ALU.max))
            dve.sem_inc(s_var, 1)
            dve.wait_ge(s_cntc, NS + 2)
            dve.wait_ge(s_ow, 2 * NS)
            for r in range(2):
                dve.wait_ge(s_scat[r], 16)
            flat = cnt.rearrange("p s h -> p (s h)")

            def ceil_shift(outf, tmp_i, inf, n):
                c.link(dve.tensor_scalar(tmp_i, inf, float(2 ** n - 1), None, ALU.add))
                c.link(dve.tensor_scalar(tmp_i, tmp_i, n, None, ALU.arith_shift_right))
                c.link(dve.tensor_copy(outf, tmp_i))

            def restart(major):
                c.link(dve.memset(keep, 1.0))
                c.link(dve.memset(keep.rearrange("p (a b) -> p a b", a=major)[:, :, 0:1], 0.0))

            ceil_shift(pcf, inc.bitcast(I32), flat, BL)
            pc3 = pcf.rearrange("p (s h) -> p s h", s=NS)
            restart(NS)
            c.link(dve.tensor_tensor_scan(inc, keep, pcf, 0.0, ALU.mult, ALU.add))
            inc3 = inc.rearrange("p (s h) -> p s h", s=NS)
            c.link(dve.tensor_tensor(lbx[:, :, 0:NB], inc3, pc3, ALU.subtract))
            c.link(dve.tensor_copy(lbx[:, :, NB:NB + 1], inc3[:, :, NB - 1:NB]))
            c.link(dve.tensor_copy(pcT, pc3.rearrange("p s h -> p h s")))
            restart(NB)
            c.link(dve.tensor_tensor_scan(inc, keep, pcT.rearrange("p h s -> p (h s)"), 0.0, ALU.mult, ALU.add))
            incT = inc.rearrange("p (h s) -> p h s", s=NS)
            ceil_shift(tpf[:, :], v49[:, :].bitcast(I32), incT[:, :, NS - 1], BPG.bit_length() - 1)
            c.link(dve.tensor_tensor_scan(ginc[:, :], ones[:, 0:NB], tpf[:, :], 0.0, ALU.mult, ALU.add))
            c.link(dve.tensor_tensor(tpf[:, :], ginc[:, :], tpf[:, :], ALU.subtract))
            c.link(dve.tensor_scalar(tpf[:, :], tpf[:, :], float(BPG), None, ALU.mult))
            c.link(dve.tensor_tensor(incT, incT, pcT, ALU.subtract))
            c.link(dve.tensor_tensor(incT, incT, spread(tpf[:, :].rearrange("p (h o) -> p h o", o=1), 2, NS), ALU.add))
            c.link(dve.tensor_tensor(big[:, :, 0:NB], incT.rearrange("p h s -> p s h"), lbx[:, :, 0:NB], ALU.subtract))
            c.link(dve.memset(big[:, :, NB:NB + 1], float(SPARE)))
            c.link(dve.tensor_copy(dlt[:, :, 0:1], big[:, :, 0:1]))
            c.link(dve.tensor_tensor(dlt[:, :, 1:NB + 1], big[:, :, 1:NB + 1], big[:, :, 0:NB], ALU.subtract))
            for k in range(HI):
                c.link(dve.scalar_tensor_tensor(big, lbx, pid[:, 1 + k:2 + k], dlt, ALU.is_le, ALU.mult))
                c.link(dve.tensor_reduce(ridxf[:, :], big, AX.X, ALU.add))
                c.link(dve.tensor_scalar(ridx[:, :, k], ridxf[:, :], pid[:, 1 + k:2 + k], None, ALU.add))
            for a in range(HG):
                c.link(dve.tensor_scalar(hm[:, a:a + 1], pid[:, 0:1], float(HG), float(a), ALU.mult, ALU.add))
            for a in range(HG):
                c.link(dve.tensor_scalar(hm49[:, a, :], ginc[:, :], hm[:, a:a + 1], None, ALU.is_le))
            c.link(dve.tensor_reduce(hm[:, :], hm49[:, :, :], AX.X, ALU.add))
            hp = hm[:, :].rearrange("p (a k) -> p a k", k=PK)
            for k in range(PK - 1, 0, -1):
                c.link(dve.scalar_tensor_tensor(hp[:, :, k - 1], hp[:, :, k], 64.0, hp[:, :, k - 1], ALU.mult, ALU.add))
            c.link(dve.tensor_copy(hmI[:, :], hp[:, :, 0]))
            dve.sem_inc(s_hm, 1)
            dve.wait_ge(s_sqrt, 2)
            inverse_root(dinv[:, 0:NB], t49[:, :], u49[:, :])
            c.link(dve.tensor_tensor(dinv[:, 0:NB], dinv[:, 0:NB], sel[:, :], ALU.mult))
            dve.wait_ge(s_xn, NB)
            dve.sem_inc(s_dinv, 1)
            c.link(dve.tensor_scalar(lbx, lbx, float(B), -1.0, ALU.mult, ALU.add))
            c.link(dve.memset(Z, 0.0))
            dve.sem_inc(s_ridx, 1)

            def rank_onehots(s, b):
                dve.tensor_tensor(O2[b], by_edge(hfb, s * SJ, SJ, NB), iotaL[:, 0:NB, :], ALU.is_equal).then_inc(s_o2, 1)

            def rank_scan(s, b):
                dve.wait_ge(s_cross, s + 1)
                l2 = spread(lbx[0:EP, ds(s, 1), 0:NB], 1, 2)
                c.link(dve.tensor_tensor(A2[:, :, 1:], bank[2][0:EP, 0:2 * NB].rearrange("p (q h) -> p q h", q=2), l2, ALU.add))
                c.link(dve.tensor_tensor(Z[:, :, 0], A2[:, 0, 1:], A2[:, 1, 0:NB], ALU.subtract))
                dve.tensor_tensor_scan(F3.rearrange("p h j -> p (h j)"), Z.rearrange("p h j -> p (h j)"),
                                       O2[b].rearrange("p h j -> p (h j)"), 0.0, ALU.add, ALU.add).then_inc(s_scan, 1)

            def rank_split(s, b, waiting=True):
                dve.wait_ge(s_rank, s + 1)
                if waiting:
                    dve.wait_ge(s_lo, s - 1)
                c.link(dve.tensor_reduce(posf[:, :], F3.rearrange("p h j -> p j h"), AX.X, ALU.add))
                c.link(dve.tensor_scalar(posd[:, :], posf[:, :], 0.5 - SUB / 2, 1.0 / SUB, ALU.add, ALU.mult))
                c.link(dve.tensor_scalar(lob[:, :], posd[:, :], ROUND, -ROUND, ALU.add, ALU.add))
                dve.tensor_scalar(nlo[:, b, :], lob[:, :], -1.0, None, ALU.mult).then_inc(s_split, 1)
                c.link(dve.scalar_tensor_tensor(subb[:, :], lob[:, :], -float(SUB), posf[:, :], ALU.mult, ALU.add))

            def place_runs(s, b, more, waiting=True):
                for u in range(2):
                    dve.wait_ge(s_half, 2 * s + u + 1)
                    sv = spread(subb[:, u * HJ:(u + 1) * HJ].rearrange("p (o j) -> p o j", o=1), 1, SUB)
                    dve.tensor_tensor(sub1h[u], sv, iotaL[:, 0:SUB, 0:HJ], ALU.is_equal).then_inc(s_sub, 1)
                    if u == 0:
                        lv = spread(lob[:, 0:HJ].rearrange("p (o j) -> p o j", o=1), 1, P)
                        dve.tensor_tensor(lo1h[0], lv, iotaL[:, :, 0:HJ], ALU.is_equal)
                    dve.wait_ge(s_sub, 2 * s + u + 1)
                    at = s * SJ + u * HJ
                    for m in range(WP):
                        dve.tensor_tensor(mv[u][:, m, 0, :, :], sub1h[u], by_edge(keyp[m], at, HJ, SUB), ALU.mult)
                    for m in range(WD):
                        ins = dve.tensor_tensor(mv[u][:, m, 1, :, :], sub1h[u], by_edge(wp[m], at, HJ, SUB), ALU.mult)
                    ins.then_inc(s_key, 1)
                    if u == 0 and more > 0:
                        rank_scan(s + 1, 1 - b)
                    if u == 0 and more > 1:
                        rank_onehots(s + 2, b)
                    if u == 1:
                        if waiting:
                            for r in range(2):
                                dve.wait_ge(s_scat[r], 16 * (HR * (s - 1)) + 16)
                        passed(dve, "dve")
                        dve.tensor_copy(sidx[:, b:b + 1, :], ridx[:, ds(s, 1), :]).then_inc(s_sidx, 1)
                if more > 0:
                    dve.wait_ge(s_key, 2 * s + 2)
                    rank_split(s + 1, 1 - b, waiting)

            rank_onehots(0, 0)
            rank_scan(0, 0)
            rank_onehots(1, 1)
            rank_split(0, 0, False)
            place_runs(0, 0, 2, False)
            with dve.Fori(0, NS // 2 - 2) as i:
                c.enter(i, 12)
                place_runs(2 * i + 1, 1, 2)
                place_runs(2 * i + 2, 0, 2)
            c.leave(NS // 2 - 2)
            place_runs(NS - 3, 1, 2)
            place_runs(NS - 2, 0, 1)
            place_runs(NS - 1, 1, 0)
            dve.wait_ge(s_half, 2 * NS + 2)
            dve.wait_ge(s_wm, 2 * NS)
            passed(dve, "dve")
            with dve.Fori(0, NT // 2) as t:
                c.enter(t, 1)
                c.mark(dve.tensor_scalar(row(ACC[:, ds(t, 1), :]), row(X[:, ds(t, 1), :]), dinv[:, ds(t, 1)], None, ALU.mult))
            c.leave(NT // 2)
            c.wait()
            dve.sem_inc(s_acc, 1)
            dve.wait_ge(s_rec, 32)
            recf, rec1f = (v.rearrange("p t r w -> p (t r w)") for v in (rec, rec1))
            dve.tensor_tensor(recf, recf, rec1f, ALU.add).then_inc(s_merged, 1)
            dve.wait_ge(s_w, 16 * 12)
            w3 = kvf.rearrange("p (h w) -> p h w", w=HW)
            wm = wmean[:, :]
            c.link(dve.tensor_reduce(wm, w3, AX.X, ALU.add))
            c.link(dve.tensor_scalar(wm, wm, 1.0 / HW, None, ALU.mult))
            c.link(dve.tensor_tensor(w3, w3, spread(wm.rearrange("p (h o) -> p h o", o=1), 2, HW), ALU.subtract))
            dve.sem_inc(s_wc, 1)
            dve.wait_ge(s_rt, 1)
            for b in range(ceil_div(CT, 4)):
                n = min(4, CT - 4 * b)
                ins = dve.tensor_copy(cidxI.rearrange("p (c t) -> p t c", t=CT)[:, 4 * b:4 * b + n, :],
                                      bank[b][:, 0:n * P].rearrange("p (t c) -> p t c", t=n))
                ins.then_inc(s_rk, 1)
            dve.wait_ge(s_rk, ceil_div(CT, 4))
            c.link(dve.tensor_scalar(rloI, cidxI, P - 1, None, ALU.bitwise_and))
            c.link(dve.tensor_copy(rlo, rloI))
            c.link(dve.tensor_scalar(cidxI, cidxI, 7, None, ALU.arith_shift_right))
            dve.wait_ge(s_hrow, 16)
            dve.wait_ge(s_rw, ceil_div(CT, 4))
            dve.wait_ge(s_acc, NT // 2 + 1)
            dve.sem_inc(s_seen["dve"], 1)

            def prep(g, slot):
                for k in range(CH):
                    dve.tensor_scalar(OH[:, slot, k, :], iota[:, :], rlo[:, ds(CH * g + k, 1)],
                                      recw[:, ds(CH * g + k, 1)], ALU.is_equal, ALU.mult)
                dve.tensor_copy(gidx[:, slot, :], cidxI[:, ds(CH * g, CH)]).then_inc(s_prep, 1)

            def add_group(g, b, blocks, k):
                h = nc.s_assert_within((blocks >> (6 * k)) & 63, 0, NB,
                                       skip_runtime_bounds_check_because="the table holds blocks")
                a = row(ACC[:, ds(h, 1), :])
                dve.wait_ge(s_sum, g + SB)
                dve.wait_ge(s_grp, g + 2)
                dve.tensor_tensor(a, a, bank[3 + b][:, 0:D], ALU.add).then_inc(s_sum, 1)

            for g in range(SLOTS - 1):
                prep(g, g)

            def body(i, with_kv, n=None):
                for u in range(UG):
                    g = UG * i + u
                    dve.wait_ge(s_grp, g + 1)
                    prep(g + SLOTS - 1, (u + SLOTS - 1) % SLOTS)
                    if u % PK == 0:
                        blocks = dve.value_load(hrow[0:1, ds(UG // PK * i + u // PK, 1)], min_val=0, max_val=64 ** PK - 1)
                    add_group(g, u % SB, blocks, u % PK)
                    if n is not None and u in MIX_READ:
                        mixed(n, MIX_READ.index(u))
                    if with_kv and u == UG * 2 // 5:
                        dve.wait_ge(s_sq, i + 1)
                        c.link(dve.tensor_reduce(ss[:, :], kvsq.rearrange("p (h w) -> p h w", w=HW), AX.X, ALU.add))
                        c.link(dve.tensor_scalar(ss[:, :], ss[:, :], 1.0 / HW, EPS, ALU.mult, ALU.add))
                        c.link(dve.tensor_tensor(pr[:, :], ss[:, 0:HEADS], ss[:, HEADS:], ALU.mult))
                        dve.sem_inc(s_pr, 1)
                    if with_kv and u == UG * 3 // 5:
                        dve.wait_ge(s_sr, i + 1)
                        inverse_root(rr[:, :], pr[:, :], r2[:, :])
                        dve.wait_ge(s_dot, i + 1)
                        dve.tensor_tensor(kn.rearrange("p (h w) -> p h w", w=HW), bank[1][:, :].rearrange("p (h w) -> p h w", w=HW),
                                          spread(rr[:, :].rearrange("p (h o) -> p h o", o=1), 2, HW), ALU.mult).then_inc(s_kn, 1)

            with dve.Fori(0, NB) as i:
                c.enter(i, 8)
                body(i, True)
            c.leave(NB)
            dve.wait_ge(s_dot, NB + 2)
            c.link(dve.memset(dots, 0.0))
            for j in range(PAIRS):
                for q in range(2):
                    r0, r1 = q * HW, (q + 1) * HW
                    c.mark(dve.tensor_copy(dots[r0:r1, j, r0:r1], bank[2][r0:r1, j * P + r0:j * P + r1]))
            c.wait()
            dve.sem_inc(s_dd, 1)
            c.link(dve.tensor_tensor(b2o[:, :], b2o[:, :], brow[:, :], ALU.add))

            def mixed(n, b):
                t = 2 * n + b
                dve.wait_ge(m_x[b], 16 * n + 16)
                c.link(dve.tensor_tensor(xin[:, b, :], xin[:, b, :], b2o[:, :], ALU.add))
                dve.wait_ge(m_p, t + 3)
                passed(dve, "dve")
                dve.tensor_tensor(row(X[:, ds(t, 1), :]), bank[b][:, 0:D], xin[:, b, :], ALU.add).then_inc(m_done, 1)

            with dve.Fori(0, NB // 2) as i:
                c.enter(i, 2)
                body(i + NB, False, i)
            c.leave(NB // 2)
            mixed(NB // 2, 0)
            with dve.Fori(NB + NB // 2, NIT) as i:
                body(i, False)
            dve.wait_ge(s_sum, NG + SB)
            dve.wait_ge(m_done, NB + 2)
            dve.sem_inc(s_added, 1)
            with dve.Fori(0, NT // 2) as i:
                c.enter(i, 14)
                for u in range(2):
                    t = 2 * i + u
                    dve.wait_ge(a_o, t + 3)
                    dve.wait_ge(a_sum, t + 1)
                    passed(dve, "dve")
                    c.link(dve.tensor_tensor(x1s[:, u, :], bank[4 + u][:, 0:D], row(X[:, ds(t, 1), :]), ALU.add))
                    dve.sem_inc(a_x1, 1)
                    c.mark(dve.bn_stats(st2[:, u, :], x1s[:, u, :]))
                c.wait()
                passed(dve, "dve")
                for u in range(2):
                    c.mark(dve.bn_aggr(mv2[:, u, :], st2[:, u, :]))
                c.wait()
                dve.tensor_scalar(v2[:, :], mv2[:, :, 1], EPS, None, ALU.add).then_inc(b_var, 1)
                dve.wait_ge(b_root, i + 1)
                inverse_root(r2v[:, :], v2[:, :], t2[:, :])
                for u in range(2):
                    dve.wait_ge(b_tp, 2 * i + u + 1)
                    passed(dve, "dve")
                    dve.tensor_scalar(xn2[:, u, :], x1s[:, u, :], mv2[:, u, 0:1], r2v[:, u:u + 1],
                                      ALU.subtract, ALU.mult).then_inc(b_xn, 1)
                for u in range(2):
                    dve.wait_ge(b_xn, 2 * i + u + 1)
                    passed(dve, "dve")
                    c.mark(dve.tensor_tensor_reduce(prod[:, u, :], xn2[:, u, :], wr[:, :], 1.0, 0.0, ALU.mult, ALU.add, wcol[:, u:u + 1]))
                c.wait()
                c.link(dve.tensor_copy(wt[:, ds(2 * i, 2)], wcol[:, :]))
            c.leave(NT // 2)
            c.link(dve.tensor_scalar(wt[:, 0:NB], wt[:, 0:NB], brc[:, 0:1], None, ALU.add))
            bits = wt[:, 0:NB].bitcast(I32)
            c.link(dve.tensor_scalar(keyI[:, :], bits, 31, 0x7FFFFFFF, ALU.arith_shift_right, ALU.bitwise_and))
            c.link(dve.tensor_tensor(keyI[:, :], keyI[:, :], bits, ALU.bitwise_xor))
            c.link(dve.tensor_scalar(kbI[:, :], keyI[:, :], 16, None, ALU.arith_shift_right))
            c.link(dve.tensor_scalar(khi[:, :], kbI[:, :], 32768.0, None, ALU.add))
            c.link(dve.tensor_scalar(kbI[:, :], keyI[:, :], 0xFFFF, None, ALU.bitwise_and))
            c.link(dve.tensor_copy(klo[:, :], kbI[:, :]))
            c.link(dve.tensor_scalar(tk[4][:, :], pid[:, 0:1], float(LAST), None, ALU.is_lt))
            c.link(dve.tensor_scalar(tk[3][:, :], tk[4][:, :], -1.0, None, ALU.add))
            c.link(dve.tensor_scalar(khi[:, xpart:NB], khi[:, xpart:NB], tk[4][:, :], tk[3][:, :], ALU.mult, ALU.add))
            top, need = tk[0][:, :], tk[1][:, :]

            def search(values, n):
                c.link(dve.memset(top, 0.0))
                with dve.Fori(0, SD) as i:
                    c.enter(i, 5)
                    c.link(dve.tensor_scalar(cand[:, :], row(steps[:, ds(i, 1), :]), top, None, ALU.add))
                    c.link(dve.tensor_tensor(reach[:, :, :], spread(values.rearrange("p (o h) -> p o h", o=1), 1, SR),
                                             spread(cand[:, :].rearrange("p (k o) -> p k o", o=1), 2, NB), ALU.is_ge))
                    c.link(dve.tensor_reduce(cnts[:, :], reach[:, :, :], AX.X, ALU.add))
                    dve.sem_inc(k_cnt, 1)
                    dve.wait_ge(k_sum, SD * n + i + 1)
                    c.link(dve.scalar_tensor_tensor(cand[:, :], bank[7][:, 0:SR], float(TOP), cand[:, :], ALU.is_ge, ALU.mult))
                    c.link(dve.tensor_reduce(top, cand[:, :], AX.X, ALU.max))
                c.leave(SD)

            search(khi[:, :], 0)
            c.link(dve.tensor_scalar(gtm[:, :], khi[:, :], top, 65537.0, ALU.is_gt, ALU.mult))
            c.link(dve.tensor_scalar(eqm[:, :], khi[:, :], top, None, ALU.is_equal))
            c.link(dve.tensor_scalar(klo[:, :], klo[:, :], 1.0, None, ALU.add))
            c.link(dve.tensor_tensor(comb[:, :], klo[:, :], eqm[:, :], ALU.mult))
            c.link(dve.tensor_tensor(comb[:, :], comb[:, :], gtm[:, :], ALU.add))
            c.link(dve.tensor_scalar(comb[:, :], comb[:, :], -1.0, None, ALU.add))
            search(comb[:, :], 1)
            c.link(dve.tensor_scalar(eqm[:, :], comb[:, :], top, None, ALU.is_equal))
            c.link(dve.tensor_scalar(sel[:, :], comb[:, :], top, None, ALU.is_gt))
            c.link(dve.tensor_reduce(cnts[:, 0:1], sel[:, :], AX.X, ALU.add))
            dve.sem_inc(k_cnt, 1)
            dve.wait_ge(k_sum, 2 * SD + 1)
            c.link(dve.tensor_scalar(need, bank[7][:, 0:1], -1.0, float(TOP), ALU.mult, ALU.add))
            c.link(dve.tensor_copy(v49[:, :], bank[7][:, 2 * P:2 * P + NB]))
            c.link(dve.tensor_tensor_scan(u49[:, :], ones[:, 0:NB], v49[:, :], 0.0, ALU.mult, ALU.add))
            c.link(dve.tensor_tensor(u49[:, :], u49[:, :], v49[:, :], ALU.subtract))
            c.link(dve.tensor_tensor(u49[:, :], u49[:, :], bank[7][:, P:P + NB], ALU.add))
            c.link(dve.tensor_scalar(u49[:, :], u49[:, :], need, None, ALU.is_lt))
            c.link(dve.tensor_tensor(u49[:, :], u49[:, :], eqm[:, :], ALU.mult))
            c.link(dve.tensor_tensor(sel[:, :], sel[:, :], u49[:, :], ALU.add))
            c.link(dve.tensor_tensor(wsel[:, :], wt[:, 0:NB], sel[:, :], ALU.mult))

            def finish(i):
                for q in range(7):
                    t = 7 * i + q
                    dve.wait_ge(c_free, t + 3)
                    passed(dve, "dve")
                    c.link(dve.tensor_tensor(ot[:, q, :], ot[:, q, :], fb2[:, :], ALU.add))
                    dve.scalar_tensor_tensor(ot[:, q, :], ot[:, q, :], wsel[:, ds(t, 1)], row(X[:, ds(t, 1), :]),
                                             ALU.mult, ALU.add).then_inc(c_ot, 1)

            dve.wait_ge(a_sum, NT + 2)
            with dve.Fori(0, NB // 7) as i:
                c.enter(i, 7)
                finish(i)
            c.leave(NB // 7)


_INS = ['x', 'src', 'dst', 'edge_weight', 'L0_gnn_b', 'L0_gnn_W1', 'L0_gnn_b1', 'L0_gnn_W2', 'L0_gnn_b2',
        'L0_mix_b_out', 'L0_ffn_wr', 'L0_ffn_br', 'L0_ffn_w1', 'L0_ffn_b1', 'L0_ffn_w2', 'L0_ffn_b2']


def kernel(**inputs):
    import numpy as _np
    import concourse.bacc as _bacc
    from concourse import mybir as _mybir
    from concourse.bass_utils import run_bass_kernel_spmd as _run

    nc = _bacc.Bacc("TRN2", target_bir_lowering=False, num_devices=1)
    qkv = _np.asarray(inputs['L0_mix_w_qkv'])
    inner = qkv.shape[0] // 3
    laid = {name: _np.asarray(inputs[name]) for name in _INS}
    laid['wq'] = qkv[:inner]
    laid['kvT'] = qkv[inner:].T
    laid['woT'] = _np.asarray(inputs['L0_mix_w_out']).T
    laid['WT'] = _np.asarray(inputs['L0_gnn_W']).T
    arrays, aps = {}, {}
    for name, a in laid.items():
        a = _np.ascontiguousarray(a)
        arrays[f"in_{name}_dram"] = a
        aps[name] = nc.dram_tensor(f"in_{name}_dram", a.shape, _mybir.dt.from_np(a.dtype), kind="ExternalInput").ap()
    out = nc.dram_tensor("out_0_dram", laid['x'].shape, _mybir.dt.float32, kind="ExternalOutput").ap()
    gps_layer(nc, aps, out)
    r = _run(nc, [arrays], core_ids=[0])
    return r.results[0]["out_0_dram"]
```
